# Optimizing a Trainium2 kernel written in Bass

```python
import numpy as np
import jax
import jax.numpy as jnp

def _softmax(x, axis=-1):
    return jax.nn.softmax(x, axis=axis)

def _gelu(x):
    return jax.nn.gelu(x, approximate=True)

def _silu(x):
    return jax.nn.silu(x)

def _sigmoid(x):
    return jax.nn.sigmoid(x)

def _layernorm(x, axis=-1, eps=1e-05):
    m = jnp.mean(x, axis=axis, keepdims=True)
    v = jnp.var(x, axis=axis, keepdims=True)
    return (x - m) / jnp.sqrt(v + eps)

def _scatter_add(tgt, idx, src, axis=0):
    return tgt.at[idx].add(src)

def _segment_sum(src, seg, n):
    return jax.ops.segment_sum(src, seg, n)
kernel_name = 'mk_lm_tower_d1_tok_ids512_r4_b3e938'

def setup_inputs(seed: int=0):
    np.random.seed(seed)
    _w = jnp.asarray

    def _rec_inputs():
        import jax
        import jax.numpy as jnp
        _rk = jax.random.key(seed)
        x = jax.random.randint(jax.random.fold_in(_rk, 1), (32, 96), 0, 31983, jnp.int32)
        return x
    x = _rec_inputs()

    def _L0_tok_setup():
        import jax, jax.numpy as jnp
        import numpy as np
        D_MODEL = 128
        D_FF = 512
        VOCAB = 8000
        B, N = (2, 96)
        EPS = 1e-06

        def positional_encoding(n, d):
            pos = np.arange(n)[:, None].astype(np.float64)
            i = np.arange(d)[None, :]
            ang = pos / np.power(10000.0, 2 * (i // 2) / np.float32(d))
            ang[:, 0::2] = np.sin(ang[:, 0::2])
            ang[:, 1::2] = np.cos(ang[:, 1::2])
            return jnp.asarray(ang, dtype=jnp.float32)

        def layer_norm(x, gamma, beta):
            mu = jnp.mean(x, axis=-1, keepdims=True)
            var = jnp.mean(jnp.square(x - mu), axis=-1, keepdims=True)
            return (x - mu) / jnp.sqrt(var + EPS) * gamma + beta
        key = jax.random.key(seed)
        ks = jax.random.split(key, 12)
        s = 0.02
        return {'tokens': jax.random.randint(ks[0], (B, N), 0, VOCAB, dtype=jnp.int32), 'emb': jax.random.normal(ks[1], (VOCAB, D_MODEL), jnp.float32) * s, 'Wq': jax.random.normal(ks[2], (D_MODEL, D_MODEL), jnp.float32) * s, 'bq': jnp.zeros((D_MODEL,), jnp.float32), 'Wk': jax.random.normal(ks[3], (D_MODEL, D_MODEL), jnp.float32) * s, 'bk': jnp.zeros((D_MODEL,), jnp.float32), 'Wv': jax.random.normal(ks[4], (D_MODEL, D_MODEL), jnp.float32) * s, 'bv': jnp.zeros((D_MODEL,), jnp.float32), 'attn_scale': jax.random.normal(ks[5], (D_MODEL,), jnp.float32) * 0.05, 'Wo': jax.random.normal(ks[6], (D_MODEL, D_MODEL), jnp.float32) * s, 'bo': jnp.zeros((D_MODEL,), jnp.float32), 'g1': jnp.ones((D_MODEL,), jnp.float32), 'beta1': jnp.zeros((D_MODEL,), jnp.float32), 'W1': jax.random.normal(ks[7], (D_MODEL, D_FF), jnp.float32) * s, 'bf1': jnp.zeros((D_FF,), jnp.float32), 'W2': jax.random.normal(ks[8], (D_FF, D_MODEL), jnp.float32) * s, 'bf2': jnp.zeros((D_MODEL,), jnp.float32), 'g2': jnp.ones((D_MODEL,), jnp.float32), 'beta2': jnp.zeros((D_MODEL,), jnp.float32)}
    _L0_tok_all = _L0_tok_setup()
    _L0_tok_in = {k: v for k, v in _L0_tok_all.items() if k in ('emb', 'Wq', 'bq', 'Wk', 'bk', 'Wv', 'bv', 'attn_scale', 'Wo', 'bo', 'g1', 'beta1', 'W1', 'bf1', 'W2', 'bf2', 'g2', 'beta2')}
    del _L0_tok_all

    def _L0_attn_setup():
        import jax, jax.numpy as jnp
        import numpy as np
        B, T, K, H = (8, 256, 128, 8)
        key = jax.random.key(seed)
        kx, kq, kk, kv, ko = jax.random.split(key, 5)
        s = 0.02
        return {'x': jax.random.normal(kx, (B, T, K), dtype=jnp.float32), 'Wq': jax.random.normal(kq, (K * H, K), dtype=jnp.float32) * s, 'Wk': jax.random.normal(kk, (K * H, K), dtype=jnp.float32) * s, 'Wv': jax.random.normal(kv, (K * H, K), dtype=jnp.float32) * s, 'Wo': jax.random.normal(ko, (K, K * H), dtype=jnp.float32) * s}
    _L0_attn_all = _L0_attn_setup()
    _L0_attn_in = {k: v for k, v in _L0_attn_all.items() if k in ('Wq', 'Wk', 'Wv', 'Wo')}
    del _L0_attn_all

    def _L0_ffn_setup():
        import jax, jax.numpy as jnp
        import numpy as np
        D, E, DR, K, DFF, DSH = (128, 64, 64, 2, 512, 256)
        TEMP = 0.7
        SHARED_SCALE = 0.25
        EPS = 1e-05

        def _ln(x, g, b):
            m = jnp.mean(x, axis=-1, keepdims=True)
            v = jnp.mean(jnp.square(x - m), axis=-1, keepdims=True)
            return (x - m) * jax.lax.rsqrt(v + EPS) * g + b
        key = jax.random.key(seed)
        ks = jax.random.split(key, 16)
        s = 0.02
        return {'x': jax.random.normal(ks[0], (1, 128, D), dtype=jnp.float32), 'ln1_g': jnp.ones((D,), jnp.float32), 'ln1_b': jnp.zeros((D,), jnp.float32), 'Wr': jax.random.normal(ks[1], (D, DR), jnp.float32) * s, 'codebook': jax.random.normal(ks[2], (E, DR), jnp.float32), 'W1': jax.random.normal(ks[3], (E, D, DFF), jnp.float32) * s, 'b1': jnp.zeros((E, DFF), jnp.float32), 'W2': jax.random.normal(ks[4], (E, DFF, D), jnp.float32) * s, 'b2': jnp.zeros((E, D), jnp.float32), 'Ws1': jax.random.normal(ks[5], (D, DSH), jnp.float32) * s, 'bs1': jnp.zeros((DSH,), jnp.float32), 'Ws2': jax.random.normal(ks[6], (DSH, D), jnp.float32) * s, 'bs2': jnp.zeros((D,), jnp.float32), 'ffln_g': jnp.ones((D,), jnp.float32), 'ffln_b': jnp.zeros((D,), jnp.float32), 'Wf1': jax.random.normal(ks[7], (D, DFF), jnp.float32) * s, 'bf1': jnp.zeros((DFF,), jnp.float32), 'Wf2': jax.random.normal(ks[8], (DFF, D), jnp.float32) * s, 'bf2': jnp.zeros((D,), jnp.float32)}
    _L0_ffn_all = _L0_ffn_setup()
    _L0_ffn_in = {k: v for k, v in _L0_ffn_all.items() if k in ('ln1_g', 'ln1_b', 'Wr', 'codebook', 'W1', 'b1', 'W2', 'b2', 'Ws1', 'bs1', 'Ws2', 'bs2', 'ffln_g', 'ffln_b', 'Wf1', 'bf1', 'Wf2', 'bf2')}
    del _L0_ffn_all
    return {'x': x, 'L0_tok_emb': _L0_tok_in['emb'], 'L0_tok_Wq': _L0_tok_in['Wq'], 'L0_tok_bq': _L0_tok_in['bq'], 'L0_tok_Wk': _L0_tok_in['Wk'], 'L0_tok_bk': _L0_tok_in['bk'], 'L0_tok_Wv': _L0_tok_in['Wv'], 'L0_tok_bv': _L0_tok_in['bv'], 'L0_tok_attn_scale': _L0_tok_in['attn_scale'], 'L0_tok_Wo': _L0_tok_in['Wo'], 'L0_tok_bo': _L0_tok_in['bo'], 'L0_tok_g1': _L0_tok_in['g1'], 'L0_tok_beta1': _L0_tok_in['beta1'], 'L0_tok_W1': _L0_tok_in['W1'], 'L0_tok_bf1': _L0_tok_in['bf1'], 'L0_tok_W2': _L0_tok_in['W2'], 'L0_tok_bf2': _L0_tok_in['bf2'], 'L0_tok_g2': _L0_tok_in['g2'], 'L0_tok_beta2': _L0_tok_in['beta2'], 'L0_attn_Wq': _L0_attn_in['Wq'], 'L0_attn_Wk': _L0_attn_in['Wk'], 'L0_attn_Wv': _L0_attn_in['Wv'], 'L0_attn_Wo': _L0_attn_in['Wo'], 'L0_ffn_ln1_g': _L0_ffn_in['ln1_g'], 'L0_ffn_ln1_b': _L0_ffn_in['ln1_b'], 'L0_ffn_Wr': _L0_ffn_in['Wr'], 'L0_ffn_codebook': _L0_ffn_in['codebook'], 'L0_ffn_W1': _L0_ffn_in['W1'], 'L0_ffn_b1': _L0_ffn_in['b1'], 'L0_ffn_W2': _L0_ffn_in['W2'], 'L0_ffn_b2': _L0_ffn_in['b2'], 'L0_ffn_Ws1': _L0_ffn_in['Ws1'], 'L0_ffn_bs1': _L0_ffn_in['bs1'], 'L0_ffn_Ws2': _L0_ffn_in['Ws2'], 'L0_ffn_bs2': _L0_ffn_in['bs2'], 'L0_ffn_ffln_g': _L0_ffn_in['ffln_g'], 'L0_ffn_ffln_b': _L0_ffn_in['ffln_b'], 'L0_ffn_Wf1': _L0_ffn_in['Wf1'], 'L0_ffn_bf1': _L0_ffn_in['bf1'], 'L0_ffn_Wf2': _L0_ffn_in['Wf2'], 'L0_ffn_bf2': _L0_ffn_in['bf2']}

def reference(x, L0_tok_emb, L0_tok_Wq, L0_tok_bq, L0_tok_Wk, L0_tok_bk, L0_tok_Wv, L0_tok_bv, L0_tok_attn_scale, L0_tok_Wo, L0_tok_bo, L0_tok_g1, L0_tok_beta1, L0_tok_W1, L0_tok_bf1, L0_tok_W2, L0_tok_bf2, L0_tok_g2, L0_tok_beta2, L0_attn_Wq, L0_attn_Wk, L0_attn_Wv, L0_attn_Wo, L0_ffn_ln1_g, L0_ffn_ln1_b, L0_ffn_Wr, L0_ffn_codebook, L0_ffn_W1, L0_ffn_b1, L0_ffn_W2, L0_ffn_b2, L0_ffn_Ws1, L0_ffn_bs1, L0_ffn_Ws2, L0_ffn_bs2, L0_ffn_ffln_g, L0_ffn_ffln_b, L0_ffn_Wf1, L0_ffn_bf1, L0_ffn_Wf2, L0_ffn_bf2):
    import jax
    import jax.numpy as jnp

    def _L0_tok_ref(tokens, emb, Wq, bq, Wk, bk, Wv, bv, attn_scale, Wo, bo, g1, beta1, W1, bf1, W2, bf2, g2, beta2):
        import jax, jax.numpy as jnp
        import numpy as np
        D_MODEL = 128
        D_FF = 512
        VOCAB = 8000
        B, N = (2, 96)
        EPS = 1e-06

        def positional_encoding(n, d):
            pos = np.arange(n)[:, None].astype(np.float64)
            i = np.arange(d)[None, :]
            ang = pos / np.power(10000.0, 2 * (i // 2) / np.float32(d))
            ang[:, 0::2] = np.sin(ang[:, 0::2])
            ang[:, 1::2] = np.cos(ang[:, 1::2])
            return jnp.asarray(ang, dtype=jnp.float32)

        def layer_norm(x, gamma, beta):
            mu = jnp.mean(x, axis=-1, keepdims=True)
            var = jnp.mean(jnp.square(x - mu), axis=-1, keepdims=True)
            return (x - mu) / jnp.sqrt(var + EPS) * gamma + beta
        x = emb[tokens] * jnp.sqrt(jnp.float32(D_MODEL))
        x = x + positional_encoding(N, D_MODEL)[None, :, :]
        q = x @ Wq + bq
        k = x @ Wk + bk
        v = x @ Wv + bv
        scores = jnp.einsum('d,bijd->bij', attn_scale, jnp.tanh(q[:, :, None, :] + k[:, None, :, :]))
        weights = jax.nn.softmax(scores, axis=-1)
        attn = jnp.einsum('bij,bjd->bid', weights, v)
        attn = attn @ Wo + bo
        x = layer_norm(x + attn, g1, beta1)
        h = jax.nn.relu(x @ W1 + bf1)
        y = h @ W2 + bf2
        return layer_norm(x + y, g2, beta2)

    def _L0_attn_ref(x, Wq, Wk, Wv, Wo):
        import jax, jax.numpy as jnp
        import numpy as np
        B, T, K, H = (8, 256, 128, 8)
        b, t, k = x.shape
        h = H
        scale = k ** 0.25

        def proj(W):
            return (x @ W.T).reshape(b, t, h, k).transpose(0, 2, 1, 3)
        q = proj(Wq) / scale
        kk_ = proj(Wk) / scale
        v = proj(Wv)
        dot = jnp.einsum('bhtd,bhsd->bhts', q, kk_)
        causal = jnp.tril(jnp.ones((t, t), dtype=bool))
        dot = jnp.where(causal[None, None], dot, -jnp.inf)
        attn = jax.nn.softmax(dot, axis=-1)
        out = jnp.einsum('bhts,bhsd->bhtd', attn, v)
        out = out.transpose(0, 2, 1, 3).reshape(b, t, h * k)
        return out @ Wo.T

    def _L0_ffn_ref(x, ln1_g, ln1_b, Wr, codebook, W1, b1, W2, b2, Ws1, bs1, Ws2, bs2, ffln_g, ffln_b, Wf1, bf1, Wf2, bf2):
        import jax, jax.numpy as jnp
        import numpy as np
        D, E, DR, K, DFF, DSH = (128, 64, 64, 2, 512, 256)
        TEMP = 0.7
        SHARED_SCALE = 0.25
        EPS = 1e-05

        def _ln(x, g, b):
            m = jnp.mean(x, axis=-1, keepdims=True)
            v = jnp.mean(jnp.square(x - m), axis=-1, keepdims=True)
            return (x - m) * jax.lax.rsqrt(v + EPS) * g + b
        B, S, _ = x.shape
        T = B * S
        h = _ln(x, ln1_g, ln1_b).reshape(T, D)
        r = h @ Wr
        logits = r @ codebook.T / TEMP
        probs = jax.nn.softmax(logits, axis=-1)
        vals, idx = jax.lax.top_k(probs, K)
        w = vals / jnp.sum(vals, axis=-1, keepdims=True)
        combine = jnp.zeros((T, E), x.dtype).at[jnp.arange(T)[:, None], idx].set(w)
        eh = jax.nn.silu(jnp.einsum('td,edf->tef', h, W1) + b1)
        eo = jnp.einsum('tef,efd->ted', eh, W2) + b2
        moe = jnp.einsum('te,ted->td', combine, eo)
        shared = (jax.nn.silu(h @ Ws1 + bs1) @ Ws2 + bs2) * SHARED_SCALE
        hmoe = (moe + shared).reshape(B, S, D)
        f = _ln(hmoe, ffln_g, ffln_b)
        f = jax.nn.silu(f @ Wf1 + bf1) @ Wf2 + bf2
        return x + hmoe + f
    h = _L0_tok_ref(x, L0_tok_emb, L0_tok_Wq, L0_tok_bq, L0_tok_Wk, L0_tok_bk, L0_tok_Wv, L0_tok_bv, L0_tok_attn_scale, L0_tok_Wo, L0_tok_bo, L0_tok_g1, L0_tok_beta1, L0_tok_W1, L0_tok_bf1, L0_tok_W2, L0_tok_bf2, L0_tok_g2, L0_tok_beta2)
    h = h + _L0_attn_ref(_layernorm(h, axis=-1), L0_attn_Wq, L0_attn_Wk, L0_attn_Wv, L0_attn_Wo)
    h = h + _L0_ffn_ref(_layernorm(h, axis=-1), L0_ffn_ln1_g, L0_ffn_ln1_b, L0_ffn_Wr, L0_ffn_codebook, L0_ffn_W1, L0_ffn_b1, L0_ffn_W2, L0_ffn_b2, L0_ffn_Ws1, L0_ffn_bs1, L0_ffn_Ws2, L0_ffn_bs2, L0_ffn_ffln_g, L0_ffn_ffln_b, L0_ffn_Wf1, L0_ffn_bf1, L0_ffn_Wf2, L0_ffn_bf2)
    return h

_drawn_inputs = setup_inputs


def setup_inputs(seed=0):
    import zlib

    import numpy as np

    out = dict(_drawn_inputs(seed))
    spreads = {'L0_tok_bq': (0.0, 2.0),
     'L0_tok_bk': (0.0, 2.0),
     'L0_tok_bv': (0.0, 0.1),
     'L0_tok_bo': (0.0, 0.1),
     'L0_tok_g1': (1.0, 0.2),
     'L0_tok_beta1': (0.0, 0.1),
     'L0_tok_bf1': (0.0, 0.293),
     'L0_tok_bf2': (0.0, 0.1),
     'L0_tok_g2': (1.0, 0.2),
     'L0_tok_beta2': (0.0, 0.1),
     'L0_ffn_ln1_g': (1.0, 0.557),
     'L0_ffn_ln1_b': (0.0, 0.561),
     'L0_ffn_b1': (0.0, 0.784),
     'L0_ffn_b2': (0.0, 0.1),
     'L0_ffn_bs1': (0.0, 0.8),
     'L0_ffn_bs2': (0.0, 0.609),
     'L0_ffn_ffln_g': (1.0, 0.6),
     'L0_ffn_ffln_b': (0.0, 2.0),
     'L0_ffn_bf1': (0.0, 0.662),
     'L0_ffn_bf2': (0.0, 0.1)}
    factors = {'L0_tok_Wq': 198.462,
     'L0_tok_Wk': 37.719,
     'L0_tok_attn_scale': 37.6,
     'L0_attn_Wq': 8.0,
     'L0_attn_Wk': 8.0,
     'L0_ffn_Ws1': 8.0,
     'L0_ffn_Ws2': 8.0}
    for name, (base, spread) in spreads.items():
        noise = np.random.default_rng([zlib.crc32(name.encode()), seed]).standard_normal(out[name].shape)
        drawn = base * np.exp(spread * noise) if base else spread * noise
        out[name] = jnp.asarray(drawn.astype(out[name].dtype))
    for name, factor in factors.items():
        out[name] = (out[name] * factor).astype(out[name].dtype)
    return out
```

```python
from contextlib import ExitStack

import concourse.bass as bass
import numpy as np
from concourse import mybir

F32 = mybir.dt.float32
I32 = mybir.dt.int32
U32 = mybir.dt.uint32
ACT = mybir.ActivationFunctionType
ALU = mybir.AluOpType
AX = mybir.AxisListType

B, N, D = 32, 96, 128
G = 2
PAIRS = B // G
TN = G * N
T = B * N
VOCAB, DFF, H = 8000, 512, 8
FC = DFF // D
E, DR, TOPK, DSH = 64, 64, 2, 256
SC2 = DSH // D
TILE = 128
RING = 3
MAXT = (T * TOPK - E) // TILE + E + 1
TABN = E * T
QG = N // 32
CROWS = 12
CPB = N // CROWS
CH = G * CPB
CW = CROWS * N
TRING = 4
POOL_CHUNKS = (2, 5, 8, 11, 14)
BIGS = 18
ACT_BIG = (0, 2, 4, 6, 8, 14, 16)
EPS_TOK, EPS = 1e-6, 1e-5
SCALE = 1.0 / float(D) ** 0.5
TEMP = 0.7
SHARED = 0.25
NEG = -1.0e30
DVE_LINKS = 31
WCOLS = 2 * DFF + FC

ROWS = ["bv", "bo", "g1", "beta1", "bf2", "g2", "beta2", "bs2", "fbf2"]


def program(nc, io, out):
    with ExitStack() as ctx:
        def sb(name, shape, dt=F32):
            return ctx.enter_context(nc.sbuf_tensor(name, shape, dt))

        def ps(name):
            return ctx.enter_context(nc.psum_tensor(name, [128, 512], F32))

        tok_dram = nc.dram_tensor("tok_dram", (TOPK * T, D), F32).ap()
        tab_dram = nc.dram_tensor("tab_dram", (TABN, 1), I32).ap()
        eo_dram = nc.dram_tensor("eo_dram", (TOPK * T, D), F32).ap()

        ident = sb("ident", [128, 128])
        tri = sb("tri", [N, N])
        ones = sb("ones", [N, 128])
        mask = sb("mask", [N, N])
        pe_rows = sb("pe_rows", [N, D])
        iota_e = sb("iota_e", [128, E])
        iota_t = sb("iota_t", [128, 1])
        row = {n: sb("row_" + n, [N, D]) for n in ROWS}
        wqkv = sb("wqkv", [D, 3, D])
        wo = sb("wo", [D, D])
        w1 = sb("w1", [D, DFF])
        w2 = sb("w2", [D, FC, D])
        spread = sb("spread", [128, PAIRS * G * TOPK * D])
        raw = spread[:, 0:4 * H * D].rearrange("p (a n) -> p a n", a=4)
        mh = sb("mh", [D, H * D])
        vo = sb("vo", [D, H * D])
        wr = sb("wr", [D, DR])
        cbT = sb("cbT", [DR, E])
        ws1 = sb("ws1", [D, DSH])
        ws2 = sb("ws2", [D, SC2, D])
        wf1 = sb("wf1", [D, DFF])
        wf2 = sb("wf2", [D, FC, D])
        cols = sb("cols", [D, 7 + FC + SC2 + FC])
        bq, bk, ascale = cols[:, 0:1], cols[:, 1:2], cols[:, 2:3]
        ln1_g, ln1_b, ffln_g, ffln_b = (cols[:, i:i + 1] for i in range(3, 7))
        bf1 = cols[:, 7:7 + FC]
        bs1 = cols[:, 7 + FC:7 + FC + SC2]
        fbf1 = cols[:, 7 + FC + SC2:]
        apad = sb("apad", [D, 64])
        neghalf = sb("neghalf", [N, G])
        bs2q = sb("bs2q", [N, D])
        sentinel = sb("sentinel", [128, TABN // 128], I32)

        tok_i = sb("tok_i", [N, B], I32)
        tok_f = sb("tok_f", [N, B])
        neg_f = sb("neg_f", [N, B])
        eidx = sb("eidx", [N, B], I32)
        choice = sb("choice", [N, B * TOPK], I32)
        res = sb("res", [N, PAIRS, G, D])
        hall = sb("hall", [D, PAIRS, TN])
        wts = sb("wts", [N, PAIRS, G * TOPK])
        ei_now = sb("ei_now", [N, G], I32)
        tid_now = sb("tid_now", [N, G * TOPK], I32)
        slot_now = sb("slot_now", [N, G * TOPK], I32)
        emb_rows = sb("emb_rows", [N, G, D])
        xs = sb("xs", [N, G, D])
        xT = sb("xT", [D, TN])
        qT = sb("qT", [D, TN])
        kT = sb("kT", [D, TN])
        vrow = sb("vrow", [N, G, D])
        tbuf = sb("tbuf", [D, TRING, CW])
        nmax = sb("nmax", [N, G])
        esum = sb("esum", [N, G])
        rsum = sb("rsum", [N, G])
        p1 = sb("p1", [N, G, N])
        p1T = sb("p1T", [N, G, N])
        aT = sb("aT", [D, TN])
        x1 = sb("x1", [N, G, D])
        xn = sb("xn", [N, G, D])
        xg = sb("xg", [N, G, D])
        x1n = sb("x1n", [N, G, D])
        x1b = sb("x1b", [N, G, D])
        x1T = sb("x1T", [D, TN])
        hid = sb("hid", [D, FC, TN])
        x2 = sb("x2", [N, G, D])
        h0 = sb("h0", [N, G, D])
        xa = sb("xa", [N, G, D])
        xaT = sb("xaT", [D, TN])
        gT = sb("gT", [D, H, TN])
        vv = sb("vv", [N, G, H * D])
        pr = sb("pr", [N, G * H, N])
        prT = sb("prT", [N, G * H, N])
        mx2 = sb("mx2", [N, G * H])
        nb2 = sb("nb2", [N, G * H])
        es2 = sb("es2", [N, G * H])
        rs2 = sb("rs2", [N, G * H])
        h1 = sb("h1", [N, G, D])
        h1n = sb("h1n", [N, G, D])
        tn = sb("tn", [N, G, D])
        hT = sb("hT", [D, TN])
        rT = sb("rT", [DR, TN])
        lg = sb("lg", [N, G, E])
        top = sb("top", [N, G, 8])
        topi = sb("topi", [N, G, 8], U32)
        topf = sb("topf", [N, G * TOPK])
        gap = sb("gap", [N, G])
        egap = sb("egap", [N, G])
        egap1 = sb("egap1", [N, G])
        wnow = sb("wnow", [N, G, TOPK])
        oh = sb("oh", [N, G, TOPK, E])
        ohs = sb("ohs", [N, G, E])
        cum = sb("cum", [N, E])
        rjunk = sb("rjunk", [N, G * TOPK, E])
        rank = sb("rank", [N, G * TOPK])
        slotf = sb("slotf", [N, G * TOPK])
        stat = sb("stat", [N, G, 6])
        mv = sb("mv", [N, G, 2])
        ve = sb("ve", [N, G])
        rstd = sb("rstd", [N, G])
        vr = sb("vr", [N, G])
        rstd2 = sb("rstd2", [N, G])

        cntf = sb("cntf", [MAXT, E])
        cnti = sb("cnti", [MAXT, E], I32)
        ntf = sb("ntf", [MAXT, E])
        tend = sb("tend", [MAXT, E])
        le = sb("le", [MAXT, E])
        lejunk = sb("lejunk", [MAXT, E])
        tcol = sb("tcol", [MAXT, 8])
        ui = sb("ui", [MAXT, 1], I32)
        uii = sb("uii", [MAXT, 1], I32)
        tinfo = sb("tinfo", [MAXT, 5])
        ttab = sb("ttab", [1, 2 * MAXT + 3], I32)
        wbuf = sb("wbuf", [D, RING, WCOLS])
        b2buf = sb("b2buf", [1, RING, D])
        iall = sb("iall", [TILE, MAXT], I32)
        igather = sb("igather", [TILE, RING], I32)
        iscatter = sb("iscatter", [TILE, RING], I32)
        hrow = [sb(f"hrow{r}", [TILE, D]) for r in range(RING)]
        hbT = sb("hbT", [D, RING, TILE])
        act_h = sb("act_h", [D, RING, DFF])
        eo = [sb(f"eo{r}", [TILE, D]) for r in range(RING)]

        er = spread[0:N, :].rearrange("p (a g k d) -> p a g k d", a=PAIRS, g=G, k=TOPK)
        wl = sb("wl", [N, G * TOPK])
        sh = sb("sh", [D, SC2, TN])
        hm1 = sb("hm1", [N, G, D])
        hm2 = sb("hm2", [N, G, D])
        hm = sb("hm", [N, G, D])
        rh = sb("rh", [N, G, D])
        rh2 = sb("rh2", [N, G, D])
        fn = sb("fn", [N, G, D])
        fT = sb("fT", [D, TN])
        fh = sb("fh", [D, FC, TN])
        of = sb("of", [N, G, D])

        b_s, b_qk, b_v, b_t, b_y = ps("b_s"), ps("b_qk"), ps("b_v"), ps("b_t"), ps("b_y")
        big = [ps("big0"), ps("big1"), ps("big2")]
        p_score = b_s[0:N, 0:TN].rearrange("p (g n) -> p g n", g=G)
        p_v = b_v[0:N, 0:G * D].rearrange("p (g n) -> p g n", g=G)
        p_xT = b_v[:, 256:256 + TN]
        p_y = b_y[0:N, 0:G * D].rearrange("p (g n) -> p g n", g=G)
        p_lg = b_y[0:N, 0:G * E]
        p_rank = b_y[0:N, 128:128 + G * E].rearrange("p (g n) -> p g n", g=G)

        s = {n: ctx.enter_context(nc.semaphore("s_" + n)) for n in [
            "early", "late", "consts", "gate", "raw_mm", "raw_ev", "pool_c", "tab_init", "ids",
            "emb", "xs", "xs_t", "xT", "qkv", "qk_ev", "v_ev", "add_v", "add_p", "tanh", "score",
            "nmax", "exp1", "p1t_ps", "p1T", "aT_ps", "aT", "y", "x1n", "x1b", "x1T_ps", "x1T",
            "big", "big_a", "big_v", "y2", "xa", "xaT_ps", "xaT", "nb2", "exp2", "rs2", "pn",
            "o", "tn", "tn_st", "hT_ps", "hT", "hcopy", "rT_ps", "rT", "lg", "gap", "egap", "oh",
            "rank_ps", "rank", "slot", "tid", "ei", "scat", "ve", "rstd", "chain", "res",
            "cnt", "tinfo", "trow", "ttab",
            "w0", "w1", "w2", "i0", "i1", "i2", "h0", "h1", "h2", "st0", "st1", "st2",
            "tr", "hbT", "g1", "silu", "g2", "eo",
            "er", "copied", "sh_ps", "sh", "ys", "hm", "rh", "fve", "frstd", "fn", "fT_ps", "fT", "f1",
            "fa", "f2", "of", "out"]}
        s_w, s_i, s_h, s_st = [s["w0"], s["w1"], s["w2"]], [s["i0"], s["i1"], s["i2"]], [s["h0"], s["h1"], s["h2"]], [s["st0"], s["st1"], s["st2"]]
        block = ctx.enter_context(nc.Block())

        def gate(eng, sem, value):
            eng.wait_ge(sem, value)
            eng.sem_inc(s["gate"], 1)

        def turns_less(eng, n):
            at = 2 * MAXT + n
            return eng.value_load(ttab[0:1, at:at + 1], min_val=RING - n, max_val=MAXT // RING - n)

        def big_freed(eng, p, u):
            u = u - 3
            if u < 0:
                u, p = u + BIGS, p - 1
            if isinstance(p, int) and p < 0:
                return
            emptied(eng, p, u)

        def emptied(eng, p, u):
            if u in ACT_BIG:
                eng.wait_ge(s["big_a"], p * len(ACT_BIG) + ACT_BIG.index(u) + 1)
            else:
                rest = [x for x in range(BIGS) if x not in ACT_BIG]
                eng.wait_ge(s["big_v"], p * len(rest) + rest.index(u) + 1)

        def filled(eng, p, u, alone=False):
            eng.wait_ge(s["big"], p * BIGS + u + 1)
            if alone:
                eng.sem_inc(s["gate"], 1)

        def pipeline(eng, begin, chunk, side_post, side_pre, loop=None):
            def body(p, post, pre):
                begin(p)
                if post:
                    for f in side_post.get(-1, []):
                        f(p - 1)
                for c in range(CH):
                    chunk(p, c)
                    if post:
                        for f in side_post.get(c, []):
                            f(p - 1)
                    if pre:
                        for f in side_pre.get(c, []):
                            f(p + 1)
            for c in range(CH):
                for f in side_pre.get(c, []):
                    f(0)
            body(0, False, True)
            body(1, True, True)
            if loop is not None:
                loop.enter(2)
            with eng.Fori(2, PAIRS - 1) as p:
                if loop is not None:
                    loop.at(p)
                body(p, True, True)
            if loop is not None:
                loop.leave(PAIRS - 1)
            body(PAIRS - 1, True, False)
            for c in [-1, *range(CH)]:
                for f in side_post.get(c, []):
                    f(PAIRS - 1)

        @block.sync
        def _(sp):
            def load(dst, src, sem):
                sp.dma_start(dst, src).then_inc(sem, 16)

            load(tok_i[:, :], io["x"], s["ids"])
            load(ident[:, :], io["ident"], s["early"])
            load(wqkv[:, 0, :], io["L0_tok_Wq"], s["early"])
            load(wqkv[:, 1, :], io["L0_tok_Wk"], s["early"])
            load(wqkv[:, 2, :], io["L0_tok_Wv"], s["early"])
            load(cols[:, :], io["cols"], s["early"])
            load(pe_rows[:, :], io["pe"], s["early"])
            for n in ROWS:
                load(row[n][:, :], io["row_" + n].partition_broadcast(N), s["early"])
            for i, n in enumerate(["Wq", "Wk", "Wv", "WoT"]):
                load(raw[:, i, :].rearrange("p (h d) -> p h d", h=H),
                     io["attn_" + n].rearrange("(h k) d -> k h d", h=H), s["late"])
            load(wo[:, :], io["L0_tok_Wo"], s["late"])
            load(w1[:, :], io["L0_tok_W1"], s["late"])
            load(w2[:, :, :], io["L0_tok_W2"].rearrange("(c p) n -> p c n", p=D), s["late"])
            load(wr[:, :], io["L0_ffn_Wr"], s["late"])
            load(cbT[:, :], io["cbT"], s["late"])
            load(mask[:, :], io["mask"], s["late"])
            load(tri[:, :], io["tri"], s["late"])
            load(ws1[:, :], io["L0_ffn_Ws1"], s["late"])
            load(ws2[:, :, :], io["L0_ffn_Ws2"].rearrange("(c p) n -> p c n", p=D), s["late"])
            load(wf1[:, :], io["L0_ffn_Wf1"], s["late"])
            load(wf2[:, :, :], io["L0_ffn_Wf2"].rearrange("(c p) n -> p c n", p=D), s["late"])
            sp.wait_ge(s["pool_c"], 1)
            load(tab_dram.rearrange("(p n) a -> p (n a)", p=128), sentinel[:, :], s["tab_init"])

            def store_tokens(p):
                gate(sp, s["tn"], p + 1)
                rows = tok_dram[bass.ds(p * TN * TOPK, TN * TOPK), :]
                for k in range(TOPK):
                    sp.dma_start(rows.rearrange("(g n k) d -> n g k d", g=G, k=TOPK)[:, :, k, :],
                                 tn[:, :, :]).then_inc(s["tn_st"], 16)

            store_tokens(0)
            with sp.Fori(1, PAIRS) as p:
                store_tokens(p)

            sp.wait_ge(s["ttab"], 1)
            turns = turns_less(sp, 0)
            sp.wait_ge(s["scat"], 16 * TOPK * B)

            def load_tile(u, r, again=True):
                t = u * RING + r
                if again:
                    gate(sp, s["g2"], t - RING + 1)
                e = sp.value_load(ttab[0:1, bass.ds(t, 1)], min_val=0, max_val=E - 1)
                off = sp.value_load(ttab[0:1, bass.ds(MAXT + t, 1)], min_val=0, max_val=TABN - TILE)
                sp.dma_start(wbuf[:, r, :], io["wpack"][bass.ds(e, 1), :, :]).then_inc(s_w[r], 16)
                sp.dma_start(b2buf[0:1, r, :], io["L0_ffn_b2"][bass.ds(e, 1), :]).then_inc(s_w[r], 16)
                if again:
                    gate(sp, s_h[r], u * 16)
                sp.dma_start(iall[:, bass.ds(t, 1)], tab_dram[bass.ds(off, TILE), :]).then_inc(s_i[r], 16)

            for r in range(RING):
                load_tile(0, r, again=False)
            with sp.Fori(1, turns) as u:
                for r in range(RING):
                    load_tile(u, r)

            for r in range(RING):
                gate(sp, s_st[r], turns * 16)

            def load_results(p):
                rows = eo_dram[bass.ds(p * TN * TOPK, TN * TOPK), :]
                sp.dma_start(er[:, bass.ds(p, 1), :, :, :].rearrange("n a g k d -> n (a g) (k d)"),
                             rows.rearrange("(g n k) d -> n g (k d)", g=G, k=TOPK)).then_inc(s["er"], 16)

            load_results(0)
            with sp.Fori(1, PAIRS) as p:
                gate(sp, s["er"], 16 * p)
                load_results(p)

            def store_out(p):
                gate(sp, s["of"], p + 1)
                sp.dma_start(out[bass.ds(p * G, G), :, :].rearrange("g n d -> n g d"),
                             of[:, :, :]).then_inc(s["out"], 16)

            store_out(0)
            with sp.Fori(1, PAIRS) as p:
                store_out(p)
            sp.wait_ge(s["out"], 16 * PAIRS)
            sp.wait_ge(s["tn_st"], 16 * TOPK * PAIRS)

        @block.gpsimd
        def _(pool):
            pool.memset(sentinel[:, :], TOPK * T).then_inc(s["pool_c"], 1)
            pool.memset(neghalf[:, :], -0.5).then_inc(s["pool_c"], 1)
            pool.memset(ones[:, :], 1.0).then_inc(s["pool_c"], 1)
            pool.memset(cum[:, :], 0.0).then_inc(s["pool_c"], 1)
            pool.memset(apad[:, :], 0.0).then_inc(s["pool_c"], 1)
            pool.iota(choice[:, :], [[TOPK * N, B], [1, TOPK]], base=0, channel_multiplier=TOPK)\
                .then_inc(s["pool_c"], 1)
            pool.iota(iota_e[:, :], [[1, E]], base=0, channel_multiplier=0,
                      allow_small_or_imprecise_dtypes=True).then_inc(s["pool_c"], 1)
            pool.iota(iota_t[:, :], [[1, 1]], base=0, channel_multiplier=1,
                      allow_small_or_imprecise_dtypes=True).then_inc(s["pool_c"], 1)
            for r in range(RING):
                pool.memset(hrow[r][:, :], 0.0).then_inc(s["pool_c"], 1)

            def gather_emb(p):
                if isinstance(p, int) and p == 0:
                    pool.wait_ge(s["ids"], 17)
                else:
                    gate(pool, s["xs"], p)
                pool.tensor_copy(ei_now[:, :], eidx[:, bass.ds(p * G, G)]).then_inc(s["ei"], 1)
                gate(pool, s["ei"], p + 1)
                for g in range(G):
                    pool.indirect_dma_start(
                        emb_rows[:, g, :], None, io["L0_tok_emb"],
                        bass.IndirectOffsetOnAxis(ap=ei_now[:, g:g + 1].bitcast(U32), axis=0),
                        bounds_check=VOCAB - 1, oob_is_err=False).then_inc(s["emb"], 16)

            def begin(p):
                pass

            def chunk(p, c):
                if c not in POOL_CHUNKS:
                    return
                if c == POOL_CHUNKS[0]:
                    pool.wait_ge(s["qk_ev"], p + 1)
                if not (isinstance(p, int) and p == 0 and c < TRING):
                    pool.wait_ge(s["score"], p * CH + c - TRING + 1)
                g, cc = c // CPB, c % CPB
                qv = qT[:, g * N:(g + 1) * N].rearrange("p (a m) -> p a m", a=QG)[:, :, 4 * cc:4 * cc + 4]
                kv = kT[:, g * N:(g + 1) * N]
                pool.tensor_tensor(
                    tbuf[:, c % TRING, :].rearrange("p (a m n) -> p a m n", a=QG, m=4),
                    qv.unsqueeze(3).to_broadcast([D, QG, 4, N]),
                    kv.unsqueeze(1).unsqueeze(1).to_broadcast([D, QG, 4, N]), ALU.add).then_inc(s["add_p"], 1)

            def rstd_of(k):
                def f(p):
                    pool.wait_ge(s["ve"], 5 * p + k + 1)
                    pool.tensor_tensor((rstd2 if k == 4 else rstd)[:, :], ve[:, :], neghalf[:, :],
                                       ALU.pow).then_inc(s["rstd"], 1)
                return f

            def x1_bias(p):
                pool.wait_ge(s["x1n"], p + 1)
                pool.tensor_tensor(x1b[:, :, :], x1n[:, :, :],
                                   row["bf2"][:, :].unsqueeze(1).to_broadcast([N, G, D]),
                                   ALU.add).then_inc(s["x1b"], 1)

            def normalise(k):
                def f(p):
                    pool.wait_ge(s["rs2"], 4 * p + k + 1)
                    v = pr[:, 4 * k:4 * k + 4, :]
                    pool.tensor_tensor(v, v, rs2[:, 4 * k:4 * k + 4].unsqueeze(2).to_broadcast([N, 4, N]),
                                       ALU.mult).then_inc(s["pn"], 1)
                return f

            def keep_h(p):
                gate(pool, s["hT"], p + 1)
                pool.tensor_copy(hall[:, bass.ds(p, 1), :], hT[:, :]).then_inc(s["hcopy"], 1)

            def scatter_ids(p):
                if isinstance(p, int) and p == 0:
                    pool.wait_ge(s["tab_init"], 16)
                gate(pool, s["slot"], p + 1)
                if not (isinstance(p, int) and p == 0):
                    gate(pool, s["scat"], p * 16 * G * TOPK)
                pool.tensor_copy(tid_now[:, :], choice[:, bass.ds(p * G * TOPK, G * TOPK)]).then_inc(s["tid"], 1)
                gate(pool, s["tid"], p + 1)
                for g in range(G):
                    for k in range(TOPK):
                        j = g * TOPK + k
                        pool.indirect_dma_start(
                            tab_dram, bass.IndirectOffsetOnAxis(ap=slot_now[:, j:j + 1].bitcast(U32), axis=0),
                            tid_now[:, j:j + 1], None, bounds_check=TABN - 1,
                            oob_is_err=False).then_inc(s["scat"], 16)

            pipeline(pool, begin, chunk,
                     {2: [rstd_of(0)], 3: [x1_bias], 5: [rstd_of(1)], 6: [rstd_of(2)],
                      10: [normalise(0), normalise(1)], 12: [normalise(2), normalise(3)],
                      13: [rstd_of(3), rstd_of(4)], 14: [keep_h], 15: [scatter_ids]},
                     {0: [gather_emb]})

            pool.wait_ge(s["ttab"], 1)
            turns = turns_less(pool, 0)
            pool.wait_ge(s["tn_st"], 16 * TOPK * PAIRS)

            def gather_tile(u, r, again=True):
                t = u * RING + r
                gate(pool, s_i[r], (u + 1) * 16)
                if again:
                    gate(pool, s["tr"], t - RING + 1)
                pool.tensor_copy(igather[:, r:r + 1], iall[:, bass.ds(t, 1)]).then_inc(s["copied"], 1)
                if again:
                    gate(pool, s["copied"], 2 * t - RING + 1)
                else:
                    pool.wait_ge(s["copied"], t + 1)
                pool.indirect_dma_start(
                    hrow[r][:, :], None, tok_dram,
                    bass.IndirectOffsetOnAxis(ap=igather[:, r:r + 1].bitcast(U32), axis=0),
                    bounds_check=TOPK * T - 1, oob_is_err=False).then_inc(s_h[r], 16)

            def scatter_tile(u, r, after):
                t = u * RING + r
                gate(pool, s["eo"], t + 1)
                pool.tensor_copy(iscatter[:, r:r + 1], iall[:, bass.ds(t, 1)]).then_inc(s["copied"], 1)
                gate(pool, s["copied"], after + 1)
                pool.indirect_dma_start(
                    eo_dram, bass.IndirectOffsetOnAxis(ap=iscatter[:, r:r + 1].bitcast(U32), axis=0),
                    eo[r][:, :], None, bounds_check=TOPK * T - 1, oob_is_err=False).then_inc(s_st[r], 16)

            for r in range(RING):
                gather_tile(0, r, again=False)
            with pool.Fori(1, turns) as u:
                for r in range(RING):
                    gather_tile(u, r)
                    scatter_tile(u - 1, r, 2 * (u * RING + r) - RING + 1)
            last = turns_less(pool, 1)
            for r in range(RING):
                scatter_tile(last, r, 2 * RING * last + RING + r)

            def rstd_last(p):
                pool.wait_ge(s["fve"], p + 1)
                pool.tensor_tensor(rstd[:, :], ve[:, :], neghalf[:, :], ALU.pow).then_inc(s["frstd"], 1)

            rstd_last(0)
            with pool.Fori(1, PAIRS) as p:
                rstd_last(p)

        @block.scalar
        def _(act):
            act.preload_act_table(ACT.Exp)
            act.wait_ge(s["early"], 16 * (6 + len(ROWS)))

            def begin(p):
                pass

            def chunk(p, c):
                if c in POOL_CHUNKS:
                    act.wait_ge(s["add_p"], p * len(POOL_CHUNKS) + POOL_CHUNKS.index(c) + 1)
                else:
                    mine = [x for x in range(CH) if x not in POOL_CHUNKS]
                    act.wait_ge(s["add_v"], p * len(mine) + mine.index(c) + 1)
                v = tbuf[:, c % TRING, :]
                act.activation(v, v, ACT.Tanh).then_inc(s["tanh"], 1)

            def xT_copy(p):
                act.wait_ge(s["xs_t"], p + 1)
                act.activation(xT[:, :], p_xT, ACT.Identity).then_inc(s["xT"], 1)

            def exp1(p):
                act.wait_ge(s["nmax"], p + 1)
                for g in range(G):
                    last = act.activation(p1[:, g, :], p_score[:, g, :], ACT.Exp, bias=nmax[:, g:g + 1],
                                          accum_out=esum[:, g:g + 1])
                last.then_inc(s["exp1"], 1)

            def aT_copy(p):
                act.wait_ge(s["aT_ps"], p + 1)
                act.activation(aT[:, :], b_t[:, 0:TN], ACT.Identity).then_inc(s["aT"], 1)

            def x1T_copy(p):
                act.wait_ge(s["x1T_ps"], p + 1)
                act.activation(x1T[:, :], b_t[:, 0:TN], ACT.Identity).then_inc(s["x1T"], 1)

            def relu(p):
                filled(act, p, 0)
                for c in range(2):
                    last = act.activation(hid[:, c, :], big[0][:, c * TN:(c + 1) * TN], ACT.Relu,
                                          bias=bf1[:, c:c + 1])
                last.then_inc(s["big_a"], 1)

            def xaT_copy(p):
                act.wait_ge(s["xaT_ps"], p + 1)
                act.activation(xaT[:, :], b_t[:, 0:TN], ACT.Identity).then_inc(s["xaT"], 1)

            def g_copy(k):
                def f(p):
                    filled(act, p, 2 + k)
                    act.activation(gT[:, 2 * k:2 * k + 2, :].rearrange("p a n -> p (a n)"),
                                   big[(2 + k) % 3][:, 0:2 * TN], ACT.Identity).then_inc(s["big_a"], 1)
                return f

            def vv_copy(k):
                def f(p):
                    filled(act, p, 6 + k)
                    act.activation(vv[:, k // 2, (k % 2) * 512:(k % 2 + 1) * 512],
                                   big[(6 + k) % 3][0:N, :], ACT.Identity).then_inc(s["big_a"], 1)
                return f

            def exp2(k):
                def f(p):
                    act.wait_ge(s["nb2"], 4 * p + k + 1)
                    for j in range(4 * k, 4 * k + 4):
                        last = act.activation(pr[:, j, :], pr[:, j, :], ACT.Exp, bias=nb2[:, j:j + 1],
                                              scale=SCALE, accum_out=es2[:, j:j + 1])
                    last.then_inc(s["exp2"], 1)
                return f

            def prT_copy(k):
                def f(p):
                    filled(act, p, 14 + k)
                    act.activation(prT[:, 4 * k:4 * k + 4, :].rearrange("p a n -> p (a n)"),
                                   big[(14 + k) % 3][0:N, 0:4 * N], ACT.Identity).then_inc(s["big_a"], 1)
                return f

            def hT_affine(p):
                act.wait_ge(s["hT_ps"], p + 1)
                if not (isinstance(p, int) and p == 0):
                    act.wait_ge(s["hcopy"], p)
                act.activation(hT[:, :], b_t[:, 0:TN], ACT.Identity, bias=ln1_b, scale=ln1_g).then_inc(s["hT"], 1)

            def rT_copy(p):
                act.wait_ge(s["rT_ps"], p + 1)
                act.activation(rT[:, :], b_t[0:DR, 0:TN], ACT.Identity).then_inc(s["rT"], 1)

            def gate_exp(p):
                act.wait_ge(s["gap"], p + 1)
                act.activation(egap[:, :], gap[:, :], ACT.Exp, scale=1.0 / TEMP).then_inc(s["egap"], 1)

            pipeline(act, begin, chunk,
                     {-1: [exp1], 1: [aT_copy], 3: [x1T_copy], 4: [relu], 7: [xaT_copy],
                      8: [g_copy(0), g_copy(2)], 9: [vv_copy(0), vv_copy(2)],
                      10: [exp2(0), exp2(1)], 11: [exp2(2), exp2(3)], 12: [prT_copy(0), prT_copy(2)],
                      14: [hT_affine, rT_copy], 15: [gate_exp]},
                     {5: [xT_copy]})

            act.preload_act_table(ACT.Silu)
            act.wait_ge(s["ttab"], 1)
            turns = turns_less(act, 0)

            def silu(u, r):
                t = u * RING + r
                act.wait_ge(s["g1"], t + 1)
                for c in range(FC):
                    last = act.activation(act_h[:, r, c * TILE:(c + 1) * TILE],
                                          big[r][:, c * TILE:(c + 1) * TILE], ACT.Silu,
                                          bias=wbuf[:, r, 2 * DFF + c:2 * DFF + c + 1])
                last.then_inc(s["silu"], 1)

            for r in range(RING):
                silu(0, r)
            with act.Fori(1, turns) as u:
                for r in range(RING):
                    silu(u, r)

            def silu_shared(p):
                act.wait_ge(s["sh_ps"], p + 1)
                for c in range(SC2):
                    last = act.activation(sh[:, c, :], b_t[:, c * TN:(c + 1) * TN], ACT.Silu,
                                          bias=bs1[:, c:c + 1])
                last.then_inc(s["sh"], 1)

            def silu_last(p):
                for c in range(FC):
                    if c % 2 == 0:
                        act.wait_ge(s["f1"], 2 * p + c // 2 + 1)
                    last = act.activation(fh[:, c, :], big[c // 2][:, (c % 2) * TN:(c % 2 + 1) * TN],
                                          ACT.Silu, bias=fbf1[:, c:c + 1])
                last.then_inc(s["fa"], 1)

            silu_shared(0)
            silu_shared(1)
            silu_last(0)
            with act.Fori(2, PAIRS) as p:
                silu_shared(p)
                silu_last(p - 1)
            silu_last(PAIRS - 1)

        @block.vector
        def _(dve):
            class Chain:
                count, base, first = 0, None, 0

                def link(self, ins):
                    self.count += 1
                    ins.then_inc(s["chain"], 1)

                def now(self):
                    return self.count if self.base is None else self.base + self.count

                def wait(self):
                    dve.wait_ge(s["chain"], self.now())

                def gate(self):
                    gate(dve, s["chain"], self.now())

                def enter(self, p):
                    self.start, self.first = self.count, p

                def at(self, p):
                    self.base = p * DVE_LINKS + (self.start - self.first * DVE_LINKS)
                    self.count = 0

                def leave(self, p):
                    assert self.count == DVE_LINKS, self.count
                    self.base, self.count = None, self.start + (p - self.first) * DVE_LINKS

            ch = Chain()

            dve.wait_ge(s["ids"], 16)
            ch.link(dve.tensor_copy(tok_f[:, :], tok_i[:, :]))
            ch.wait()
            ch.link(dve.tensor_scalar(neg_f[:, :], tok_f[:, :], 0.0, float(VOCAB), ALU.is_lt, ALU.mult))
            ch.wait()
            ch.link(dve.tensor_tensor(tok_f[:, :], tok_f[:, :], neg_f[:, :], ALU.add))
            ch.wait()
            dve.tensor_scalar(eidx[:, :], tok_f[:, :], 0.0, float(VOCAB - 1), ALU.max, ALU.min).then_inc(s["ids"], 1)
            dve.wait_ge(s["early"], 16 * (6 + len(ROWS)))
            dve.wait_ge(s["pool_c"], 8 + RING)
            dve.tensor_scalar(bs2q[:, :], row["bs2"][:, :], SHARED, None, ALU.mult)
            dve.tensor_copy(apad[:, 31:32], ascale).then_inc(s["consts"], 1)

            def begin(p):
                dve.wait_ge(s["qkv"], p + 1)
                if not (isinstance(p, int) and p == 0):
                    dve.wait_ge(s["add_p"], p * len(POOL_CHUNKS))
                    dve.wait_ge(s["add_v"], p * (CH - len(POOL_CHUNKS)))
                dve.tensor_scalar(qT[:, :], b_qk[:, 0:TN], bq, None, ALU.add)
                dve.tensor_scalar(kT[:, :], b_qk[:, TN:2 * TN], bk, None, ALU.add).then_inc(s["qk_ev"], 1)
                dve.wait_ge(s["qk_ev"], p + 1)
                if isinstance(p, int) and p == 0:
                    v_copy(0)

            def chunk(p, c):
                if c in POOL_CHUNKS:
                    return
                if not (isinstance(p, int) and p == 0 and c < TRING):
                    dve.wait_ge(s["score"], p * CH + c - TRING + 1)
                g, cc = c // CPB, c % CPB
                qv = qT[:, g * N:(g + 1) * N].rearrange("p (a m) -> p a m", a=QG)[:, :, 4 * cc:4 * cc + 4]
                kv = kT[:, g * N:(g + 1) * N]
                dve.tensor_tensor(
                    tbuf[:, c % TRING, :].rearrange("p (a m n) -> p a m n", a=QG, m=4),
                    qv.unsqueeze(3).to_broadcast([D, QG, 4, N]),
                    kv.unsqueeze(1).unsqueeze(1).to_broadcast([D, QG, 4, N]), ALU.add).then_inc(s["add_v"], 1)

            def v_copy(p):
                dve.wait_ge(s["qkv"], p + 1)
                dve.tensor_tensor(vrow[:, :, :], p_v, row["bv"][:, :].unsqueeze(1).to_broadcast([N, G, D]),
                                  ALU.add).then_inc(s["v_ev"], 1)

            def next_v(p):
                if not (isinstance(p, int) and p == PAIRS - 1):
                    v_copy(p + 1)

            def x_rows(p):
                dve.wait_ge(s["emb"], 16 * G * (p + 1))
                dve.scalar_tensor_tensor(xs[:, :, :], emb_rows[:, :, :], float(np.float32(D) ** np.float32(0.5)),
                                         pe_rows[:, :].unsqueeze(1).to_broadcast([N, G, D]),
                                         ALU.mult, ALU.add).then_inc(s["xs"], 1)
                dve.wait_ge(s["xs"], p + 1)
                dve.tensor_tensor(res[:, bass.ds(p, 1), :, :].rearrange("p a g d -> p (a g) d"), xs[:, :, :],
                                  row["bo"][:, :].unsqueeze(1).to_broadcast([N, G, D]), ALU.add).then_inc(s["res"], 1)

            def softmax1_max(p):
                dve.wait_ge(s["score"], CH * (p + 1))
                dve.tensor_reduce(nmax[:, :], p_score, AX.X, ALU.max, negate=True).then_inc(s["nmax"], 1)

            def p1T_copy(p):
                dve.wait_ge(s["exp1"], p + 1)
                ch.link(dve.reciprocal(rsum[:, :], esum[:, :]))
                dve.wait_ge(s["p1t_ps"], p + 1)
                dve.tensor_copy(p1T[:, :, :].rearrange("p g n -> p (g n)"), b_t[0:N, 0:TN]).then_inc(s["p1T"], 1)

            def ln_stats(p, k, x, eps):
                for g in range(G):
                    last = dve.bn_stats(stat[:, g, :], x[:, g, :])
                ch.link(last)
                ch.gate()
                for g in range(G):
                    last = dve.bn_aggr(mv[:, g, :], stat[:, g, :])
                ch.link(last)
                ch.wait()
                dve.tensor_scalar(ve[:, :], mv[:, :, 1], eps, None, ALU.add).then_inc(s["ve"], 1)

            def ln_apply(p, k, x, y):
                dve.wait_ge(s["rstd"], 5 * p + k + 1)
                for g in range(G):
                    last = dve.tensor_scalar(y[:, g, :], x[:, g, :], mv[:, g, 0:1], rstd[:, g:g + 1],
                                             ALU.subtract, ALU.mult)
                return last

            def gamma_beta(gamma, beta, y):
                ch.wait()
                ch.link(dve.tensor_tensor(xg[:, :, :], xn[:, :, :],
                                          row[gamma][:, :].unsqueeze(1).to_broadcast([N, G, D]), ALU.mult))
                ch.wait()
                return dve.tensor_tensor(y[:, :, :], xg[:, :, :],
                                         row[beta][:, :].unsqueeze(1).to_broadcast([N, G, D]), ALU.add)

            def x1_rows(p):
                dve.wait_ge(s["y"], p + 1)
                ch.wait()
                for g in range(G):
                    last = dve.scalar_tensor_tensor(
                        x1[:, g, :], p_y[:, g, :], rsum[:, g:g + 1],
                        res[:, bass.ds(p, 1), g, :].rearrange("p a d -> p (a d)"), ALU.mult, ALU.add)
                ch.link(last)
                ch.wait()
                ln_stats(p, 0, x1, EPS_TOK)

            def x1_norm(p):
                ch.link(ln_apply(p, 0, x1, xn))
                gamma_beta("g1", "beta1", x1n).then_inc(s["x1n"], 1)

            def relu(p):
                filled(dve, p, 1)
                for c in range(2, 4):
                    last = dve.tensor_scalar(hid[:, c, :], big[1][:, (c - 2) * TN:(c - 1) * TN], bf1[:, c:c + 1],
                                             0.0, ALU.add, ALU.max)
                last.then_inc(s["big_v"], 1)

            def x2_rows(p):
                dve.wait_ge(s["y2"], p + 1)
                dve.wait_ge(s["x1b"], p + 1)
                ch.link(dve.tensor_tensor(x2[:, :, :], p_y, x1b[:, :, :], ALU.add))
                ch.wait()
                ln_stats(p, 1, x2, EPS_TOK)

            def x2_norm(p):
                ch.link(ln_apply(p, 1, x2, xn))
                ch.link(gamma_beta("g2", "beta2", h0))
                ch.wait()
                ln_stats(p, 2, h0, EPS)

            def xa_norm(p):
                ln_apply(p, 2, h0, xa).then_inc(s["xa"], 1)

            def g_copy(k):
                def f(p):
                    filled(dve, p, 2 + k)
                    dve.tensor_copy(gT[:, 2 * k:2 * k + 2, :].rearrange("p a n -> p (a n)"),
                                    big[(2 + k) % 3][:, 0:2 * TN]).then_inc(s["big_v"], 1)
                return f

            def vv_copy(k):
                def f(p):
                    filled(dve, p, 6 + k)
                    dve.tensor_copy(vv[:, k // 2, (k % 2) * 512:(k % 2 + 1) * 512],
                                    big[(6 + k) % 3][0:N, :]).then_inc(s["big_v"], 1)
                return f

            def mask_max(k):
                def f(p):
                    filled(dve, p, 10 + k, alone=True)
                    for j in range(4):
                        h = 4 * k + j
                        last = dve.tensor_tensor_reduce(
                            pr[:, h, :], big[(10 + k) % 3][0:N, j * N:(j + 1) * N], mask[:, :],
                            1.0, -3.0e38, ALU.add, ALU.max, mx2[:, h:h + 1])
                    last.then_inc(s["big_v"], 1)
                    rest = [x for x in range(BIGS) if x not in ACT_BIG]
                    dve.wait_ge(s["big_v"], p * len(rest) + rest.index(10 + k) + 1)
                    dve.tensor_scalar(nb2[:, 4 * k:4 * k + 4], mx2[:, 4 * k:4 * k + 4], -SCALE, None,
                                      ALU.mult).then_inc(s["nb2"], 1)
                return f

            def inv_sums(k):
                def f(p):
                    dve.wait_ge(s["exp2"], 4 * p + k + 1)
                    dve.reciprocal(rs2[:, 4 * k:4 * k + 4], es2[:, 4 * k:4 * k + 4]).then_inc(s["rs2"], 1)
                return f

            def prT_copy(k):
                def f(p):
                    filled(dve, p, 14 + k)
                    dve.tensor_copy(prT[:, 4 * k:4 * k + 4, :].rearrange("p a n -> p (a n)"),
                                    big[(14 + k) % 3][0:N, 0:4 * N]).then_inc(s["big_v"], 1)
                return f

            def h1_rows(p):
                dve.wait_ge(s["o"], p + 1)
                ch.link(dve.tensor_tensor(h1[:, :, :], p_y, h0[:, :, :], ALU.add))
                ch.wait()
                ln_stats(p, 3, h1, EPS)

            def h1_norm(p):
                ch.link(ln_apply(p, 3, h1, h1n))
                ch.link(dve.tensor_tensor(vr[:, :], mv[:, :, 1], rstd[:, :], ALU.mult))
                ch.wait()
                ch.link(dve.tensor_tensor(vr[:, :], vr[:, :], rstd[:, :], ALU.mult))
                ch.wait()
                dve.tensor_scalar(ve[:, :], vr[:, :], EPS, None, ALU.add).then_inc(s["ve"], 1)
                dve.tensor_tensor(res[:, bass.ds(p, 1), :, :].rearrange("p a g d -> p (a g) d"),
                                  h1[:, :, :], h1n[:, :, :], ALU.add).then_inc(s["res"], 1)
                dve.wait_ge(s["rstd"], 5 * p + 5)
                if not (isinstance(p, int) and p == 0):
                    dve.wait_ge(s["tn_st"], 16 * TOPK * p)
                for g in range(G):
                    last = dve.tensor_scalar(tn[:, g, :], h1n[:, g, :], rstd2[:, g:g + 1], None, ALU.mult)
                last.then_inc(s["tn"], 1)

            def route(p):
                dve.wait_ge(s["lg"], p + 1)
                ch.link(dve.tensor_copy(lg[:, :, :].rearrange("p g e -> p (g e)"), p_lg))
                ch.gate()
                for g in range(G):
                    last = dve.max(top[:, g, :], lg[:, g, :])
                ch.link(last)
                ch.gate()
                for g in range(G):
                    last = dve.max_index(topi[:, g, :], top[:, g, :], lg[:, g, :])
                ch.link(last)
                dve.tensor_tensor(gap[:, :], top[:, :, 1], top[:, :, 0], ALU.subtract).then_inc(s["gap"], 1)
                ch.wait()
                ch.link(dve.tensor_copy(topf[:, :].rearrange("p (g k) -> p g k", g=G), topi[:, :, 0:TOPK]))
                ch.wait()
                for g in range(G):
                    for k in range(TOPK):
                        j = g * TOPK + k
                        last = dve.tensor_scalar(oh[:, g, k, :], iota_e[0:N, :], topf[:, j:j + 1], None,
                                                 ALU.is_equal)
                ch.link(last)
                ch.wait()
                dve.tensor_tensor(ohs[:, :, :], oh[:, :, 0, :], oh[:, :, 1, :], ALU.add).then_inc(s["oh"], 1)
                dve.wait_ge(s["egap"], p + 1)
                ch.link(dve.tensor_scalar(egap1[:, :], egap[:, :], 1.0, None, ALU.add))
                ch.wait()
                ch.link(dve.reciprocal(wnow[:, :, 0], egap1[:, :]))
                ch.wait()
                ch.link(dve.tensor_tensor(wnow[:, :, 1], egap[:, :], wnow[:, :, 0], ALU.mult))
                ch.wait()
                dve.tensor_scalar(wts[:, bass.ds(p, 1), :].rearrange("p a j -> p (a j)"),
                                  wnow[:, :, :].rearrange("p g k -> p (g k)"), 1.0, None,
                                  ALU.mult).then_inc(s["res"], 1)

            def ranks(p):
                dve.wait_ge(s["rank_ps"], p + 1)
                for g in range(G):
                    for k in range(TOPK):
                        j = g * TOPK + k
                        last = dve.tensor_tensor_reduce(rjunk[:, j, :], p_rank[:, g, :], oh[:, g, k, :], 1.0, 0.0,
                                                        ALU.mult, ALU.add, rank[:, j:j + 1])
                last.then_inc(s["rank"], 1)
                ch.link(dve.tensor_tensor(cum[:, :], cum[:, :], ohs[:, 0, :], ALU.add))
                ch.wait()
                ch.link(dve.tensor_tensor(cum[:, :], cum[:, :], ohs[:, 1, :], ALU.add))
                ch.wait()
                ch.link(dve.scalar_tensor_tensor(slotf[:, :], topf[:, :], float(T), rank[:, :], ALU.mult, ALU.add))
                ch.wait()
                if not (isinstance(p, int) and p == 0):
                    dve.wait_ge(s["scat"], p * 16 * G * TOPK)
                dve.tensor_scalar(slot_now[:, :], slotf[:, :], 1.0, None, ALU.mult).then_inc(s["slot"], 1)

            def products():
                for i in range(4):
                    dve.wait_ge(s["raw_mm"], i + 1)
                    bank = [big[0], big[1], big[2], b_t][i]
                    dst = (mh if i < 2 else vo)[:, (i % 2) * 512:(i % 2 + 1) * 512]
                    dve.tensor_copy(dst, bank[:, :]).then_inc(s["raw_ev"], 1)

            def pre_or_products(p):
                x_rows(p)
                if isinstance(p, int) and p == 0:
                    products()

            pipeline(dve, begin, chunk,
                     {-1: [softmax1_max], 0: [p1T_copy], 1: [x1_rows], 2: [next_v], 3: [x1_norm], 4: [relu],
                      5: [x2_rows], 6: [x2_norm], 7: [xa_norm], 8: [g_copy(1), g_copy(3)],
                      9: [vv_copy(1), vv_copy(3)], 10: [mask_max(0), mask_max(1), inv_sums(0), inv_sums(1)],
                      11: [mask_max(2), mask_max(3), inv_sums(2), inv_sums(3)],
                      12: [prT_copy(1), prT_copy(3)], 13: [h1_rows, h1_norm], 15: [route, ranks]},
                     {5: [pre_or_products]}, ch)

            dve.wait_ge(s["cnt"], 1)
            ch.link(dve.tensor_scalar(cnti[:, :], b_t[0:MAXT, 0:E], float(TILE - 1), None, ALU.add))
            ch.wait()
            ch.link(dve.tensor_scalar(cnti[:, :], cnti[:, :], TILE.bit_length() - 1, None, ALU.logical_shift_right))
            ch.wait()
            ch.link(dve.tensor_copy(ntf[:, :], cnti[:, :]))
            ch.link(dve.memset(cntf[:, :], 1.0))
            ch.wait()
            ch.link(dve.tensor_tensor_scan(tend[:, :], cntf[:, :], ntf[:, :], 0.0, ALU.mult, ALU.add))
            ch.wait()
            ch.link(dve.tensor_scalar(le[:, :], tend[:, :], iota_t[0:MAXT, 0:1], None, ALU.is_le))
            ch.wait()
            ch.link(dve.tensor_reduce(tcol[:, 0:1], le[:, :], AX.X, ALU.add))
            ch.link(dve.tensor_tensor_reduce(lejunk[:, :], le[:, :], ntf[:, :], 1.0, 0.0, ALU.mult, ALU.add,
                                             tcol[:, 1:2]))
            ch.wait()
            ch.link(dve.tensor_scalar(tinfo[:, 0:1], tcol[:, 0:1], float(E - 1), None, ALU.min))
            ch.link(dve.tensor_tensor(tcol[:, 2:3], iota_t[0:MAXT, 0:1], tcol[:, 1:2], ALU.subtract))
            ch.link(dve.tensor_scalar(ui[:, :], tend[:, E - 1:E], float(RING - 1), 1.0 / RING, ALU.add, ALU.mult))
            ch.wait()
            ch.link(dve.tensor_scalar(tcol[:, 3:4], tcol[:, 2:3], float(TILE), None, ALU.mult))
            ch.wait()
            ch.link(dve.scalar_tensor_tensor(tcol[:, 4:5], tinfo[:, 0:1], float(T), tcol[:, 3:4], ALU.mult, ALU.add))
            ch.wait()
            dve.tensor_scalar(tinfo[:, 1:2], tcol[:, 4:5], float(TABN - TILE), None, ALU.min)
            ch.link(dve.tensor_copy(tcol[:, 5:6], ui[:, :]))
            ch.wait()
            ch.link(dve.scalar_tensor_tensor(tcol[:, 6:7], tcol[:, 5:6], float(-RING), tend[:, E - 1:E],
                                             ALU.mult, ALU.add))
            ch.wait()
            ch.link(dve.tensor_scalar(tcol[:, 7:8], tcol[:, 6:7], float(-RING), None, ALU.is_le))
            ch.wait()
            for n in range(3):
                last = dve.tensor_scalar(tinfo[:, 2 + n:3 + n], tcol[:, 5:6], tcol[:, 7:8], float(n),
                                         ALU.subtract, ALU.subtract)
            last.then_inc(s["tinfo"], 1)
            dve.wait_ge(s["trow"], 1)
            dve.tensor_copy(ttab[0:1, :], b_y[0:1, 0:2 * MAXT + 3]).then_inc(s["ttab"], 1)
            dve.wait_ge(s["ttab"], 1)
            turns = turns_less(dve, 0)

            def hb_affine(u, r):
                t = u * RING + r
                dve.wait_ge(s["tr"], t + 1)
                dve.tensor_scalar(hbT[:, r, :], b_t[:, 0:TILE], ln1_g, ln1_b, ALU.mult, ALU.add).then_inc(s["hbT"], 1)

            def eo_copy(u, r, again=True):
                t = u * RING + r
                dve.wait_ge(s["g2"], t + 1)
                if again:
                    dve.wait_ge(s_st[r], 16 * u)
                dve.tensor_copy(eo[r][:, :], [b_s, b_qk, b_v][r][:, 0:D]).then_inc(s["eo"], 1)

            hb_affine(0, 0)
            hb_affine(0, 1)
            hb_affine(0, 2)
            eo_copy(0, 0, again=False)
            hb_affine(1, 0)
            eo_copy(0, 1, again=False)
            hb_affine(1, 1)
            eo_copy(0, 2, again=False)
            hb_affine(1, 2)
            eo_copy(1, 0)
            with dve.Fori(2, turns) as u:
                hb_affine(u, 0)
                eo_copy(u - 1, 1)
                hb_affine(u, 1)
                eo_copy(u - 1, 2)
                hb_affine(u, 2)
                eo_copy(u, 0)
            for r in (1, 2):
                eo_copy(turns_less(dve, 1), r)

            def mixture(p):
                ch2.link(dve.tensor_scalar(wl[:, :], wts[:, bass.ds(p, 1), :].rearrange("p a j -> p (a j)"), 1.0,
                                           None, ALU.mult))
                dve.wait_ge(s["er"], 16 * (p + 1))
                ch2.wait()
                for g in range(G):
                    last = dve.scalar_tensor_tensor(hm1[:, g, :], er[:, bass.ds(p, 1), g, 0, :].rearrange("p a d -> p (a d)"), wl[:, 2 * g:2 * g + 1],
                                                    bs2q[:, :], ALU.mult, ALU.add)
                ch2.link(last)
                ch2.wait()
                for g in range(G):
                    last = dve.scalar_tensor_tensor(hm2[:, g, :], er[:, bass.ds(p, 1), g, 1, :].rearrange("p a d -> p (a d)"), wl[:, 2 * g + 1:2 * g + 2],
                                                    hm1[:, g, :], ALU.mult, ALU.add)
                ch2.link(last)
                ch2.wait()
                dve.wait_ge(s["ys"], p + 1)
                ch2.link(dve.scalar_tensor_tensor(hm[:, :, :], p_y, SHARED, hm2[:, :, :], ALU.mult, ALU.add))
                ch2.wait()
                for g in range(G):
                    last = dve.bn_stats(stat[:, g, :], hm[:, g, :])
                ch2.link(last)
                ch2.gate()
                for g in range(G):
                    last = dve.bn_aggr(mv[:, g, :], stat[:, g, :])
                ch2.link(last)
                ch2.wait()
                dve.tensor_scalar(ve[:, :], mv[:, :, 1], EPS, None, ALU.add).then_inc(s["fve"], 1)
                ch2.link(dve.tensor_tensor(rh2[:, :, :], hm[:, :, :],
                                           res[:, bass.ds(p, 1), :, :].rearrange("p a g d -> p (a g) d"), ALU.add))
                dve.wait_ge(s["frstd"], p + 1)
                for g in range(G):
                    last = dve.tensor_scalar(fn[:, g, :], hm[:, g, :], mv[:, g, 0:1], rstd[:, g:g + 1],
                                             ALU.subtract, ALU.mult)
                last.then_inc(s["fn"], 1)

            def f_affine(p):
                dve.wait_ge(s["fT_ps"], p + 1)
                dve.tensor_scalar(fT[:, :], b_v[:, 0:TN], ffln_g, ffln_b, ALU.mult, ALU.add).then_inc(s["fT"], 1)

            def keep_rh(p):
                if not (isinstance(p, int) and p == 0):
                    dve.wait_ge(s["of"], p)
                ch2.wait()
                ch2.link(dve.tensor_tensor(rh[:, :, :], rh2[:, :, :],
                                           row["fbf2"][:, :].unsqueeze(1).to_broadcast([N, G, D]), ALU.add))

            def output(p):
                dve.wait_ge(s["f2"], p + 1)
                ch2.wait()
                if not (isinstance(p, int) and p == 0):
                    dve.wait_ge(s["out"], 16 * p)
                dve.tensor_tensor(of[:, :, :], b_s[0:N, 0:G * D].rearrange("p (g n) -> p g n", g=G),
                                  rh[:, :, :], ALU.add).then_inc(s["of"], 1)

            class Chain2(Chain):
                def at(self, p):
                    self.base = p * 8 + (self.start - self.first * 8)
                    self.count = 0

                def leave(self, p):
                    assert self.count == 8, self.count
                    self.base, self.count = None, self.start + (p - self.first) * 8

            ch2 = Chain2()
            ch2.count = ch.count
            mixture(0)
            f_affine(0)
            keep_rh(0)
            mixture(1)
            f_affine(1)
            output(0)
            keep_rh(1)
            ch2.enter(2)
            with dve.Fori(2, PAIRS - 1) as p:
                ch2.at(p)
                mixture(p)
                f_affine(p)
                output(p - 1)
                keep_rh(p)
            ch2.leave(PAIRS - 1)
            mixture(PAIRS - 1)
            f_affine(PAIRS - 1)
            output(PAIRS - 2)
            keep_rh(PAIRS - 1)
            output(PAIRS - 1)

        @block.tensor
        def _(pe):
            pe.wait_ge(s["early"], 16 * (6 + len(ROWS)))

            def begin(p):
                pass

            def chunk(p, c):
                if c == 0:
                    if isinstance(p, int) and p == 0:
                        pe.wait_ge(s["consts"], 1)
                    else:
                        pe.wait_ge(s["exp1"], p)
                pe.wait_ge(s["tanh"], p * CH + c + 1)
                g, cc = c // CPB, c % CPB
                for m in range(4):
                    col = 4 * cc + m
                    for a in range(QG):
                        j = a * 4 + m
                        last = pe.matmul(b_s[32 * a:32 * a + 32, g * N:(g + 1) * N], apad[:, 31 - col:63 - col],
                                         tbuf[:, c % TRING, j * N:(j + 1) * N],
                                         start=(cc == 0 and m == 0), stop=(cc == CPB - 1 and m == 3))
                last.then_inc(s["score"], 1)

            def xs_turn(p):
                pe.wait_ge(s["xs"], p + 1)
                if not (isinstance(p, int) and p == 0):
                    pe.wait_ge(s["v_ev"], p)
                for g in range(G):
                    last = pe.transpose(p_xT[:, g * N:(g + 1) * N], xs[:, g, :], ident[0:N, 0:N])
                last.then_inc(s["xs_t"], 1)

            def qkv(p):
                pe.wait_ge(s["xT"], p + 1)
                if not (isinstance(p, int) and p == 0):
                    pe.wait_ge(s["qk_ev"], p)
                for i in range(2):
                    pe.matmul(b_qk[:, i * TN:(i + 1) * TN], wqkv[:, i, :], xT[:, :], start=True, stop=True)
                for g in range(G):
                    last = pe.matmul(p_v[:, g, :], xT[:, g * N:(g + 1) * N], wqkv[:, 2, :], start=True, stop=True)
                last.then_inc(s["qkv"], 1)

            def products():
                pe.wait_ge(s["late"], 16 * 15)
                for i in range(4):
                    bank = [big[0], big[1], big[2], b_t][i]
                    for j in range(4):
                        h = (i % 2) * 4 + j
                        a, b = (0, 1) if i < 2 else (2, 3)
                        last = pe.matmul(bank[:, j * D:(j + 1) * D], raw[:, a, h * D:(h + 1) * D],
                                         raw[:, b, h * D:(h + 1) * D], start=True, stop=True)
                    last.then_inc(s["raw_mm"], 1)

            def p1_turn(p):
                if isinstance(p, int) and p == 0:
                    pe.wait_ge(s["raw_ev"], 4)
                pe.wait_ge(s["exp1"], p + 1)
                for g in range(G):
                    last = pe.transpose(b_t[0:N, g * N:(g + 1) * N], p1[:, g, :], ident[0:N, 0:N])
                last.then_inc(s["p1t_ps"], 1)

            def attend1(p):
                pe.wait_ge(s["p1T"], p + 1)
                pe.wait_ge(s["v_ev"], p + 1)
                for g in range(G):
                    last = pe.matmul(b_t[:, g * N:(g + 1) * N], vrow[:, g, :], p1T[:, g, :], start=True, stop=True)
                last.then_inc(s["aT_ps"], 1)
                pe.wait_ge(s["aT"], p + 1)
                if not (isinstance(p, int) and p == 0):
                    pe.wait_ge(s["rank"], p)
                for g in range(G):
                    last = pe.matmul(p_y[:, g, :], aT[:, g * N:(g + 1) * N], wo[:, :], start=True, stop=True)
                last.then_inc(s["y"], 1)

            def x1_turn(p):
                pe.wait_ge(s["x1n"], p + 1)
                for g in range(G):
                    last = pe.transpose(b_t[:, g * N:(g + 1) * N], x1n[:, g, :], ident[0:N, 0:N])
                last.then_inc(s["x1T_ps"], 1)

            def ffn1(p):
                pe.wait_ge(s["x1T"], p + 1)
                for c in range(FC):
                    if c % 2 == 0:
                        big_freed(pe, p, c // 2)
                    last = pe.matmul(big[c // 2][:, (c % 2) * TN:(c % 2 + 1) * TN], w1[:, c * D:(c + 1) * D],
                                     x1T[:, :], start=True, stop=True)
                    if c % 2:
                        last.then_inc(s["big"], 1)

            def ffn2(p):
                emptied(pe, p, 0)
                emptied(pe, p, 1)
                for g in range(G):
                    for c in range(FC):
                        last = pe.matmul(p_y[:, g, :], hid[:, c, g * N:(g + 1) * N], w2[:, c, :],
                                         start=(c == 0), stop=(c == FC - 1))
                last.then_inc(s["y2"], 1)

            def xa_turn(p):
                pe.wait_ge(s["xa"], p + 1)
                for g in range(G):
                    last = pe.transpose(b_t[:, g * N:(g + 1) * N], xa[:, g, :], ident[0:N, 0:N])
                last.then_inc(s["xaT_ps"], 1)

            def heads_g(p):
                pe.wait_ge(s["xaT"], p + 1)
                for k in range(4):
                    big_freed(pe, p, 2 + k)
                    for j in range(2):
                        h = 2 * k + j
                        last = pe.matmul(big[(2 + k) % 3][:, j * TN:(j + 1) * TN], mh[:, h * D:(h + 1) * D],
                                         xaT[:, :], start=True, stop=True)
                    last.then_inc(s["big"], 1)

            def heads_v(p):
                for k in range(4):
                    big_freed(pe, p, 6 + k)
                    g = k // 2
                    pe.matmul(big[(6 + k) % 3][0:N, :], xaT[:, g * N:(g + 1) * N],
                              vo[:, (k % 2) * 512:(k % 2 + 1) * 512], start=True, stop=True).then_inc(s["big"], 1)

            def scores(k):
                def f(p):
                    if k == 0:
                        emptied(pe, p, 4)
                    big_freed(pe, p, 10 + k)
                    g = k // 2
                    for j in range(4):
                        h = (k % 2) * 4 + j
                        last = pe.matmul(big[(10 + k) % 3][0:N, j * N:(j + 1) * N], gT[:, h, g * N:(g + 1) * N],
                                         xaT[:, g * N:(g + 1) * N], start=True, stop=True)
                    last.then_inc(s["big"], 1)
                return f

            def pr_turn(k):
                def f(p):
                    big_freed(pe, p, 14 + k)
                    pe.wait_ge(s["pn"], 4 * p + k + 1)
                    for j in range(4):
                        last = pe.transpose(big[(14 + k) % 3][0:N, j * N:(j + 1) * N], pr[:, 4 * k + j, :],
                                            ident[0:N, 0:N])
                    last.then_inc(s["big"], 1)
                return f

            def attend2(p):
                for u in (16, 17):
                    emptied(pe, p, u)
                for g in range(G):
                    for h in range(H):
                        last = pe.matmul(p_y[:, g, :], prT[:, g * H + h, :], vv[:, g, h * D:(h + 1) * D],
                                         start=(h == 0), stop=(h == H - 1))
                last.then_inc(s["o"], 1)

            def router(p):
                pe.wait_ge(s["tn"], p + 1)
                for g in range(G):
                    last = pe.transpose(b_t[:, g * N:(g + 1) * N], tn[:, g, :], ident[0:N, 0:N])
                last.then_inc(s["hT_ps"], 1)
                pe.wait_ge(s["hT"], p + 1)
                pe.matmul(b_t[0:DR, 0:TN], wr[:, :], hT[:, :], start=True, stop=True).then_inc(s["rT_ps"], 1)
                pe.wait_ge(s["rT"], p + 1)
                for g in range(G):
                    last = pe.matmul(p_lg[:, g * E:(g + 1) * E], rT[:, g * N:(g + 1) * N], cbT[:, :],
                                     start=True, stop=True)
                last.then_inc(s["lg"], 1)

            def ranks(p):
                pe.wait_ge(s["oh"], p + 1)
                for g in range(G):
                    pe.matmul(p_rank[:, g, :], tri[:, :], ohs[:, g, :], start=True, stop=False)
                    if g == 1:
                        pe.matmul(p_rank[:, g, :], ones[:, 0:N], ohs[:, 0, :], start=False, stop=False)
                    last = pe.matmul(p_rank[:, g, :], ones[:, 0:N], cum[:, :], start=False, stop=True)
                last.then_inc(s["rank_ps"], 1)

            def pre_turn(p):
                xs_turn(p)
                if isinstance(p, int) and p == 0:
                    products()

            pipeline(pe, begin, chunk,
                     {-1: [p1_turn], 0: [attend1], 3: [x1_turn], 4: [ffn1], 5: [ffn2], 7: [xa_turn],
                      8: [heads_g], 9: [heads_v], 10: [scores(0), scores(1)], 11: [scores(2), scores(3)],
                      12: [pr_turn(0), pr_turn(1), pr_turn(2), pr_turn(3)], 13: [attend2], 14: [router],
                      15: [ranks]},
                     {5: [pre_turn], 6: [qkv]})

            pe.wait_ge(s["slot"], PAIRS)
            pe.matmul(b_t[0:MAXT, 0:E], ones[:, 0:MAXT], cum[:, :], start=True, stop=True).then_inc(s["cnt"], 1)
            pe.wait_ge(s["tinfo"], 1)
            for i in range(2):
                pe.matmul(b_y[0:1, i * MAXT:(i + 1) * MAXT], tinfo[:, i:i + 1], ident[0:MAXT, 0:MAXT],
                          start=True, stop=True)
            for i in range(3):
                last = pe.matmul(b_y[0:1, 2 * MAXT + i:2 * MAXT + i + 1], tinfo[:, 2 + i:3 + i],
                                 ident[0:MAXT, 0:1], start=True, stop=True)
            last.then_inc(s["trow"], 1)
            pe.wait_ge(s["ttab"], 1)
            turns = turns_less(pe, 0)

            def tile_turn(u, r):
                t = u * RING + r
                if not (isinstance(t, int) and t == 0):
                    pe.wait_ge(s["hbT"], t)
                pe.wait_ge(s_h[r], 16 * (u + 1))
                pe.transpose(b_t[:, 0:TILE], hrow[r][:, :], ident[:, :]).then_inc(s["tr"], 1)

            def expert1(u, r):
                t = u * RING + r
                pe.wait_ge(s["hbT"], t + 1)
                pe.wait_ge(s_w[r], 32 * (u + 1))
                for c in range(FC):
                    last = pe.matmul(big[r][:, c * TILE:(c + 1) * TILE], wbuf[:, r, c * D:(c + 1) * D],
                                     hbT[:, r, :], start=True, stop=True)
                last.then_inc(s["g1"], 1)

            def expert2(u, r, before=None):
                t = u * RING + r
                pe.wait_ge(s["silu"], t + 1)
                if before is not None:
                    pe.wait_ge(s["eo"], before * RING + r + 1)
                elif not isinstance(u, int):
                    pe.wait_ge(s["eo"], t - RING + 1)
                o = [b_s, b_qk, b_v][r][:, 0:D]
                for c in range(FC):
                    pe.matmul(o, act_h[:, r, c * TILE:(c + 1) * TILE], wbuf[:, r, DFF + c * D:DFF + (c + 1) * D],
                              start=(c == 0), stop=False)
                pe.matmul(o, ones[0:1, 0:TILE], b2buf[0:1, r, :], start=False, stop=True).then_inc(s["g2"], 1)

            tile_turn(0, 0)
            expert1(0, 0)
            tile_turn(0, 1)
            expert1(0, 1)
            tile_turn(0, 2)
            expert2(0, 0)
            expert1(0, 2)
            tile_turn(1, 0)
            expert2(0, 1)
            with pe.Fori(1, turns - 1) as u:
                expert1(u, 0)
                tile_turn(u, 1)
                expert2(u - 1, 2)
                expert1(u, 1)
                tile_turn(u, 2)
                expert2(u, 0)
                expert1(u, 2)
                tile_turn(u + 1, 0)
                expert2(u, 1)
            u, before = turns_less(pe, 1), turns_less(pe, 2)
            expert1(u, 0)
            tile_turn(u, 1)
            expert2(before, 2)
            expert1(u, 1)
            tile_turn(u, 2)
            expert2(u, 0, before)
            expert1(u, 2)
            expert2(u, 1, before)
            expert2(u, 2, before)

            def shared1(p):
                if not (isinstance(p, int) and p == 0):
                    pe.wait_ge(s["sh"], p)
                for c in range(SC2):
                    last = pe.matmul(b_t[:, c * TN:(c + 1) * TN], ws1[:, c * D:(c + 1) * D],
                                     hall[:, bass.ds(p, 1), :].rearrange("p a n -> p (a n)"),
                                     start=True, stop=True)
                last.then_inc(s["sh_ps"], 1)

            def shared2(p):
                pe.wait_ge(s["sh"], p + 1)
                if not (isinstance(p, int) and p == 0):
                    pe.wait_ge(s["fve"], p)
                for g in range(G):
                    for c in range(SC2):
                        last = pe.matmul(p_y[:, g, :], sh[:, c, g * N:(g + 1) * N], ws2[:, c, :],
                                         start=(c == 0), stop=(c == SC2 - 1))
                last.then_inc(s["ys"], 1)

            def f_turn(p):
                pe.wait_ge(s["fn"], p + 1)
                for g in range(G):
                    last = pe.transpose(b_v[:, g * N:(g + 1) * N], fn[:, g, :], ident[0:N, 0:N])
                last.then_inc(s["fT_ps"], 1)

            def last1(p):
                pe.wait_ge(s["fT"], p + 1)
                if not (isinstance(p, int) and p == 0):
                    pe.wait_ge(s["fa"], p)
                for c in range(FC):
                    last = pe.matmul(big[c // 2][:, (c % 2) * TN:(c % 2 + 1) * TN], wf1[:, c * D:(c + 1) * D],
                                     fT[:, :], start=True, stop=True)
                    if c % 2:
                        last.then_inc(s["f1"], 1)

            def last2(p):
                pe.wait_ge(s["fa"], p + 1)
                if not (isinstance(p, int) and p == 0):
                    pe.wait_ge(s["of"], p)
                for g in range(G):
                    for c in range(FC):
                        last = pe.matmul(b_s[0:N, g * D:(g + 1) * D], fh[:, c, g * N:(g + 1) * N], wf2[:, c, :],
                                         start=(c == 0), stop=(c == FC - 1))
                last.then_inc(s["f2"], 1)

            pe.wait_ge(s["eo"], turns * RING)
            pe.sem_inc(s["gate"], 1)
            shared1(0)
            shared2(0)
            f_turn(0)

            def step(p):
                shared1(p)
                last1(p - 1)
                shared2(p)
                last2(p - 1)
                f_turn(p)

            step(1)
            with pe.Fori(2, PAIRS) as p:
                step(p)
            last1(PAIRS - 1)
            last2(PAIRS - 1)


def _inputs(inputs):
    f = {k: np.ascontiguousarray(np.asarray(v)) for k, v in inputs.items()}
    a = {}
    a["x"] = np.ascontiguousarray(f["x"].T)
    a["L0_tok_emb"] = f["L0_tok_emb"]
    for n in ["L0_tok_Wq", "L0_tok_Wk", "L0_tok_Wv", "L0_tok_Wo", "L0_tok_W1", "L0_tok_W2", "L0_ffn_Wr",
              "L0_ffn_Ws1", "L0_ffn_Ws2", "L0_ffn_Wf1", "L0_ffn_Wf2", "L0_ffn_b2"]:
        a[n] = f[n]
    a["attn_Wq"], a["attn_Wk"], a["attn_Wv"] = f["L0_attn_Wq"], f["L0_attn_Wk"], f["L0_attn_Wv"]
    a["attn_WoT"] = np.ascontiguousarray(f["L0_attn_Wo"].T)
    a["cbT"] = np.ascontiguousarray(f["L0_ffn_codebook"].T)
    for n, src in zip(ROWS, ["L0_tok_bv", "L0_tok_bo", "L0_tok_g1", "L0_tok_beta1", "L0_tok_bf2", "L0_tok_g2",
                             "L0_tok_beta2", "L0_ffn_bs2", "L0_ffn_bf2"]):
        a["row_" + n] = f[src]
    a["cols"] = np.concatenate(
        [f[n].reshape(-1, D).T for n in ["L0_tok_bq", "L0_tok_bk", "L0_tok_attn_scale", "L0_ffn_ln1_g",
                                         "L0_ffn_ln1_b", "L0_ffn_ffln_g", "L0_ffn_ffln_b", "L0_tok_bf1",
                                         "L0_ffn_bs1", "L0_ffn_bf1"]], axis=1)
    w1 = f["L0_ffn_W1"]
    w2 = f["L0_ffn_W2"].reshape(E, FC, D, D).transpose(0, 2, 1, 3).reshape(E, D, DFF)
    b1 = f["L0_ffn_b1"].reshape(E, FC, D).transpose(0, 2, 1)
    a["wpack"] = np.concatenate([w1, w2, b1], axis=2)
    pos = np.arange(N)[:, None].astype(np.float64)
    i = np.arange(D)[None, :]
    ang = pos / np.power(10000.0, 2 * (i // 2) / np.float32(D))
    ang[:, 0::2] = np.sin(ang[:, 0::2])
    ang[:, 1::2] = np.cos(ang[:, 1::2])
    a["pe"] = ang.astype(np.float32)
    a["ident"] = np.eye(128, dtype=np.float32)
    a["mask"] = np.triu(np.full((N, N), NEG, np.float32), 1)
    a["tri"] = np.triu(np.ones((N, N), np.float32), 1)
    return {k: np.ascontiguousarray(v) for k, v in a.items()}


def kernel(**inputs):
    import concourse.bacc as bacc
    from concourse.bass_utils import run_bass_kernel_spmd

    nc = bacc.Bacc("TRN2", target_bir_lowering=False, num_devices=1)
    arrays = _inputs(inputs)
    io = {n: nc.dram_tensor("in_" + n, a.shape, mybir.dt.from_np(a.dtype), kind="ExternalInput").ap()
          for n, a in arrays.items()}
    out = nc.dram_tensor("out", (B, N, D), F32, kind="ExternalOutput").ap()
    program(nc, io, out)
    r = run_bass_kernel_spmd(nc, [{"in_" + n: a for n, a in arrays.items()}], core_ids=[0])
    return r.results[0]["out"]
```

```python
from contextlib import ExitStack

import concourse.bass as bass
import numpy as np
from concourse import mybir

F32 = mybir.dt.float32
I32 = mybir.dt.int32
U32 = mybir.dt.uint32
ACT = mybir.ActivationFunctionType
ALU = mybir.AluOpType
AX = mybir.AxisListType

B, N, D = 32, 96, 128
G = 2
PAIRS = B // G
TN = G * N
T = B * N
VOCAB, DFF, H = 8000, 512, 8
FC = DFF // D
E, DR, TOPK, DSH = 64, 64, 2, 256
SC2 = DSH // D
TILE = 128
RING = 4
MAXT = -(-((T * TOPK - E) // TILE + E) // RING) * RING
TABN = E * T
QG = N // 32
CROWS = 12
CPB = N // CROWS
CH = G * CPB
CW = CROWS * N
DEPTH = 3
TRING = 4
POOL_CHUNKS = (1, 6, 9, 10, 13)
BIGS = 18
ACT_BIG = (0, 2, 4, 6, 8, 14, 16)
EPS_TOK, EPS = 1e-6, 1e-5
SCALE = 1.0 / float(D) ** 0.5
TEMP = 0.7
SHARED = 0.25
NEG = -1.0e30
DVE_LINKS = 31
WCOLS = 2 * DFF + FC

ROWS = ["bv", "bo", "g1", "beta1", "bf2", "g2", "beta2", "bs2", "fbf2"]


def program(nc, io, out):
    with ExitStack() as ctx:
        def sb(name, shape, dt=F32):
            return ctx.enter_context(nc.sbuf_tensor(name, shape, dt))

        def ps(name):
            return ctx.enter_context(nc.psum_tensor(name, [128, 512], F32))

        tok_dram = nc.dram_tensor("tok_dram", (TOPK * T, D), F32).ap()
        tab_dram = nc.dram_tensor("tab_dram", (TABN, 1), I32).ap()
        eo_dram = nc.dram_tensor("eo_dram", (TOPK * T, D), F32).ap()

        ident = sb("ident", [128, 128])
        tri = sb("tri", [N, N])
        ones = sb("ones", [N, 128])
        mask = sb("mask", [N, N])
        pe_rows = sb("pe_rows", [N, D])
        iota_e = sb("iota_e", [128, E])
        iota_t = sb("iota_t", [128, 1])
        row = {n: sb("row_" + n, [N, D]) for n in ROWS}
        wqkv = sb("wqkv", [D, 3, D])
        wo = sb("wo", [D, D])
        w1 = sb("w1", [D, DFF])
        w2 = sb("w2", [D, FC, D])
        spread = sb("spread", [128, PAIRS * G * TOPK * D])
        raw = spread[:, 0:4 * H * D].rearrange("p (a n) -> p a n", a=4)
        mh = sb("mh", [D, H * D])
        vo = sb("vo", [D, H * D])
        wr = sb("wr", [D, DR])
        cbT = sb("cbT", [DR, E])
        ws1 = sb("ws1", [D, DSH])
        ws2 = sb("ws2", [D, SC2, D])
        wf1 = sb("wf1", [D, DFF])
        wf2 = sb("wf2", [D, FC, D])
        cols = sb("cols", [D, 7 + FC + SC2 + FC])
        bq, bk, ascale = cols[:, 0:1], cols[:, 1:2], cols[:, 2:3]
        ln1_g, ln1_b, ffln_g, ffln_b = (cols[:, i:i + 1] for i in range(3, 7))
        bf1 = cols[:, 7:7 + FC]
        bs1 = cols[:, 7 + FC:7 + FC + SC2]
        fbf1 = cols[:, 7 + FC + SC2:]
        apad = sb("apad", [D, 64])
        neghalf = sb("neghalf", [N, G])
        bs2q = sb("bs2q", [N, D])
        sentinel = sb("sentinel", [128, TABN // 128], I32)

        tok_i = sb("tok_i", [N, B], I32)
        tok_f = sb("tok_f", [N, B])
        neg_f = sb("neg_f", [N, B])
        eidx = sb("eidx", [N, B], I32)
        choice = sb("choice", [N, B * TOPK], I32)
        res = sb("res", [N, PAIRS, G, D])
        hall = sb("hall", [D, PAIRS, TN])
        wts = sb("wts", [N, PAIRS, G * TOPK])
        ei_now = sb("ei_now", [N, G], I32)
        tid_now = sb("tid_now", [N, G * TOPK], I32)
        slot_now = sb("slot_now", [N, G * TOPK], I32)
        emb_rows = sb("emb_rows", [N, G, D])
        xs = sb("xs", [N, G, D])
        xT = sb("xT", [D, TN])
        qT = sb("qT", [D, TN])
        kT = sb("kT", [D, TN])
        vrow = sb("vrow", [N, G, D])
        tbuf = sb("tbuf", [D, TRING, CW])
        nmax = sb("nmax", [N, G])
        esum = sb("esum", [N, G])
        rsum = sb("rsum", [N, G])
        p1 = sb("p1", [N, G, N])
        p1T = sb("p1T", [N, G, N])
        aT = sb("aT", [D, TN])
        x1 = sb("x1", [N, G, D])
        xn = sb("xn", [N, G, D])
        xg = sb("xg", [N, G, D])
        x1n = sb("x1n", [N, G, D])
        x1b = sb("x1b", [N, G, D])
        x1T = sb("x1T", [D, TN])
        hid = sb("hid", [D, FC, TN])
        x2 = sb("x2", [N, G, D])
        h0 = sb("h0", [N, G, D])
        xa = sb("xa", [N, G, D])
        xaT = sb("xaT", [D, TN])
        gT = sb("gT", [D, H, TN])
        vv = sb("vv", [N, G, H * D])
        pr = sb("pr", [N, G * H, N])
        prT = sb("prT", [N, G * H, N])
        mx2 = sb("mx2", [N, G * H])
        nb2 = sb("nb2", [N, G * H])
        es2 = sb("es2", [N, G * H])
        rs2 = sb("rs2", [N, G * H])
        h1 = sb("h1", [N, G, D])
        h1n = sb("h1n", [N, G, D])
        tn = sb("tn", [N, G, D])
        hT = sb("hT", [D, TN])
        rT = sb("rT", [DR, TN])
        lg = sb("lg", [N, G, E])
        top = sb("top", [N, G, 8])
        topi = sb("topi", [N, G, 8], U32)
        topf = sb("topf", [N, G * TOPK])
        gap = sb("gap", [N, G])
        egap = sb("egap", [N, G])
        egap1 = sb("egap1", [N, G])
        wnow = sb("wnow", [N, G, TOPK])
        oh = sb("oh", [N, G, TOPK, E])
        ohs = sb("ohs", [N, G, E])
        cum = sb("cum", [N, E])
        rjunk = sb("rjunk", [N, G * TOPK, E])
        rank = sb("rank", [N, G * TOPK])
        slotf = sb("slotf", [N, G * TOPK])
        stat = sb("stat", [N, G, 6])
        mv = sb("mv", [N, G, 2])
        ve = sb("ve", [N, G])
        mv2 = sb("mv2", [N, G, 2])
        ve2 = sb("ve2", [N, G])
        rstd3 = sb("rstd3", [N, G])
        rstd = sb("rstd", [N, G])
        vr = sb("vr", [N, G])
        rstd2 = sb("rstd2", [N, G])

        cntf = sb("cntf", [MAXT, E])
        cnti = sb("cnti", [MAXT, E], I32)
        ntf = sb("ntf", [MAXT, E])
        tend = sb("tend", [MAXT, E])
        le = sb("le", [MAXT, E])
        lejunk = sb("lejunk", [MAXT, E])
        tcol = sb("tcol", [MAXT, 8])
        ui = sb("ui", [MAXT, 1], I32)
        uii = sb("uii", [MAXT, 1], I32)
        tinfo = sb("tinfo", [MAXT, 4])
        ttab = sb("ttab", [1, MAXT + 3], I32)
        trow = sb("trow", [MAXT, 1], I32)
        idrows = sb("idrows", [MAXT, TILE], I32)
        idf = sb("idf", [MAXT, TILE])
        wbuf = sb("wbuf", [D, RING, WCOLS])
        b2buf = sb("b2buf", [1, RING, D])
        iall = sb("iall", [TILE, MAXT], I32)
        igather = sb("igather", [TILE, RING], I32)
        iscatter = sb("iscatter", [TILE, RING], I32)
        hrow = [sb(f"hrow{r}", [TILE, D]) for r in range(RING)]
        hbT = sb("hbT", [D, 2, TILE])
        act_h = sb("act_h", [D, 2, DFF])
        eo = [sb(f"eo{r}", [TILE, D]) for r in range(RING)]

        er = spread[0:N, :].rearrange("p (a g k d) -> p a g k d", a=PAIRS, g=G, k=TOPK)
        wl = sb("wl", [N, G * TOPK])
        sh = sb("sh", [D, SC2, TN])
        of = sb("of", [N, G, D])
        hm1, hm2, hm, rh, rh2, fn, fT, fh = x1, x2, h1, x1n, xg, xn, aT, hid

        b_s, b_qk, b_v, b_t, b_y = ps("b_s"), ps("b_qk"), ps("b_v"), ps("b_t"), ps("b_y")
        big = [ps("big0"), ps("big1"), ps("big2")]
        p_score = b_s[0:N, 0:TN].rearrange("p (g n) -> p g n", g=G)
        p_v = b_v[0:N, 0:G * D].rearrange("p (g n) -> p g n", g=G)
        p_o = p_v
        p_xT = b_v[:, 256:256 + TN]
        p_y = b_y[0:N, 0:G * D].rearrange("p (g n) -> p g n", g=G)
        p_lg = b_y[0:N, 0:G * E]
        p_rank = b_y[0:N, 128:128 + G * E].rearrange("p (g n) -> p g n", g=G)

        s = {n: ctx.enter_context(nc.semaphore("s_" + n)) for n in [
            "early", "late", "consts", "gate", "raw_mm", "raw_ev", "pool_c", "tab_init", "ids",
            "emb", "xs", "xs_t", "xT", "qkv", "qk_ev", "v_ev", "add_v", "add_p", "tanh", "score",
            "nmax", "exp1", "p1t_ps", "p1T", "aT_ps", "aT", "y", "x1n", "x1b", "x1T_ps", "x1T",
            "big", "big_a", "big_v", "y2", "xa", "xaT_ps", "xaT", "nb2", "exp2", "rs2", "pn",
            "o", "tn", "tn_st", "hT_ps", "hT", "hcopy", "rT_ps", "rT", "lg", "gap", "egap", "oh",
            "rank_ps", "rank", "slot", "tid", "ei", "scat", "ve", "rstd", "ve2", "rstd2", "chain", "res",
            "cnt", "tinfo", "trow", "ttab",
            "idrows", "idf", "ids_t", "iall", "cg", "cs",
            *[f"{n}{r}" for n in ("w", "h", "st") for r in range(RING)],
            "tr", "hbT", "g1", "silu", "g2", "eo",
            "er", "copied", "sh_ps", "sh", "ys", "hm", "rh", "fve", "frstd", "fn", "fT_ps", "fT", "f1",
            "fa", "f2", "of", "out"]}
        s_w, s_h, s_st = ([s[f"{n}{r}"] for r in range(RING)] for n in ("w", "h", "st"))
        block = ctx.enter_context(nc.Block())

        def gate(eng, sem, value):
            eng.wait_ge(sem, value)
            eng.sem_inc(s["gate"], 1)

        def turns_less(eng, n):
            at = MAXT + n
            return eng.value_load(ttab[0:1, at:at + 1], min_val=T * TOPK // TILE // RING - n,
                                  max_val=MAXT // RING - n)

        def big_freed(eng, p, u):
            u = u - 3
            if u < 0:
                u, p = u + BIGS, p - 1
            if isinstance(p, int) and p < 0:
                return
            emptied(eng, p, u)

        def emptied(eng, p, u):
            if u in ACT_BIG:
                eng.wait_ge(s["big_a"], p * len(ACT_BIG) + ACT_BIG.index(u) + 1)
            else:
                rest = [x for x in range(BIGS) if x not in ACT_BIG]
                eng.wait_ge(s["big_v"], p * len(rest) + rest.index(u) + 1)

        def filled(eng, p, u, alone=False):
            eng.wait_ge(s["big"], p * BIGS + u + 1)
            if alone:
                eng.sem_inc(s["gate"], 1)

        def pipeline(eng, begin, chunk, post, pre, lead, loop=None):
            def put(p, c):
                if c == 0:
                    begin(p)
                chunk(p, c)

            def body(p, posts, is_last):
                for c in range(CH):
                    if lead is not None:
                        if c + lead < CH:
                            put(p, c + lead)
                        elif not is_last:
                            put(p + 1, c + lead - CH)
                    sides(p, c, posts, not is_last)
                    if lead is None:
                        put(p, c)

            def sides(p, c, posts, has_next):
                for k in sorted(posts, reverse=True):
                    for f in post.get(c + (k - 1) * CH, []):
                        f(p - k)
                if has_next:
                    for f in pre.get(c, []):
                        f(p + 1)

            for c in range(CH):
                for f in pre.get(c, []):
                    f(0)
            for c in range(lead or 0):
                put(0, c)
            every = range(1, DEPTH + 1)
            for p in range(DEPTH + 1):
                body(p, range(1, p + 1), False)
            if loop is not None:
                loop.enter(DEPTH + 1)
            with eng.Fori(DEPTH + 1, PAIRS - 1) as p:
                if loop is not None:
                    loop.at(p)
                body(p, every, False)
            if loop is not None:
                loop.leave(PAIRS - 1)
            body(PAIRS - 1, every, True)
            for k in every:
                for c in range(CH):
                    sides(PAIRS - 1 + k, c, every[k - 1:], False)

        @block.sync
        def _(sp):
            def load(dst, src, sem):
                sp.dma_start(dst, src).then_inc(sem, 16)

            load(tok_i[:, :], io["x"], s["ids"])
            load(ident[:, :], io["ident"], s["early"])
            load(wqkv[:, 0, :], io["L0_tok_Wq"], s["early"])
            load(wqkv[:, 1, :], io["L0_tok_Wk"], s["early"])
            load(wqkv[:, 2, :], io["L0_tok_Wv"], s["early"])
            load(cols[:, :], io["cols"], s["early"])
            load(pe_rows[:, :], io["pe"], s["early"])
            for n in ROWS:
                load(row[n][:, :], io["row_" + n].partition_broadcast(N), s["early"])
            for i, n in enumerate(["Wq", "Wk", "Wv", "WoT"]):
                load(raw[:, i, :].rearrange("p (h d) -> p h d", h=H),
                     io["attn_" + n].rearrange("(h k) d -> k h d", h=H), s["late"])
            load(wo[:, :], io["L0_tok_Wo"], s["late"])
            load(w1[:, :], io["L0_tok_W1"], s["late"])
            load(w2[:, :, :], io["L0_tok_W2"].rearrange("(c p) n -> p c n", p=D), s["late"])
            load(wr[:, :], io["L0_ffn_Wr"], s["late"])
            load(cbT[:, :], io["cbT"], s["late"])
            load(mask[:, :], io["mask"], s["late"])
            load(tri[:, :], io["tri"], s["late"])
            load(ws1[:, :], io["L0_ffn_Ws1"], s["late"])
            load(ws2[:, :, :], io["L0_ffn_Ws2"].rearrange("(c p) n -> p c n", p=D), s["late"])
            load(wf1[:, :], io["L0_ffn_Wf1"], s["late"])
            load(wf2[:, :, :], io["L0_ffn_Wf2"].rearrange("(c p) n -> p c n", p=D), s["late"])
            sp.wait_ge(s["pool_c"], 1)
            load(tab_dram.rearrange("(p n) a -> p (n a)", p=128), sentinel[:, :], s["tab_init"])

            def store_tokens(p):
                gate(sp, s["tn"], p + 1)
                rows = tok_dram[bass.ds(p * TN * TOPK, TN * TOPK), :]
                for k in range(TOPK):
                    sp.dma_start(rows.rearrange("(g n k) d -> n g k d", g=G, k=TOPK)[:, :, k, :],
                                 tn[:, :, :]).then_inc(s["tn_st"], 16)

            store_tokens(0)
            with sp.Fori(1, PAIRS) as p:
                store_tokens(p)

            sp.wait_ge(s["ttab"], 1)
            turns = turns_less(sp, 0)

            def load_tile(u, r, again=True):
                t = u * RING + r
                if again:
                    gate(sp, s["g2"], t - RING + 1)
                e = sp.value_load(ttab[0:1, bass.ds(t, 1)], min_val=0, max_val=E - 1)
                sp.dma_start(wbuf[:, r, :], io["wpack"][bass.ds(e, 1), :, :]).then_inc(s_w[r], 16)
                sp.dma_start(b2buf[0:1, r, :], io["L0_ffn_b2"][bass.ds(e, 1), :]).then_inc(s_w[r], 16)

            for r in range(RING):
                load_tile(0, r, again=False)
            with sp.Fori(1, turns) as u:
                for r in range(RING):
                    load_tile(u, r)

            for r in range(RING):
                gate(sp, s_st[r], turns * 16)

            def load_results(p):
                rows = eo_dram[bass.ds(p * TN * TOPK, TN * TOPK), :]
                sp.dma_start(er[:, bass.ds(p, 1), :, :, :].rearrange("n a g k d -> n (a g) (k d)"),
                             rows.rearrange("(g n k) d -> n g (k d)", g=G, k=TOPK)).then_inc(s["er"], 16)

            load_results(0)
            with sp.Fori(1, PAIRS) as p:
                gate(sp, s["er"], 16 * p)
                load_results(p)

            def store_out(p):
                gate(sp, s["of"], p + 1)
                sp.dma_start(out[bass.ds(p * G, G), :, :].rearrange("g n d -> n g d"),
                             of[:, :, :]).then_inc(s["out"], 16)

            store_out(0)
            with sp.Fori(1, PAIRS) as p:
                store_out(p)
            sp.wait_ge(s["out"], 16 * PAIRS)
            sp.wait_ge(s["tn_st"], 16 * TOPK * PAIRS)

        @block.gpsimd
        def _(pool):
            pool.memset(sentinel[:, :], TOPK * T).then_inc(s["pool_c"], 1)
            pool.memset(neghalf[:, :], -0.5).then_inc(s["pool_c"], 1)
            pool.memset(ones[:, :], 1.0).then_inc(s["pool_c"], 1)
            pool.memset(cum[:, :], 0.0).then_inc(s["pool_c"], 1)
            pool.memset(apad[:, :], 0.0).then_inc(s["pool_c"], 1)
            pool.iota(choice[:, :], [[TOPK * N, B], [1, TOPK]], base=0, channel_multiplier=TOPK)\
                .then_inc(s["pool_c"], 1)
            pool.iota(iota_e[:, :], [[1, E]], base=0, channel_multiplier=0,
                      allow_small_or_imprecise_dtypes=True).then_inc(s["pool_c"], 1)
            pool.iota(iota_t[:, :], [[1, 1]], base=0, channel_multiplier=1,
                      allow_small_or_imprecise_dtypes=True).then_inc(s["pool_c"], 1)
            for r in range(RING):
                pool.memset(hrow[r][:, :], 0.0).then_inc(s["pool_c"], 1)

            def gather_emb(p):
                if isinstance(p, int) and p == 0:
                    pool.wait_ge(s["ids"], 17)
                else:
                    gate(pool, s["xs"], p)
                pool.tensor_copy(ei_now[:, :], eidx[:, bass.ds(p * G, G)]).then_inc(s["ei"], 1)
                gate(pool, s["ei"], p + 1)
                for g in range(G):
                    pool.indirect_dma_start(
                        emb_rows[:, g, :], None, io["L0_tok_emb"],
                        bass.IndirectOffsetOnAxis(ap=ei_now[:, g:g + 1].bitcast(U32), axis=0),
                        bounds_check=VOCAB - 1, oob_is_err=False).then_inc(s["emb"], 16)

            def begin(p):
                pass

            def chunk(p, c):
                if c not in POOL_CHUNKS:
                    return
                if c == POOL_CHUNKS[0]:
                    pool.wait_ge(s["qk_ev"], p + 1)
                if not (isinstance(p, int) and p == 0 and c < TRING):
                    pool.wait_ge(s["score"], p * CH + c - TRING + 1)
                g, cc = c // CPB, c % CPB
                qv = qT[:, g * N:(g + 1) * N].rearrange("p (a m) -> p a m", a=QG)[:, :, 4 * cc:4 * cc + 4]
                kv = kT[:, g * N:(g + 1) * N]
                pool.tensor_tensor(
                    tbuf[:, c % TRING, :].rearrange("p (a m n) -> p a m n", a=QG, m=4),
                    qv.unsqueeze(3).to_broadcast([D, QG, 4, N]),
                    kv.unsqueeze(1).unsqueeze(1).to_broadcast([D, QG, 4, N]), ALU.add).then_inc(s["add_p"], 1)

            def rstd_of(k):
                def f(p):
                    pool.wait_ge(s["ve"], 3 * p + k + 1)
                    pool.tensor_tensor(rstd[:, :], ve[:, :], neghalf[:, :], ALU.pow).then_inc(s["rstd"], 1)
                return f

            def rstd2_of(k):
                def f(p):
                    pool.wait_ge(s["ve2"], 2 * p + k + 1)
                    pool.tensor_tensor([rstd2, rstd3][k][:, :], ve2[:, :], neghalf[:, :],
                                       ALU.pow).then_inc(s["rstd2"], 1)
                return f

            def x1_bias(p):
                pool.wait_ge(s["x1n"], p + 1)
                pool.tensor_tensor(x1b[:, :, :], x1n[:, :, :],
                                   row["bf2"][:, :].unsqueeze(1).to_broadcast([N, G, D]),
                                   ALU.add).then_inc(s["x1b"], 1)

            def normalise(k):
                def f(p):
                    pool.wait_ge(s["rs2"], 4 * p + k + 1)
                    v = pr[:, 4 * k:4 * k + 4, :]
                    pool.tensor_tensor(v, v, rs2[:, 4 * k:4 * k + 4].unsqueeze(2).to_broadcast([N, 4, N]),
                                       ALU.mult).then_inc(s["pn"], 1)
                return f

            def keep_h(p):
                gate(pool, s["hT"], p + 1)
                pool.tensor_copy(hall[:, bass.ds(p, 1), :], hT[:, :]).then_inc(s["hcopy"], 1)

            def scatter_ids(p):
                if isinstance(p, int) and p == 0:
                    pool.wait_ge(s["tab_init"], 16)
                gate(pool, s["slot"], p + 1)
                if not (isinstance(p, int) and p == 0):
                    gate(pool, s["scat"], p * 16 * G * TOPK)
                pool.tensor_copy(tid_now[:, :], choice[:, bass.ds(p * G * TOPK, G * TOPK)]).then_inc(s["tid"], 1)
                gate(pool, s["tid"], p + 1)
                scatter_batch(p, 0)

            def scatter_batch(p, g):
                for k in range(TOPK):
                    j = g * TOPK + k
                    pool.indirect_dma_start(
                        tab_dram, bass.IndirectOffsetOnAxis(ap=slot_now[:, j:j + 1].bitcast(U32), axis=0),
                        tid_now[:, j:j + 1], None, bounds_check=TABN - 1,
                        oob_is_err=False).then_inc(s["scat"], 16)

            def scatter_rest(p):
                scatter_batch(p, 1)

            pipeline(pool, begin, chunk,
                     {3: [rstd_of(0)], 4: [x1_bias], 7: [rstd_of(1)], 8: [rstd_of(2)],
                      17: [normalise(0)], 18: [normalise(1)], 19: [normalise(2)], 20: [normalise(3)],
                      24: [rstd2_of(0)], 25: [rstd2_of(1)], 28: [keep_h], 37: [scatter_ids],
                      44: [scatter_rest]},
                     {6: [gather_emb]}, 3)

            pool.wait_ge(s["scat"], 16 * TOPK * B)
            pool.wait_ge(s["tinfo"], 1)
            pool.indirect_dma_start(
                idrows[:, :], None, tab_dram.rearrange("(a b) n -> a (b n)", b=TILE),
                bass.IndirectOffsetOnAxis(ap=trow[:, :].bitcast(U32), axis=0),
                bounds_check=TABN // TILE - 1, oob_is_err=False).then_inc(s["idrows"], 16)

            pool.wait_ge(s["ttab"], 1)
            turns = turns_less(pool, 0)
            pool.wait_ge(s["tn_st"], 16 * TOPK * PAIRS)

            def gather_tile(u, r, again=True):
                t = u * RING + r
                gate(pool, s["cg"], t + 1)
                if again:
                    gate(pool, s["tr"], t - RING + 1)
                pool.indirect_dma_start(
                    hrow[r][:, :], None, tok_dram,
                    bass.IndirectOffsetOnAxis(ap=igather[:, r:r + 1].bitcast(U32), axis=0),
                    bounds_check=TOPK * T - 1, oob_is_err=False).then_inc(s_h[r], 16)

            def scatter_tile(u, r):
                t = u * RING + r
                gate(pool, s["cs"], t + 1)
                gate(pool, s["eo"], t + 1)
                pool.indirect_dma_start(
                    eo_dram, bass.IndirectOffsetOnAxis(ap=iscatter[:, r:r + 1].bitcast(U32), axis=0),
                    eo[r][:, :], None, bounds_check=TOPK * T - 1, oob_is_err=False).then_inc(s_st[r], 16)

            for r in range(RING):
                gather_tile(0, r, again=False)
            gather_tile(1, 0)
            gather_tile(1, 1)
            gather_tile(1, 2)
            scatter_tile(0, 0)
            gather_tile(1, 3)
            scatter_tile(0, 1)
            with pool.Fori(2, turns) as u:
                gather_tile(u, 0)
                scatter_tile(u - 2, 2)
                gather_tile(u, 1)
                scatter_tile(u - 2, 3)
                gather_tile(u, 2)
                scatter_tile(u - 1, 0)
                gather_tile(u, 3)
                scatter_tile(u - 1, 1)
            before, last = turns_less(pool, 2), turns_less(pool, 1)
            scatter_tile(before, 2)
            scatter_tile(before, 3)
            for r in range(RING):
                if r == 1:
                    gate(pool, s_st[2], 16 * last)
                    gate(pool, s_st[3], 16 * last)
                if r:
                    gate(pool, s_st[r - 1], 16 * (last + 1))
                scatter_tile(last, r)

            def rstd_last(p):
                pool.wait_ge(s["fve"], p + 1)
                pool.tensor_tensor(rstd[:, :], ve[:, :], neghalf[:, :], ALU.pow).then_inc(s["frstd"], 1)

            rstd_last(0)
            with pool.Fori(1, PAIRS) as p:
                rstd_last(p)

        @block.scalar
        def _(act):
            act.preload_act_table(ACT.Exp)
            act.wait_ge(s["early"], 16 * (6 + len(ROWS)))

            def begin(p):
                pass

            def chunk(p, c):
                if c in POOL_CHUNKS:
                    act.wait_ge(s["add_p"], p * len(POOL_CHUNKS) + POOL_CHUNKS.index(c) + 1)
                else:
                    mine = [x for x in range(CH) if x not in POOL_CHUNKS]
                    act.wait_ge(s["add_v"], p * len(mine) + mine.index(c) + 1)
                v = tbuf[:, c % TRING, :]
                act.activation(v, v, ACT.Tanh).then_inc(s["tanh"], 1)

            def xT_copy(p):
                act.wait_ge(s["xs_t"], p + 1)
                act.activation(xT[:, :], p_xT, ACT.Identity).then_inc(s["xT"], 1)

            def exp1(p):
                act.wait_ge(s["nmax"], p + 1)
                for g in range(G):
                    last = act.activation(p1[:, g, :], p_score[:, g, :], ACT.Exp, bias=nmax[:, g:g + 1],
                                          accum_out=esum[:, g:g + 1])
                last.then_inc(s["exp1"], 1)

            def aT_copy(p):
                act.wait_ge(s["aT_ps"], p + 1)
                act.activation(aT[:, :], b_t[:, 0:TN], ACT.Identity).then_inc(s["aT"], 1)

            def x1T_copy(p):
                act.wait_ge(s["x1T_ps"], p + 1)
                act.activation(x1T[:, :], b_t[:, 0:TN], ACT.Identity).then_inc(s["x1T"], 1)

            def relu(p):
                filled(act, p, 0)
                for c in range(2):
                    last = act.activation(hid[:, c, :], big[0][:, c * TN:(c + 1) * TN], ACT.Relu,
                                          bias=bf1[:, c:c + 1])
                last.then_inc(s["big_a"], 1)

            def xaT_copy(p):
                act.wait_ge(s["xaT_ps"], p + 1)
                act.activation(xaT[:, :], b_t[:, 0:TN], ACT.Identity).then_inc(s["xaT"], 1)

            def g_copy(k):
                def f(p):
                    filled(act, p, 2 + k)
                    act.activation(gT[:, 2 * k:2 * k + 2, :].rearrange("p a n -> p (a n)"),
                                   big[(2 + k) % 3][:, 0:2 * TN], ACT.Identity).then_inc(s["big_a"], 1)
                return f

            def vv_copy(k):
                def f(p):
                    filled(act, p, 6 + k)
                    act.activation(vv[:, k // 2, (k % 2) * 512:(k % 2 + 1) * 512],
                                   big[(6 + k) % 3][0:N, :], ACT.Identity).then_inc(s["big_a"], 1)
                return f

            def exp2(k):
                def f(p):
                    act.wait_ge(s["nb2"], 4 * p + k + 1)
                    for j in range(4 * k, 4 * k + 4):
                        last = act.activation(pr[:, j, :], pr[:, j, :], ACT.Exp, bias=nb2[:, j:j + 1],
                                              scale=SCALE, accum_out=es2[:, j:j + 1])
                    last.then_inc(s["exp2"], 1)
                return f

            def prT_copy(k):
                def f(p):
                    filled(act, p, 14 + k)
                    act.activation(prT[:, 4 * k:4 * k + 4, :].rearrange("p a n -> p (a n)"),
                                   big[(14 + k) % 3][0:N, 0:4 * N], ACT.Identity).then_inc(s["big_a"], 1)
                return f

            def hT_affine(p):
                act.wait_ge(s["hT_ps"], p + 1)
                if not (isinstance(p, int) and p == 0):
                    act.wait_ge(s["hcopy"], p)
                act.activation(hT[:, :], b_t[:, 0:TN], ACT.Identity, bias=ln1_b, scale=ln1_g).then_inc(s["hT"], 1)

            def rT_copy(p):
                act.wait_ge(s["rT_ps"], p + 1)
                act.activation(rT[:, :], b_t[0:DR, 0:TN], ACT.Identity).then_inc(s["rT"], 1)

            def gate_exp(p):
                act.wait_ge(s["gap"], p + 1)
                act.activation(egap[:, :], gap[:, :], ACT.Exp, scale=1.0 / TEMP).then_inc(s["egap"], 1)

            pipeline(act, begin, chunk,
                     {0: [exp1], 2: [aT_copy], 5: [x1T_copy], 6: [relu], 10: [xaT_copy],
                      11: [g_copy(0)], 12: [g_copy(2)], 13: [vv_copy(0)], 14: [vv_copy(2)],
                      16: [exp2(0)], 17: [exp2(1)], 18: [prT_copy(0), exp2(2)], 19: [exp2(3)],
                      20: [prT_copy(2)], 27: [hT_affine], 28: [rT_copy], 30: [gate_exp]},
                     {10: [xT_copy]}, 1)

            act.preload_act_table(ACT.Silu)
            act.wait_ge(s["ttab"], 1)
            turns = turns_less(act, 0)

            def silu(u, r, after=True):
                t = u * RING + r
                act.wait_ge(s["g1"], t + 1)
                for c in range(FC):
                    last = act.activation(act_h[:, r % 2, c * TILE:(c + 1) * TILE],
                                          big[r % 2][:, c * TILE:(c + 1) * TILE], ACT.Silu,
                                          bias=wbuf[:, r, 2 * DFF + c:2 * DFF + c + 1])
                last.then_inc(s["silu"], 1)

            def gather_index(u, r):
                if not isinstance(u, int):
                    gate(act, s_h[r], 16 * u)
                elif u > 0:
                    act.wait_ge(s_h[r], 16 * u)
                act.activation(igather[:, r:r + 1], iall[:, bass.ds(u * RING + r, 1)], ACT.Identity)\
                    .then_inc(s["cg"], 1)

            def scatter_index(u, r):
                if not isinstance(u, int):
                    gate(act, s_st[r], 16 * u)
                elif u > 0:
                    act.wait_ge(s_st[r], 16 * u)
                act.activation(iscatter[:, r:r + 1], iall[:, bass.ds(u * RING + r, 1)], ACT.Identity)\
                    .then_inc(s["cs"], 1)

            act.wait_ge(s["iall"], 1)
            for r in range(RING):
                gather_index(0, r)
            for r in range(RING):
                gather_index(1, r)
                scatter_index(0, r)
                silu(0, r)
            with act.Fori(1, turns - 1) as u:
                for r in range(RING):
                    gather_index(u + 1, r)
                    scatter_index(u, r)
                    silu(u, r)
            last = turns_less(act, 1)
            for r in range(RING):
                scatter_index(last, r)
                silu(last, r)

            def silu_shared(p):
                act.wait_ge(s["sh_ps"], p + 1)
                for c in range(SC2):
                    last = act.activation(sh[:, c, :], b_t[:, c * TN:(c + 1) * TN], ACT.Silu,
                                          bias=bs1[:, c:c + 1])
                last.then_inc(s["sh"], 1)

            def silu_last(p):
                for c in range(FC):
                    if c % 2 == 0:
                        act.wait_ge(s["f1"], 2 * p + c // 2 + 1)
                    last = act.activation(fh[:, c, :], big[c // 2][:, (c % 2) * TN:(c % 2 + 1) * TN],
                                          ACT.Silu, bias=fbf1[:, c:c + 1])
                last.then_inc(s["fa"], 1)

            silu_shared(0)
            silu_shared(1)
            silu_last(0)
            with act.Fori(2, PAIRS) as p:
                silu_shared(p)
                silu_last(p - 1)
            silu_last(PAIRS - 1)

        @block.vector
        def _(dve):
            class Chain:
                count, base, first = 0, None, 0

                def link(self, ins):
                    self.count += 1
                    ins.then_inc(s["chain"], 1)

                def now(self):
                    return self.count if self.base is None else self.base + self.count

                def wait(self):
                    dve.wait_ge(s["chain"], self.now())

                def gate(self):
                    gate(dve, s["chain"], self.now())

                def enter(self, p):
                    self.start, self.first = self.count, p

                def at(self, p):
                    self.base = p * DVE_LINKS + (self.start - self.first * DVE_LINKS)
                    self.count = 0

                def leave(self, p):
                    assert self.count == DVE_LINKS, self.count
                    self.base, self.count = None, self.start + (p - self.first) * DVE_LINKS

            ch = Chain()

            dve.wait_ge(s["ids"], 16)
            ch.link(dve.tensor_copy(tok_f[:, :], tok_i[:, :]))
            ch.wait()
            ch.link(dve.tensor_scalar(neg_f[:, :], tok_f[:, :], 0.0, float(VOCAB), ALU.is_lt, ALU.mult))
            ch.wait()
            ch.link(dve.tensor_tensor(tok_f[:, :], tok_f[:, :], neg_f[:, :], ALU.add))
            ch.wait()
            dve.tensor_scalar(eidx[:, :], tok_f[:, :], 0.0, float(VOCAB - 1), ALU.max, ALU.min).then_inc(s["ids"], 1)
            dve.wait_ge(s["early"], 16 * (6 + len(ROWS)))
            dve.wait_ge(s["pool_c"], 8 + RING)
            dve.tensor_scalar(bs2q[:, :], row["bs2"][:, :], SHARED, None, ALU.mult)
            dve.tensor_copy(apad[:, 31:32], ascale).then_inc(s["consts"], 1)

            def begin(p):
                dve.wait_ge(s["qkv"], p + 1)
                if not (isinstance(p, int) and p == 0):
                    dve.wait_ge(s["add_p"], p * len(POOL_CHUNKS))
                    dve.wait_ge(s["add_v"], p * (CH - len(POOL_CHUNKS)))
                dve.tensor_scalar(qT[:, :], b_qk[:, 0:TN], bq, None, ALU.add)
                dve.tensor_scalar(kT[:, :], b_qk[:, TN:2 * TN], bk, None, ALU.add).then_inc(s["qk_ev"], 1)
                dve.wait_ge(s["qk_ev"], p + 1)
                if isinstance(p, int) and p == 0:
                    v_copy(0)

            def chunk(p, c):
                if c in POOL_CHUNKS:
                    return
                if not (isinstance(p, int) and p == 0 and c < TRING):
                    dve.wait_ge(s["score"], p * CH + c - TRING + 1)
                g, cc = c // CPB, c % CPB
                qv = qT[:, g * N:(g + 1) * N].rearrange("p (a m) -> p a m", a=QG)[:, :, 4 * cc:4 * cc + 4]
                kv = kT[:, g * N:(g + 1) * N]
                dve.tensor_tensor(
                    tbuf[:, c % TRING, :].rearrange("p (a m n) -> p a m n", a=QG, m=4),
                    qv.unsqueeze(3).to_broadcast([D, QG, 4, N]),
                    kv.unsqueeze(1).unsqueeze(1).to_broadcast([D, QG, 4, N]), ALU.add).then_inc(s["add_v"], 1)

            def v_copy(p):
                dve.wait_ge(s["qkv"], p + 1)
                dve.tensor_tensor(vrow[:, :, :], p_v, row["bv"][:, :].unsqueeze(1).to_broadcast([N, G, D]),
                                  ALU.add).then_inc(s["v_ev"], 1)

            def next_v(p):
                if not (isinstance(p, int) and p == PAIRS - 1):
                    dve.wait_ge(s["aT_ps"], p + 1)
                    v_copy(p + 1)

            def x_rows(p):
                dve.wait_ge(s["emb"], 16 * G * (p + 1))
                dve.scalar_tensor_tensor(xs[:, :, :], emb_rows[:, :, :], float(np.float32(D) ** np.float32(0.5)),
                                         pe_rows[:, :].unsqueeze(1).to_broadcast([N, G, D]),
                                         ALU.mult, ALU.add).then_inc(s["xs"], 1)
                dve.wait_ge(s["xs"], p + 1)
                dve.tensor_tensor(res[:, bass.ds(p, 1), :, :].rearrange("p a g d -> p (a g) d"), xs[:, :, :],
                                  row["bo"][:, :].unsqueeze(1).to_broadcast([N, G, D]), ALU.add).then_inc(s["res"], 1)

            def softmax1_max(p):
                dve.wait_ge(s["score"], CH * (p + 1))
                dve.tensor_reduce(nmax[:, :], p_score, AX.X, ALU.max, negate=True).then_inc(s["nmax"], 1)

            def p1T_copy(p):
                dve.wait_ge(s["exp1"], p + 1)
                ch.link(dve.reciprocal(rsum[:, :], esum[:, :]))
                dve.wait_ge(s["p1t_ps"], p + 1)
                dve.tensor_copy(p1T[:, :, :].rearrange("p g n -> p (g n)"), b_t[0:N, 0:TN]).then_inc(s["p1T"], 1)

            def ln_stats(x, eps, mv=mv, ve=ve, done="ve"):
                for g in range(G):
                    last = dve.bn_stats(stat[:, g, :], x[:, g, :])
                ch.link(last)
                ch.gate()
                for g in range(G):
                    last = dve.bn_aggr(mv[:, g, :], stat[:, g, :])
                ch.link(last)
                ch.wait()
                dve.tensor_scalar(ve[:, :], mv[:, :, 1], eps, None, ALU.add).then_inc(s[done], 1)

            def ln_apply(p, k, x, y):
                dve.wait_ge(s["rstd"], 3 * p + k + 1)
                for g in range(G):
                    last = dve.tensor_scalar(y[:, g, :], x[:, g, :], mv[:, g, 0:1], rstd[:, g:g + 1],
                                             ALU.subtract, ALU.mult)
                return last

            def gamma_beta(gamma, beta, y):
                ch.wait()
                ch.link(dve.tensor_tensor(xg[:, :, :], xn[:, :, :],
                                          row[gamma][:, :].unsqueeze(1).to_broadcast([N, G, D]), ALU.mult))
                ch.wait()
                return dve.tensor_tensor(y[:, :, :], xg[:, :, :],
                                         row[beta][:, :].unsqueeze(1).to_broadcast([N, G, D]), ALU.add)

            def x1_rows(p):
                dve.wait_ge(s["y"], p + 1)
                ch.wait()
                for g in range(G):
                    last = dve.scalar_tensor_tensor(
                        x1[:, g, :], p_y[:, g, :], rsum[:, g:g + 1],
                        res[:, bass.ds(p, 1), g, :].rearrange("p a d -> p (a d)"), ALU.mult, ALU.add)
                ch.link(last)
                ch.wait()
                ln_stats(x1, EPS_TOK)

            def x1_norm(p):
                ch.link(ln_apply(p, 0, x1, xn))
                gamma_beta("g1", "beta1", x1n).then_inc(s["x1n"], 1)

            def relu(p):
                filled(dve, p, 1)
                for c in range(2, 4):
                    last = dve.tensor_scalar(hid[:, c, :], big[1][:, (c - 2) * TN:(c - 1) * TN], bf1[:, c:c + 1],
                                             0.0, ALU.add, ALU.max)
                last.then_inc(s["big_v"], 1)

            def x2_rows(p):
                dve.wait_ge(s["y2"], p + 1)
                dve.wait_ge(s["x1b"], p + 1)
                ch.link(dve.tensor_tensor(x2[:, :, :], p_y, x1b[:, :, :], ALU.add))
                ch.wait()
                ln_stats(x2, EPS_TOK)

            def x2_norm(p):
                ch.link(ln_apply(p, 1, x2, xn))
                ch.link(gamma_beta("g2", "beta2", h0))
                ch.wait()
                ln_stats(h0, EPS)

            def xa_norm(p):
                ln_apply(p, 2, h0, xa).then_inc(s["xa"], 1)

            def g_copy(k):
                def f(p):
                    filled(dve, p, 2 + k)
                    dve.tensor_copy(gT[:, 2 * k:2 * k + 2, :].rearrange("p a n -> p (a n)"),
                                    big[(2 + k) % 3][:, 0:2 * TN]).then_inc(s["big_v"], 1)
                return f

            def vv_copy(k):
                def f(p):
                    filled(dve, p, 6 + k)
                    dve.tensor_copy(vv[:, k // 2, (k % 2) * 512:(k % 2 + 1) * 512],
                                    big[(6 + k) % 3][0:N, :]).then_inc(s["big_v"], 1)
                return f

            def mask_max(k):
                def f(p):
                    filled(dve, p, 10 + k, alone=True)
                    for j in range(4):
                        h = 4 * k + j
                        last = dve.tensor_tensor_reduce(
                            pr[:, h, :], big[(10 + k) % 3][0:N, j * N:(j + 1) * N], mask[:, :],
                            1.0, -3.0e38, ALU.add, ALU.max, mx2[:, h:h + 1])
                    last.then_inc(s["big_v"], 1)
                    rest = [x for x in range(BIGS) if x not in ACT_BIG]
                    dve.wait_ge(s["big_v"], p * len(rest) + rest.index(10 + k) + 1)
                    dve.tensor_scalar(nb2[:, 4 * k:4 * k + 4], mx2[:, 4 * k:4 * k + 4], -SCALE, None,
                                      ALU.mult).then_inc(s["nb2"], 1)
                return f

            def inv_sums(k):
                def f(p):
                    dve.wait_ge(s["exp2"], 4 * p + k + 1)
                    dve.reciprocal(rs2[:, 4 * k:4 * k + 4], es2[:, 4 * k:4 * k + 4]).then_inc(s["rs2"], 1)
                return f

            def prT_copy(k):
                def f(p):
                    filled(dve, p, 14 + k)
                    dve.tensor_copy(prT[:, 4 * k:4 * k + 4, :].rearrange("p a n -> p (a n)"),
                                    big[(14 + k) % 3][0:N, 0:4 * N]).then_inc(s["big_v"], 1)
                return f

            def h1_rows(p):
                dve.wait_ge(s["o"], p + 1)
                ch.link(dve.tensor_tensor(h1[:, :, :], p_o, h0[:, :, :], ALU.add))
                ch.wait()
                ln_stats(h1, EPS, mv2, ve2, "ve2")

            def h1_norm(p):
                dve.wait_ge(s["rstd2"], 2 * p + 1)
                for g in range(G):
                    last = dve.tensor_scalar(h1n[:, g, :], h1[:, g, :], mv2[:, g, 0:1], rstd2[:, g:g + 1],
                                             ALU.subtract, ALU.mult)
                ch.link(last)
                ch.link(dve.tensor_tensor(vr[:, :], mv2[:, :, 1], rstd2[:, :], ALU.mult))
                ch.wait()
                ch.link(dve.tensor_tensor(vr[:, :], vr[:, :], rstd2[:, :], ALU.mult))
                ch.wait()
                dve.tensor_scalar(ve2[:, :], vr[:, :], EPS, None, ALU.add).then_inc(s["ve2"], 1)
                dve.tensor_tensor(res[:, bass.ds(p, 1), :, :].rearrange("p a g d -> p (a g) d"),
                                  h1[:, :, :], h1n[:, :, :], ALU.add).then_inc(s["res"], 1)

            def tn_rows(p):
                dve.wait_ge(s["rstd2"], 2 * p + 2)
                if not (isinstance(p, int) and p == 0):
                    dve.wait_ge(s["tn_st"], 16 * TOPK * p)
                for g in range(G):
                    last = dve.tensor_scalar(tn[:, g, :], h1n[:, g, :], rstd3[:, g:g + 1], None, ALU.mult)
                last.then_inc(s["tn"], 1)

            def route(p):
                dve.wait_ge(s["lg"], p + 1)
                ch.link(dve.tensor_copy(lg[:, :, :].rearrange("p g e -> p (g e)"), p_lg))
                ch.gate()
                for g in range(G):
                    last = dve.max(top[:, g, :], lg[:, g, :])
                ch.link(last)
                ch.gate()
                for g in range(G):
                    last = dve.max_index(topi[:, g, :], top[:, g, :], lg[:, g, :])
                ch.link(last)
                dve.tensor_tensor(gap[:, :], top[:, :, 1], top[:, :, 0], ALU.subtract).then_inc(s["gap"], 1)

            def one_hot(p):
                ch.wait()
                ch.link(dve.tensor_copy(topf[:, :].rearrange("p (g k) -> p g k", g=G), topi[:, :, 0:TOPK]))
                ch.wait()
                for g in range(G):
                    for k in range(TOPK):
                        j = g * TOPK + k
                        last = dve.tensor_scalar(oh[:, g, k, :], iota_e[0:N, :], topf[:, j:j + 1], None,
                                                 ALU.is_equal)
                ch.link(last)
                ch.wait()
                dve.tensor_tensor(ohs[:, :, :], oh[:, :, 0, :], oh[:, :, 1, :], ALU.add).then_inc(s["oh"], 1)

            def gate_weights(p):
                dve.wait_ge(s["egap"], p + 1)
                ch.link(dve.tensor_scalar(egap1[:, :], egap[:, :], 1.0, None, ALU.add))
                ch.wait()
                ch.link(dve.reciprocal(wnow[:, :, 0], egap1[:, :]))
                ch.wait()
                ch.link(dve.tensor_tensor(wnow[:, :, 1], egap[:, :], wnow[:, :, 0], ALU.mult))
                ch.wait()
                dve.tensor_scalar(wts[:, bass.ds(p, 1), :].rearrange("p a j -> p (a j)"),
                                  wnow[:, :, :].rearrange("p g k -> p (g k)"), 1.0, None,
                                  ALU.mult).then_inc(s["res"], 1)

            def ranks(p):
                dve.wait_ge(s["rank_ps"], p + 1)
                for g in range(G):
                    for k in range(TOPK):
                        j = g * TOPK + k
                        last = dve.tensor_tensor_reduce(rjunk[:, j, :], p_rank[:, g, :], oh[:, g, k, :], 1.0, 0.0,
                                                        ALU.mult, ALU.add, rank[:, j:j + 1])
                last.then_inc(s["rank"], 1)
                ch.link(dve.tensor_tensor(cum[:, :], cum[:, :], ohs[:, 0, :], ALU.add))
                ch.wait()
                ch.link(dve.tensor_tensor(cum[:, :], cum[:, :], ohs[:, 1, :], ALU.add))
                ch.wait()
                ch.link(dve.scalar_tensor_tensor(slotf[:, :], topf[:, :], float(T), rank[:, :], ALU.mult, ALU.add))
                ch.wait()
                if not (isinstance(p, int) and p == 0):
                    dve.wait_ge(s["scat"], p * 16 * G * TOPK)
                dve.tensor_scalar(slot_now[:, :], slotf[:, :], 1.0, None, ALU.mult).then_inc(s["slot"], 1)

            def products():
                for i in range(4):
                    dve.wait_ge(s["raw_mm"], i + 1)
                    bank = [big[0], big[1], big[2], b_t][i]
                    dst = (mh if i < 2 else vo)[:, (i % 2) * 512:(i % 2 + 1) * 512]
                    dve.tensor_copy(dst, bank[:, :]).then_inc(s["raw_ev"], 1)

            def pre_or_products(p):
                x_rows(p)
                if isinstance(p, int) and p == 1:
                    products()

            pipeline(dve, begin, chunk,
                     {0: [softmax1_max], 1: [p1T_copy], 2: [next_v], 3: [x1_rows], 4: [x1_norm], 6: [relu],
                      7: [x2_rows], 8: [x2_norm], 9: [xa_norm], 11: [g_copy(1)], 12: [g_copy(3)],
                      13: [vv_copy(1)], 14: [vv_copy(3)], 15: [mask_max(0)], 16: [mask_max(1)],
                      17: [inv_sums(0), mask_max(2)], 18: [inv_sums(1), mask_max(3)],
                      19: [inv_sums(2), prT_copy(1)], 20: [inv_sums(3)], 21: [prT_copy(3)],
                      24: [h1_rows], 25: [h1_norm], 26: [tn_rows], 29: [route], 30: [one_hot],
                      31: [gate_weights, ranks]},
                     {9: [pre_or_products]}, 2, ch)

            dve.wait_ge(s["cnt"], 1)
            ch.link(dve.tensor_scalar(cnti[:, :], b_t[0:MAXT, 0:E], float(TILE - 1), None, ALU.add))
            ch.wait()
            ch.link(dve.tensor_scalar(cnti[:, :], cnti[:, :], TILE.bit_length() - 1, None, ALU.logical_shift_right))
            ch.wait()
            ch.link(dve.tensor_copy(ntf[:, :], cnti[:, :]))
            ch.link(dve.memset(cntf[:, :], 1.0))
            ch.wait()
            ch.link(dve.tensor_tensor_scan(tend[:, :], cntf[:, :], ntf[:, :], 0.0, ALU.mult, ALU.add))
            ch.wait()
            ch.link(dve.tensor_scalar(le[:, :], tend[:, :], iota_t[0:MAXT, 0:1], None, ALU.is_le))
            ch.wait()
            ch.link(dve.tensor_reduce(tcol[:, 0:1], le[:, :], AX.X, ALU.add))
            ch.link(dve.tensor_tensor_reduce(lejunk[:, :], le[:, :], ntf[:, :], 1.0, 0.0, ALU.mult, ALU.add,
                                             tcol[:, 1:2]))
            ch.wait()
            ch.link(dve.tensor_scalar(tinfo[:, 0:1], tcol[:, 0:1], float(E - 1), None, ALU.min))
            ch.link(dve.tensor_tensor(tcol[:, 2:3], iota_t[0:MAXT, 0:1], tcol[:, 1:2], ALU.subtract))
            ch.link(dve.tensor_scalar(ui[:, :], tend[:, E - 1:E], float(RING - 1), 1.0 / RING, ALU.add, ALU.mult))
            ch.wait()
            ch.link(dve.scalar_tensor_tensor(tcol[:, 3:4], tinfo[:, 0:1], float(T // TILE), tcol[:, 2:3],
                                             ALU.mult, ALU.add))
            ch.wait()
            dve.tensor_scalar(trow[:, :], tcol[:, 3:4], float(TABN // TILE - 1), None, ALU.min)
            ch.link(dve.tensor_copy(tcol[:, 5:6], ui[:, :]))
            ch.wait()
            ch.link(dve.scalar_tensor_tensor(tcol[:, 6:7], tcol[:, 5:6], float(-RING), tend[:, E - 1:E],
                                             ALU.mult, ALU.add))
            ch.wait()
            ch.link(dve.tensor_scalar(tcol[:, 7:8], tcol[:, 6:7], float(-RING), None, ALU.is_le))
            ch.wait()
            for n in range(3):
                last = dve.tensor_scalar(tinfo[:, 1 + n:2 + n], tcol[:, 5:6], tcol[:, 7:8], float(n),
                                         ALU.subtract, ALU.subtract)
            last.then_inc(s["tinfo"], 1)
            dve.wait_ge(s["trow"], 1)
            dve.tensor_copy(ttab[0:1, :], b_y[0:1, 0:MAXT + 3]).then_inc(s["ttab"], 1)
            dve.wait_ge(s["ttab"], 1)
            turns = turns_less(dve, 0)
            dve.wait_ge(s["idrows"], 16)
            dve.tensor_copy(idf[:, :], idrows[:, :]).then_inc(s["idf"], 1)
            dve.wait_ge(s["ids_t"], 1)
            dve.tensor_copy(iall[:, :], b_v[:, 0:MAXT]).then_inc(s["iall"], 1)

            def hb_affine(u, r):
                t = u * RING + r
                dve.wait_ge(s["tr"], t + 1)
                dve.tensor_scalar(hbT[:, r % 2, :], b_t[:, 0:TILE], ln1_g, ln1_b, ALU.mult, ALU.add)\
                    .then_inc(s["hbT"], 1)

            def eo_copy(u, r):
                t = u * RING + r
                dve.wait_ge(s["g2"], t + 1)
                if not (isinstance(u, int) and u == 0):
                    dve.wait_ge(s_st[r], 16 * u)
                dve.tensor_copy(eo[r][:, :], [b_s, b_qk][r % 2][:, 0:D]).then_inc(s["eo"], 1)

            def turn(u, before):
                for r in range(RING):
                    hb_affine(u, r)
                    if r >= 2:
                        eo_copy(u, r - 2)
                    elif before is not None:
                        eo_copy(before, r + 2)

            turn(0, None)
            turn(1, 0)
            with dve.Fori(2, turns) as u:
                turn(u, u - 1)
            for r in (2, 3):
                eo_copy(turns_less(dve, 1), r)

            def mixture(p):
                ch2.link(dve.tensor_scalar(wl[:, :], wts[:, bass.ds(p, 1), :].rearrange("p a j -> p (a j)"), 1.0,
                                           None, ALU.mult))
                dve.wait_ge(s["er"], 16 * (p + 1))
                ch2.wait()
                for g in range(G):
                    last = dve.scalar_tensor_tensor(hm1[:, g, :], er[:, bass.ds(p, 1), g, 0, :].rearrange("p a d -> p (a d)"), wl[:, 2 * g:2 * g + 1],
                                                    bs2q[:, :], ALU.mult, ALU.add)
                ch2.link(last)
                ch2.wait()
                for g in range(G):
                    last = dve.scalar_tensor_tensor(hm2[:, g, :], er[:, bass.ds(p, 1), g, 1, :].rearrange("p a d -> p (a d)"), wl[:, 2 * g + 1:2 * g + 2],
                                                    hm1[:, g, :], ALU.mult, ALU.add)
                ch2.link(last)
                ch2.wait()
                dve.wait_ge(s["ys"], p + 1)
                ch2.link(dve.scalar_tensor_tensor(hm[:, :, :], p_y, SHARED, hm2[:, :, :], ALU.mult, ALU.add))
                ch2.wait()
                for g in range(G):
                    last = dve.bn_stats(stat[:, g, :], hm[:, g, :])
                ch2.link(last)
                ch2.gate()
                for g in range(G):
                    last = dve.bn_aggr(mv[:, g, :], stat[:, g, :])
                ch2.link(last)
                ch2.wait()
                dve.tensor_scalar(ve[:, :], mv[:, :, 1], EPS, None, ALU.add).then_inc(s["fve"], 1)
                ch2.link(dve.tensor_tensor(rh2[:, :, :], hm[:, :, :],
                                           res[:, bass.ds(p, 1), :, :].rearrange("p a g d -> p (a g) d"), ALU.add))
                dve.wait_ge(s["frstd"], p + 1)
                for g in range(G):
                    last = dve.tensor_scalar(fn[:, g, :], hm[:, g, :], mv[:, g, 0:1], rstd[:, g:g + 1],
                                             ALU.subtract, ALU.mult)
                last.then_inc(s["fn"], 1)

            def f_affine(p):
                dve.wait_ge(s["fT_ps"], p + 1)
                dve.tensor_scalar(fT[:, :], b_v[:, 0:TN], ffln_g, ffln_b, ALU.mult, ALU.add).then_inc(s["fT"], 1)

            def keep_rh(p):
                if not (isinstance(p, int) and p == 0):
                    dve.wait_ge(s["of"], p)
                ch2.wait()
                ch2.link(dve.tensor_tensor(rh[:, :, :], rh2[:, :, :],
                                           row["fbf2"][:, :].unsqueeze(1).to_broadcast([N, G, D]), ALU.add))

            def output(p):
                dve.wait_ge(s["f2"], p + 1)
                ch2.wait()
                if not (isinstance(p, int) and p == 0):
                    dve.wait_ge(s["out"], 16 * p)
                dve.tensor_tensor(of[:, :, :], b_s[0:N, 0:G * D].rearrange("p (g n) -> p g n", g=G),
                                  rh[:, :, :], ALU.add).then_inc(s["of"], 1)

            class Chain2(Chain):
                def at(self, p):
                    self.base = p * 8 + (self.start - self.first * 8)
                    self.count = 0

                def leave(self, p):
                    assert self.count == 8, self.count
                    self.base, self.count = None, self.start + (p - self.first) * 8

            ch2 = Chain2()
            ch2.count = ch.count
            mixture(0)
            f_affine(0)
            keep_rh(0)
            mixture(1)
            f_affine(1)
            output(0)
            keep_rh(1)
            ch2.enter(2)
            with dve.Fori(2, PAIRS - 1) as p:
                ch2.at(p)
                mixture(p)
                f_affine(p)
                output(p - 1)
                keep_rh(p)
            ch2.leave(PAIRS - 1)
            mixture(PAIRS - 1)
            f_affine(PAIRS - 1)
            output(PAIRS - 2)
            keep_rh(PAIRS - 1)
            output(PAIRS - 1)

        @block.tensor
        def _(pe):
            pe.wait_ge(s["early"], 16 * (6 + len(ROWS)))

            def begin(p):
                pass

            def chunk(p, c):
                if c == 0:
                    if isinstance(p, int) and p == 0:
                        pe.wait_ge(s["consts"], 1)
                    else:
                        pe.wait_ge(s["exp1"], p)
                pe.wait_ge(s["tanh"], p * CH + c + 1)
                g, cc = c // CPB, c % CPB
                for m in range(4):
                    col = 4 * cc + m
                    for a in range(QG):
                        j = a * 4 + m
                        last = pe.matmul(b_s[32 * a:32 * a + 32, g * N:(g + 1) * N], apad[:, 31 - col:63 - col],
                                         tbuf[:, c % TRING, j * N:(j + 1) * N],
                                         start=(cc == 0 and m == 0), stop=(cc == CPB - 1 and m == 3))
                last.then_inc(s["score"], 1)

            def xs_turn(p):
                pe.wait_ge(s["xs"], p + 1)
                if not (isinstance(p, int) and p == 0):
                    pe.wait_ge(s["v_ev"], p)
                if not (isinstance(p, int) and p < 3):
                    pe.wait_ge(s["ve2"], 2 * p - 5)
                for g in range(G):
                    last = pe.transpose(p_xT[:, g * N:(g + 1) * N], xs[:, g, :], ident[0:N, 0:N])
                last.then_inc(s["xs_t"], 1)

            def qkv(p):
                pe.wait_ge(s["xT"], p + 1)
                if not (isinstance(p, int) and p == 0):
                    pe.wait_ge(s["qk_ev"], p)
                for i in range(2):
                    pe.matmul(b_qk[:, i * TN:(i + 1) * TN], wqkv[:, i, :], xT[:, :], start=True, stop=True)
                for g in range(G):
                    last = pe.matmul(p_v[:, g, :], xT[:, g * N:(g + 1) * N], wqkv[:, 2, :], start=True, stop=True)
                last.then_inc(s["qkv"], 1)

            def products():
                pe.wait_ge(s["late"], 16 * 15)
                for i in range(4):
                    bank = [big[0], big[1], big[2], b_t][i]
                    for j in range(4):
                        h = (i % 2) * 4 + j
                        a, b = (0, 1) if i < 2 else (2, 3)
                        last = pe.matmul(bank[:, j * D:(j + 1) * D], raw[:, a, h * D:(h + 1) * D],
                                         raw[:, b, h * D:(h + 1) * D], start=True, stop=True)
                    last.then_inc(s["raw_mm"], 1)

            def p1_turn(p):
                if isinstance(p, int) and p == 0:
                    pe.wait_ge(s["raw_ev"], 4)
                pe.wait_ge(s["exp1"], p + 1)
                for g in range(G):
                    last = pe.transpose(b_t[0:N, g * N:(g + 1) * N], p1[:, g, :], ident[0:N, 0:N])
                last.then_inc(s["p1t_ps"], 1)

            def attend1(p):
                pe.wait_ge(s["p1T"], p + 1)
                pe.wait_ge(s["v_ev"], p + 1)
                for g in range(G):
                    last = pe.matmul(b_t[:, g * N:(g + 1) * N], vrow[:, g, :], p1T[:, g, :], start=True, stop=True)
                last.then_inc(s["aT_ps"], 1)

            def project1(p):
                pe.wait_ge(s["aT"], p + 1)
                if not (isinstance(p, int) and p < 2):
                    pe.wait_ge(s["rank"], p - 1)
                for g in range(G):
                    last = pe.matmul(p_y[:, g, :], aT[:, g * N:(g + 1) * N], wo[:, :], start=True, stop=True)
                last.then_inc(s["y"], 1)

            def x1_turn(p):
                pe.wait_ge(s["x1n"], p + 1)
                for g in range(G):
                    last = pe.transpose(b_t[:, g * N:(g + 1) * N], x1n[:, g, :], ident[0:N, 0:N])
                last.then_inc(s["x1T_ps"], 1)

            def ffn1(p):
                pe.wait_ge(s["x1T"], p + 1)
                for c in range(FC):
                    if c % 2 == 0:
                        big_freed(pe, p, c // 2)
                    last = pe.matmul(big[c // 2][:, (c % 2) * TN:(c % 2 + 1) * TN], w1[:, c * D:(c + 1) * D],
                                     x1T[:, :], start=True, stop=True)
                    if c % 2:
                        last.then_inc(s["big"], 1)

            def ffn2(p):
                emptied(pe, p, 0)
                emptied(pe, p, 1)
                for g in range(G):
                    for c in range(FC):
                        last = pe.matmul(p_y[:, g, :], hid[:, c, g * N:(g + 1) * N], w2[:, c, :],
                                         start=(c == 0), stop=(c == FC - 1))
                last.then_inc(s["y2"], 1)

            def xa_turn(p):
                pe.wait_ge(s["xa"], p + 1)
                for g in range(G):
                    last = pe.transpose(b_t[:, g * N:(g + 1) * N], xa[:, g, :], ident[0:N, 0:N])
                last.then_inc(s["xaT_ps"], 1)

            def heads_g(k):
                def f(p):
                    pe.wait_ge(s["xaT"], p + 1)
                    big_freed(pe, p, 2 + k)
                    for j in range(2):
                        h = 2 * k + j
                        last = pe.matmul(big[(2 + k) % 3][:, j * TN:(j + 1) * TN], mh[:, h * D:(h + 1) * D],
                                         xaT[:, :], start=True, stop=True)
                    last.then_inc(s["big"], 1)
                return f

            def heads_v(k):
                def f(p):
                    big_freed(pe, p, 6 + k)
                    g = k // 2
                    pe.matmul(big[(6 + k) % 3][0:N, :], xaT[:, g * N:(g + 1) * N],
                              vo[:, (k % 2) * 512:(k % 2 + 1) * 512], start=True, stop=True).then_inc(s["big"], 1)
                return f

            def scores(k):
                def f(p):
                    if k == 0:
                        emptied(pe, p, 4)
                    big_freed(pe, p, 10 + k)
                    g = k // 2
                    for j in range(4):
                        h = (k % 2) * 4 + j
                        last = pe.matmul(big[(10 + k) % 3][0:N, j * N:(j + 1) * N], gT[:, h, g * N:(g + 1) * N],
                                         xaT[:, g * N:(g + 1) * N], start=True, stop=True)
                    last.then_inc(s["big"], 1)
                return f

            def pr_turn(k):
                def f(p):
                    big_freed(pe, p, 14 + k)
                    pe.wait_ge(s["pn"], 4 * p + k + 1)
                    for j in range(4):
                        last = pe.transpose(big[(14 + k) % 3][0:N, j * N:(j + 1) * N], pr[:, 4 * k + j, :],
                                            ident[0:N, 0:N])
                    last.then_inc(s["big"], 1)
                return f

            def attend2(k):
                def f(p):
                    if k == 0:
                        pe.wait_ge(s["v_ev"], min(p + 3, PAIRS) if isinstance(p, int) else p + 3)
                    emptied(pe, p, 14 + k)
                    g = k // 2
                    for h in range((k % 2) * 4, (k % 2) * 4 + 4):
                        last = pe.matmul(p_o[:, g, :], prT[:, g * H + h, :], vv[:, g, h * D:(h + 1) * D],
                                         start=(h == 0), stop=(h == H - 1))
                    if k == 3:
                        last.then_inc(s["o"], 1)
                return f

            def tn_turn(p):
                pe.wait_ge(s["tn"], p + 1)
                pe.wait_ge(s["xaT"], min(p + 2, PAIRS) if isinstance(p, int) else p + 2)
                for g in range(G):
                    last = pe.transpose(b_t[:, g * N:(g + 1) * N], tn[:, g, :], ident[0:N, 0:N])
                last.then_inc(s["hT_ps"], 1)

            def router(p):
                pe.wait_ge(s["hT"], p + 1)
                pe.matmul(b_t[0:DR, 0:TN], wr[:, :], hT[:, :], start=True, stop=True).then_inc(s["rT_ps"], 1)

            def logits(p):
                pe.wait_ge(s["rT"], p + 1)
                pe.wait_ge(s["ve"], 3 * min(p + 1, PAIRS - 1) + 2 if isinstance(p, int) else 3 * p + 5)
                for g in range(G):
                    last = pe.matmul(p_lg[:, g * E:(g + 1) * E], rT[:, g * N:(g + 1) * N], cbT[:, :],
                                     start=True, stop=True)
                last.then_inc(s["lg"], 1)

            def ranks(p):
                pe.wait_ge(s["oh"], p + 1)
                for g in range(G):
                    pe.matmul(p_rank[:, g, :], tri[:, :], ohs[:, g, :], start=True, stop=False)
                    if g == 1:
                        pe.matmul(p_rank[:, g, :], ones[:, 0:N], ohs[:, 0, :], start=False, stop=False)
                    last = pe.matmul(p_rank[:, g, :], ones[:, 0:N], cum[:, :], start=False, stop=True)
                last.then_inc(s["rank_ps"], 1)

            def pre_turn(p):
                xs_turn(p)
                if isinstance(p, int) and p == 1:
                    products()

            pipeline(pe, begin, chunk,
                     {1: [p1_turn], 2: [attend1], 3: [project1], 5: [x1_turn], 6: [ffn1], 7: [ffn2],
                      10: [xa_turn], 11: [heads_g(0), heads_g(1)], 12: [heads_g(2), heads_g(3)],
                      13: [heads_v(0), heads_v(1)], 14: [heads_v(2), heads_v(3)], 15: [scores(0)],
                      16: [scores(1)], 17: [scores(2)], 18: [scores(3), pr_turn(0)],
                      19: [pr_turn(1), attend2(0)], 20: [pr_turn(2), attend2(1)],
                      21: [pr_turn(3), attend2(2)], 22: [attend2(3)], 27: [tn_turn], 28: [router],
                      29: [logits], 31: [ranks]},
                     {10: [pre_turn], 11: [qkv]}, None)

            pe.wait_ge(s["slot"], PAIRS)
            pe.matmul(b_t[0:MAXT, 0:E], ones[:, 0:MAXT], cum[:, :], start=True, stop=True).then_inc(s["cnt"], 1)
            pe.wait_ge(s["tinfo"], 1)
            pe.matmul(b_y[0:1, 0:MAXT], tinfo[:, 0:1], ident[0:MAXT, 0:MAXT], start=True, stop=True)
            for i in range(3):
                last = pe.matmul(b_y[0:1, MAXT + i:MAXT + i + 1], tinfo[:, 1 + i:2 + i],
                                 ident[0:MAXT, 0:1], start=True, stop=True)
            last.then_inc(s["trow"], 1)
            pe.wait_ge(s["idf"], 1)
            pe.transpose(b_v[:, 0:MAXT], idf[:, :], ident[0:MAXT, 0:MAXT]).then_inc(s["ids_t"], 1)
            pe.wait_ge(s["ttab"], 1)
            turns = turns_less(pe, 0)

            def tile_turn(u, r):
                t = u * RING + r
                if not (isinstance(t, int) and t == 0):
                    pe.wait_ge(s["hbT"], t)
                pe.wait_ge(s_h[r], 16 * (u + 1))
                pe.transpose(b_t[:, 0:TILE], hrow[r][:, :], ident[:, :]).then_inc(s["tr"], 1)

            def expert1(u, r):
                t = u * RING + r
                pe.wait_ge(s["hbT"], t + 1)
                pe.wait_ge(s_w[r], 32 * (u + 1))
                for c in range(FC):
                    last = pe.matmul(big[r % 2][:, c * TILE:(c + 1) * TILE], wbuf[:, r, c * D:(c + 1) * D],
                                     hbT[:, r % 2, :], start=True, stop=True)
                last.then_inc(s["g1"], 1)

            def expert2(u, r, before):
                t = u * RING + r
                pe.wait_ge(s["silu"], t + 1)
                if r:
                    if not (isinstance(t, int) and t < 2):
                        pe.wait_ge(s["eo"], t - 1)
                elif before is not None:
                    pe.wait_ge(s["eo"], before * RING + RING - 1)
                o = [b_s, b_qk][r % 2][:, 0:D]
                for c in range(FC):
                    pe.matmul(o, act_h[:, r % 2, c * TILE:(c + 1) * TILE],
                              wbuf[:, r, DFF + c * D:DFF + (c + 1) * D], start=(c == 0), stop=False)
                pe.matmul(o, ones[0:1, 0:TILE], b2buf[0:1, r, :], start=False, stop=True).then_inc(s["g2"], 1)

            def turn(u, before, after):
                for r in range(RING):
                    expert1(u, r)
                    if r < RING - 1:
                        tile_turn(u, r + 1)
                    elif after is not None:
                        tile_turn(after, 0)
                    if r:
                        expert2(u, r - 1, before)
                    elif before is not None:
                        expert2(before, RING - 1, None)

            tile_turn(0, 0)
            turn(0, None, 1)
            with pe.Fori(1, turns - 1) as u:
                turn(u, u - 1, u + 1)
            last, before = turns_less(pe, 1), turns_less(pe, 2)
            turn(last, before, None)
            expert2(last, RING - 1, before)

            def shared1(p):
                if not (isinstance(p, int) and p == 0):
                    pe.wait_ge(s["sh"], p)
                for c in range(SC2):
                    last = pe.matmul(b_t[:, c * TN:(c + 1) * TN], ws1[:, c * D:(c + 1) * D],
                                     hall[:, bass.ds(p, 1), :].rearrange("p a n -> p (a n)"),
                                     start=True, stop=True)
                last.then_inc(s["sh_ps"], 1)

            def shared2(p):
                pe.wait_ge(s["sh"], p + 1)
                if not (isinstance(p, int) and p == 0):
                    pe.wait_ge(s["fve"], p)
                for g in range(G):
                    for c in range(SC2):
                        last = pe.matmul(p_y[:, g, :], sh[:, c, g * N:(g + 1) * N], ws2[:, c, :],
                                         start=(c == 0), stop=(c == SC2 - 1))
                last.then_inc(s["ys"], 1)

            def f_turn(p):
                pe.wait_ge(s["fn"], p + 1)
                for g in range(G):
                    last = pe.transpose(b_v[:, g * N:(g + 1) * N], fn[:, g, :], ident[0:N, 0:N])
                last.then_inc(s["fT_ps"], 1)

            def last1(p):
                pe.wait_ge(s["fT"], p + 1)
                if not (isinstance(p, int) and p == 0):
                    pe.wait_ge(s["fa"], p)
                for c in range(FC):
                    last = pe.matmul(big[c // 2][:, (c % 2) * TN:(c % 2 + 1) * TN], wf1[:, c * D:(c + 1) * D],
                                     fT[:, :], start=True, stop=True)
                    if c % 2:
                        last.then_inc(s["f1"], 1)

            def last2(p):
                pe.wait_ge(s["fa"], p + 1)
                if not (isinstance(p, int) and p == 0):
                    pe.wait_ge(s["of"], p)
                for g in range(G):
                    for c in range(FC):
                        last = pe.matmul(b_s[0:N, g * D:(g + 1) * D], fh[:, c, g * N:(g + 1) * N], wf2[:, c, :],
                                         start=(c == 0), stop=(c == FC - 1))
                last.then_inc(s["f2"], 1)

            pe.wait_ge(s["eo"], turns * RING)
            pe.sem_inc(s["gate"], 1)
            shared1(0)
            shared2(0)
            f_turn(0)

            def step(p):
                shared1(p)
                last1(p - 1)
                shared2(p)
                last2(p - 1)
                f_turn(p)

            step(1)
            with pe.Fori(2, PAIRS) as p:
                step(p)
            last1(PAIRS - 1)
            last2(PAIRS - 1)


def _inputs(inputs):
    f = {k: np.ascontiguousarray(np.asarray(v)) for k, v in inputs.items()}
    a = {}
    a["x"] = np.ascontiguousarray(f["x"].T)
    a["L0_tok_emb"] = f["L0_tok_emb"]
    for n in ["L0_tok_Wq", "L0_tok_Wk", "L0_tok_Wv", "L0_tok_Wo", "L0_tok_W1", "L0_tok_W2", "L0_ffn_Wr",
              "L0_ffn_Ws1", "L0_ffn_Ws2", "L0_ffn_Wf1", "L0_ffn_Wf2", "L0_ffn_b2"]:
        a[n] = f[n]
    a["attn_Wq"], a["attn_Wk"], a["attn_Wv"] = f["L0_attn_Wq"], f["L0_attn_Wk"], f["L0_attn_Wv"]
    a["attn_WoT"] = np.ascontiguousarray(f["L0_attn_Wo"].T)
    a["cbT"] = np.ascontiguousarray(f["L0_ffn_codebook"].T)
    for n, src in zip(ROWS, ["L0_tok_bv", "L0_tok_bo", "L0_tok_g1", "L0_tok_beta1", "L0_tok_bf2", "L0_tok_g2",
                             "L0_tok_beta2", "L0_ffn_bs2", "L0_ffn_bf2"]):
        a["row_" + n] = f[src]
    a["cols"] = np.concatenate(
        [f[n].reshape(-1, D).T for n in ["L0_tok_bq", "L0_tok_bk", "L0_tok_attn_scale", "L0_ffn_ln1_g",
                                         "L0_ffn_ln1_b", "L0_ffn_ffln_g", "L0_ffn_ffln_b", "L0_tok_bf1",
                                         "L0_ffn_bs1", "L0_ffn_bf1"]], axis=1)
    w1 = f["L0_ffn_W1"]
    w2 = f["L0_ffn_W2"].reshape(E, FC, D, D).transpose(0, 2, 1, 3).reshape(E, D, DFF)
    b1 = f["L0_ffn_b1"].reshape(E, FC, D).transpose(0, 2, 1)
    a["wpack"] = np.concatenate([w1, w2, b1], axis=2)
    pos = np.arange(N)[:, None].astype(np.float64)
    i = np.arange(D)[None, :]
    ang = pos / np.power(10000.0, 2 * (i // 2) / np.float32(D))
    ang[:, 0::2] = np.sin(ang[:, 0::2])
    ang[:, 1::2] = np.cos(ang[:, 1::2])
    a["pe"] = ang.astype(np.float32)
    a["ident"] = np.eye(128, dtype=np.float32)
    a["mask"] = np.triu(np.full((N, N), NEG, np.float32), 1)
    a["tri"] = np.triu(np.ones((N, N), np.float32), 1)
    return {k: np.ascontiguousarray(v) for k, v in a.items()}


def kernel(**inputs):
    import concourse.bacc as bacc
    from concourse.bass_utils import run_bass_kernel_spmd

    nc = bacc.Bacc("TRN2", target_bir_lowering=False, num_devices=1)
    arrays = _inputs(inputs)
    io = {n: nc.dram_tensor("in_" + n, a.shape, mybir.dt.from_np(a.dtype), kind="ExternalInput").ap()
          for n, a in arrays.items()}
    out = nc.dram_tensor("out", (B, N, D), F32, kind="ExternalOutput").ap()
    program(nc, io, out)
    r = run_bass_kernel_spmd(nc, [{"in_" + n: a for n, a in arrays.items()}], core_ids=[0])
    return r.results[0]["out"]
```

```python
from contextlib import ExitStack

import concourse.bass as bass
import numpy as np
from concourse import mybir

F32 = mybir.dt.float32
I32 = mybir.dt.int32
U32 = mybir.dt.uint32
ACT = mybir.ActivationFunctionType
ALU = mybir.AluOpType
AX = mybir.AxisListType

B, N, D = 32, 96, 128
G = 2
PAIRS = B // G
TN = G * N
T = B * N
VOCAB, DFF, H = 8000, 512, 8
FC = DFF // D
E, DR, TOPK, DSH = 64, 64, 2, 256
SC2 = DSH // D
TILE = 128
RING = 4
MAXT = -(-((T * TOPK - E) // TILE + E) // RING) * RING
RESULT_LOADS = ((0, 1), (1, 2), (2, PAIRS))
TABN = E * T
QG = 4
QR = N // QG
SR = 32 * QG
CROWS = 12
CQ = CROWS // QG
CPB = N // CROWS
CH = G * CPB
CW = CROWS * N
DEPTH = 3
TRING = 4
POOL_CHUNKS = (1, 2, 3, 4, 5, 9, 14)
BIGS = 18
ACT_BIG = (0, 1, 2, 3, 4, 7, 15, 16)
EPS_TOK, EPS = 1e-6, 1e-5
SCALE = 1.0 / float(D) ** 0.5
TEMP = 0.7
SHARED = 0.25
NEG = -1.0e30
DVE_LINKS = 29
WCOLS = 2 * DFF + FC

ROWS = ["bv", "bo", "g1", "beta1", "bf2", "g2", "beta2", "bs2", "fbf2"]


def program(nc, io, out):
    with ExitStack() as ctx:
        def sb(name, shape, dt=F32):
            return ctx.enter_context(nc.sbuf_tensor(name, shape, dt))

        def ps(name):
            return ctx.enter_context(nc.psum_tensor(name, [128, 512], F32))

        tok_dram = nc.dram_tensor("tok_dram", (TOPK * T, D), F32).ap()
        tab_dram = nc.dram_tensor("tab_dram", (TABN, 1), I32).ap()
        eo_dram = nc.dram_tensor("eo_dram", (TOPK * T, D), F32).ap()

        ident = sb("ident", [128, 128])
        tri = sb("tri", [N, N])
        ones = sb("ones", [N, 128])
        mask = sb("mask", [N, N])
        pe_rows = sb("pe_rows", [N, D])
        iota_e = sb("iota_e", [128, E])
        iota_t = sb("iota_t", [128, 1])
        row = {n: sb("row_" + n, [N, D]) for n in ROWS}
        wqkv = sb("wqkv", [D, 3, D])
        wo = sb("wo", [D, D])
        w1 = sb("w1", [D, DFF])
        w2 = sb("w2", [D, FC, D])
        spread = sb("spread", [128, PAIRS * G * TOPK * D])
        raw = spread[:, 0:4 * H * D].rearrange("p (a n) -> p a n", a=4)
        mh = sb("mh", [D, H * D])
        vo = sb("vo", [D, H * D])
        wr = sb("wr", [D, DR])
        cbT = sb("cbT", [DR, E])
        ws1 = sb("ws1", [D, DSH])
        ws2 = sb("ws2", [D, SC2, D])
        wf1 = sb("wf1", [D, DFF])
        wf2 = sb("wf2", [D, FC, D])
        cols = sb("cols", [D, 7 + FC + SC2 + FC])
        bq, bk, ascale = cols[:, 0:1], cols[:, 1:2], cols[:, 2:3]
        ln1_g, ln1_b, ffln_g, ffln_b = (cols[:, i:i + 1] for i in range(3, 7))
        bf1 = cols[:, 7:7 + FC]
        bs1 = cols[:, 7 + FC:7 + FC + SC2]
        fbf1 = cols[:, 7 + FC + SC2:]
        apad = sb("apad", [D, 64])
        neghalf = sb("neghalf", [N, G])
        bs2q = sb("bs2q", [N, D])
        sentinel = sb("sentinel", [128, TABN // 128], I32)

        tok_i = sb("tok_i", [N, B], I32)
        tok_f = sb("tok_f", [N, B])
        neg_f = sb("neg_f", [N, B])
        eidx = sb("eidx", [N, B], I32)
        choice = sb("choice", [N, B * TOPK], I32)
        res = sb("res", [N, PAIRS, G, D])
        hall = sb("hall", [D, PAIRS, TN])
        wts = sb("wts", [N, PAIRS, G * TOPK])
        ei_now = sb("ei_now", [N, G], I32)
        tid_now = sb("tid_now", [N, G * TOPK], I32)
        slot_now = sb("slot_now", [N, G * TOPK], I32)
        emb_rows = sb("emb_rows", [N, G, D])
        xs = sb("xs", [N, G, D])
        xT = sb("xT", [D, TN])
        qT = sb("qT", [D, TN])
        kT = sb("kT", [D, TN])
        vrow = sb("vrow", [N, G, D])
        tbuf = sb("tbuf", [D, TRING, CW])
        nmax = sb("nmax", [SR, G])
        esum = sb("esum", [SR, G])
        rsum = sb("rsum", [SR, G])
        p1 = sb("p1", [SR, G, N])
        p1T = sb("p1T", [N, G, N])
        aT = sb("aT", [D, TN])
        x1 = sb("x1", [N, G, D])
        xn = sb("xn", [N, G, D])
        xg = sb("xg", [N, G, D])
        x1n = sb("x1n", [N, G, D])
        x1b = sb("x1b", [N, G, D])
        x1T = sb("x1T", [D, TN])
        hid = sb("hid", [D, FC, TN])
        x2 = sb("x2", [N, G, D])
        h0 = sb("h0", [N, G, D])
        xa = sb("xa", [N, G, D])
        xaT = sb("xaT", [D, TN])
        gT = sb("gT", [D, H, TN])
        vv = sb("vv", [N, G, H * D])
        pr = sb("pr", [N, G * H, N])
        prT = sb("prT", [N, G * H, N])
        mx2 = sb("mx2", [N, G * H])
        nb2 = sb("nb2", [N, G * H])
        es2 = sb("es2", [N, G * H])
        rs2 = sb("rs2", [N, G * H])
        h1 = sb("h1", [N, G, D])
        h1n = sb("h1n", [N, G, D])
        tn = sb("tn", [N, G, D])
        hT = sb("hT", [D, TN])
        rT = sb("rT", [DR, TN])
        lg = sb("lg", [N, G, E])
        top = sb("top", [N, G, 8])
        topi = sb("topi", [N, G, 8], U32)
        topf = sb("topf", [N, G * TOPK])
        gap = sb("gap", [N, G])
        egap = sb("egap", [N, G])
        egap1 = sb("egap1", [N, G])
        wnow = sb("wnow", [N, G, TOPK])
        oh = sb("oh", [N, G, TOPK, E])
        ohs = sb("ohs", [N, G, E])
        cum = sb("cum", [N, E])
        rjunk = sb("rjunk", [N, G * TOPK, E])
        rank = sb("rank", [N, G * TOPK])
        slotf = sb("slotf", [N, G * TOPK])
        stat = sb("stat", [N, G, 6])
        mv = sb("mv", [N, G, 2])
        ve = sb("ve", [N, G])
        mv2 = sb("mv2", [N, G, 2])
        ve2 = sb("ve2", [N, G])
        rstd3 = sb("rstd3", [N, G])
        rstd = sb("rstd", [N, G])
        vr = sb("vr", [N, G])
        rstd2 = sb("rstd2", [N, G])

        cntf = sb("cntf", [MAXT, E])
        cnti = sb("cnti", [MAXT, E], I32)
        ntf = sb("ntf", [MAXT, E])
        tend = sb("tend", [MAXT, E])
        le = sb("le", [MAXT, E])
        lejunk = sb("lejunk", [MAXT, E])
        tcol = sb("tcol", [MAXT, 8])
        ui = sb("ui", [MAXT, 1], I32)
        tinfo = sb("tinfo", [MAXT, 4])
        ttab = sb("ttab", [1, MAXT + 3], I32)
        trow = sb("trow", [MAXT, 1], I32)
        idrows = sb("idrows", [MAXT, TILE], I32)
        idf = sb("idf", [MAXT, TILE])
        wbuf = sb("wbuf", [D, RING, WCOLS])
        b2buf = sb("b2buf", [TILE, RING, D])
        iall = sb("iall", [TILE, MAXT], I32)
        igather = sb("igather", [TILE, RING], I32)
        iscatter = sb("iscatter", [TILE, RING], I32)
        hrow = [sb(f"hrow{r}", [TILE, D]) for r in range(RING)]
        hbT = sb("hbT", [D, 2, TILE])
        act_h = sb("act_h", [D, 2, DFF])
        eo = [sb(f"eo{r}", [TILE, D]) for r in range(RING)]

        er = spread[0:N, :].rearrange("p (a g k d) -> p a g k d", a=PAIRS, g=G, k=TOPK)
        wl = sb("wl", [N, G * TOPK])
        sh = sb("sh", [D, SC2, TN])
        of = sb("of", [N, G, D])
        hm1, hm2, hm, rh, rh2, fn, fT, fh = x1, x2, h1, x1n, xg, xn, aT, hid

        b_s, b_qk, b_v, b_t, b_y = ps("b_s"), ps("b_qk"), ps("b_v"), ps("b_t"), ps("b_y")
        big = [ps("big0"), ps("big1"), ps("big2")]
        p_score = b_s[0:SR, 0:TN].rearrange("p (g n) -> p g n", g=G)
        p_v = b_v[0:N, 0:G * D].rearrange("p (g n) -> p g n", g=G)
        p_o = p_v
        p_xT = b_v[:, 256:256 + TN]
        p_y = b_y[0:N, 0:G * D].rearrange("p (g n) -> p g n", g=G)
        p_rT = b_y[0:DR, 0:TN]
        p_lg = b_y[0:N, 192:192 + G * E]
        p_rank = b_y[0:N, 320:320 + G * E].rearrange("p (g n) -> p g n", g=G)

        s = {n: ctx.enter_context(nc.semaphore("s_" + n)) for n in [
            "early", "late", "consts", "gate", "raw_mm", "raw_ev", "pool_c", "tab_init", "ids",
            "emb", "xs", "xs_t", "xT", "qkv", "qk_ev", "v_ev", "add_v", "add_p", "tanh", "score",
            "nmax", "exp1", "p1n", "p1t_ps", "p1T", "aT_ps", "aT", "y", "x1n", "x1b", "x1T_ps", "x1T",
            "big", "big_a", "big_v", "y2", "xa", "xaT_ps", "xaT", "nb2", "exp2", "rs2", "pn",
            "o", "tn", "tn_st", "hT_ps", "hT", "hcopy", "rT_ps", "rT", "lg", "gap", "egap", "oh",
            "rank_ps", "rank", "slot", "tid", "ei", "scat", "ve", "rstd", "ve2", "rstd2", "chain", "res",
            "cnt", "tinfo", "trow", "ttab",
            "idrows", "idf", "ids_t", "iall", "cg", "cs",
            *[f"{n}{r}" for n in ("w", "h", "st") for r in range(RING)],
            "tr", "hbT", "g1", "silu", "g2", "eo",
            *[f"er{i}" for i in range(len(RESULT_LOADS))], "sh_ps", "sh", "ys", "fve", "frstd", "fn", "fT_ps", "fT", "f1",
            "fa", "f2", "of", "out"]}
        s_w, s_h, s_st = ([s[f"{n}{r}"] for r in range(RING)] for n in ("w", "h", "st"))
        block = ctx.enter_context(nc.Block())

        def gate(eng, sem, value):
            eng.wait_ge(sem, value)
            eng.sem_inc(s["gate"], 1)

        def turns_less(eng, n):
            at = MAXT + n
            return eng.value_load(ttab[0:1, at:at + 1], min_val=T * TOPK // TILE // RING - n,
                                  max_val=MAXT // RING - n)

        def big_freed(eng, p, u):
            u = u - 3
            if u < 0:
                u, p = u + BIGS, p - 1
            if isinstance(p, int) and p < 0:
                return
            emptied(eng, p, u)

        def emptied(eng, p, u):
            if u in ACT_BIG:
                eng.wait_ge(s["big_a"], p * len(ACT_BIG) + ACT_BIG.index(u) + 1)
            else:
                rest = [x for x in range(BIGS) if x not in ACT_BIG]
                eng.wait_ge(s["big_v"], p * len(rest) + rest.index(u) + 1)

        def all_emptied(eng, p, uses):
            for theirs in (set(ACT_BIG), set(range(BIGS)) - set(ACT_BIG)):
                if theirs & set(uses):
                    emptied(eng, p, max(theirs & set(uses)))

        def filled(eng, p, u, alone=False):
            eng.wait_ge(s["big"], p * BIGS + u + 1)
            if alone:
                eng.sem_inc(s["gate"], 1)

        def pipeline(eng, begin, chunk, post, pre, lead, loop=None):
            def put(p, c):
                if c == 0:
                    begin(p)
                chunk(p, c)

            def body(p, posts, is_last):
                for c in range(CH):
                    if lead is not None:
                        if c + lead < CH:
                            put(p, c + lead)
                        elif not is_last:
                            put(p + 1, c + lead - CH)
                    sides(p, c, posts, not is_last)
                    if lead is None:
                        put(p, c)

            def sides(p, c, posts, has_next):
                for k in sorted(posts, reverse=True):
                    for f in post.get(c + (k - 1) * CH, []):
                        f(p - k)
                if has_next:
                    for f in pre.get(c, []):
                        f(p + 1)

            for c in range(CH):
                for f in pre.get(c, []):
                    f(0)
            for c in range(lead or 0):
                put(0, c)
            every = range(1, DEPTH + 1)
            for p in range(DEPTH + 1):
                body(p, range(p + 1), False)
            if loop is not None:
                loop.enter(DEPTH + 1)
            with eng.Fori(DEPTH + 1, PAIRS - 1) as p:
                if loop is not None:
                    loop.at(p)
                body(p, (0, *every), False)
            if loop is not None:
                loop.leave(PAIRS - 1)
            body(PAIRS - 1, (0, *every), True)
            for k in every:
                for c in range(CH):
                    sides(PAIRS - 1 + k, c, every[k - 1:], False)

        @block.sync
        def _(sp):
            def load(dst, src, sem):
                sp.dma_start(dst, src).then_inc(sem, 16)

            load(tok_i[:, :], io["x"], s["ids"])
            load(ident[:, :], io["ident"], s["early"])
            load(wqkv[:, 0, :], io["L0_tok_Wq"], s["early"])
            load(wqkv[:, 1, :], io["L0_tok_Wk"], s["early"])
            load(wqkv[:, 2, :], io["L0_tok_Wv"], s["early"])
            load(cols[:, :], io["cols"], s["early"])
            load(pe_rows[:, :], io["pe"], s["early"])
            for n in ROWS:
                load(row[n][:, :], io["row_" + n].partition_broadcast(N), s["early"])
            for i, n in enumerate(["Wq", "Wk", "Wv", "WoT"]):
                load(raw[:, i, :].rearrange("p (h d) -> p h d", h=H),
                     io["attn_" + n].rearrange("(h k) d -> k h d", h=H), s["late"])
            load(wo[:, :], io["L0_tok_Wo"], s["late"])
            load(w1[:, :], io["L0_tok_W1"], s["late"])
            load(w2[:, :, :], io["L0_tok_W2"].rearrange("(c p) n -> p c n", p=D), s["late"])
            load(wr[:, :], io["L0_ffn_Wr"], s["late"])
            load(cbT[:, :], io["cbT"], s["late"])
            load(mask[:, :], io["mask"], s["late"])
            load(tri[:, :], io["tri"], s["late"])
            load(ws1[:, :], io["L0_ffn_Ws1"], s["late"])
            load(ws2[:, :, :], io["L0_ffn_Ws2"].rearrange("(c p) n -> p c n", p=D), s["late"])
            load(wf1[:, :], io["L0_ffn_Wf1"], s["late"])
            load(wf2[:, :, :], io["L0_ffn_Wf2"].rearrange("(c p) n -> p c n", p=D), s["late"])
            sp.wait_ge(s["pool_c"], 1)
            load(tab_dram.rearrange("(p n) a -> p (n a)", p=128), sentinel[:, :], s["tab_init"])

            def store_tokens(p):
                gate(sp, s["tn"], p + 1)
                rows = tok_dram[bass.ds(p * TN * TOPK, TN * TOPK), :]
                for k in range(TOPK):
                    sp.dma_start(rows.rearrange("(g n k) d -> n g k d", g=G, k=TOPK)[:, :, k, :],
                                 tn[:, :, :]).then_inc(s["tn_st"], 16)

            store_tokens(0)
            with sp.Fori(1, PAIRS) as p:
                store_tokens(p)

            sp.wait_ge(s["ttab"], 1)
            turns = turns_less(sp, 0)

            def load_tile(u, r, again=True):
                t = u * RING + r
                if again:
                    gate(sp, s["eo"], t - RING + 1)
                e = sp.value_load(ttab[0:1, bass.ds(t, 1)], min_val=0, max_val=E - 1)
                sp.dma_start(wbuf[:, r, :], io["wpack"][bass.ds(e, 1), :, :]).then_inc(s_w[r], 16)
                sp.dma_start(b2buf[:, r, :], io["L0_ffn_b2"][bass.ds(e, 1), :].rearrange("a d -> (a d)")
                             .partition_broadcast(TILE)).then_inc(s_w[r], 16)

            for r in range(RING):
                load_tile(0, r, again=False)
            with sp.Fori(1, turns) as u:
                for r in range(RING):
                    load_tile(u, r)

            for r in range(RING):
                gate(sp, s_st[r], turns * 16)

            for i, (first, past) in enumerate(RESULT_LOADS):
                sp.dma_start(er[:, first:past, :, :, :].rearrange("n a g k d -> n (a g) (k d)"),
                             eo_dram[first * TN * TOPK:past * TN * TOPK, :].rearrange(
                                 "(a n k) d -> n a (k d)", n=N, k=TOPK)).then_inc(s[f"er{i}"], 16)

            def store_out(p):
                gate(sp, s["of"], p + 1)
                sp.dma_start(out[bass.ds(p * G, G), :, :].rearrange("g n d -> n g d"),
                             of[:, :, :]).then_inc(s["out"], 16)

            store_out(0)
            with sp.Fori(1, PAIRS) as p:
                store_out(p)
            sp.wait_ge(s["out"], 16 * PAIRS)
            sp.wait_ge(s["tn_st"], 16 * TOPK * PAIRS)

        @block.gpsimd
        def _(pool):
            pool.memset(sentinel[:, :], TOPK * T).then_inc(s["pool_c"], 1)
            pool.memset(neghalf[:, :], -0.5).then_inc(s["pool_c"], 1)
            pool.memset(ones[:, :], 1.0).then_inc(s["pool_c"], 1)
            pool.memset(cum[:, :], 0.0).then_inc(s["pool_c"], 1)
            pool.memset(apad[:, :], 0.0).then_inc(s["pool_c"], 1)
            pool.iota(choice[:, :], [[TOPK * N, B], [1, TOPK]], base=0, channel_multiplier=TOPK)\
                .then_inc(s["pool_c"], 1)
            pool.iota(iota_e[:, :], [[1, E]], base=0, channel_multiplier=0,
                      allow_small_or_imprecise_dtypes=True).then_inc(s["pool_c"], 1)
            pool.iota(iota_t[:, :], [[1, 1]], base=0, channel_multiplier=1,
                      allow_small_or_imprecise_dtypes=True).then_inc(s["pool_c"], 1)
            for r in range(RING):
                pool.memset(hrow[r][:, :], 0.0).then_inc(s["pool_c"], 1)

            def gather_emb(p):
                if isinstance(p, int) and p == 0:
                    pool.wait_ge(s["ids"], 17)
                else:
                    gate(pool, s["xs"], p)
                pool.tensor_copy(ei_now[:, :], eidx[:, bass.ds(p * G, G)]).then_inc(s["ei"], 1)
                gate(pool, s["ei"], p + 1)
                for g in range(G):
                    pool.indirect_dma_start(
                        emb_rows[:, g, :], None, io["L0_tok_emb"],
                        bass.IndirectOffsetOnAxis(ap=ei_now[:, g:g + 1].bitcast(U32), axis=0),
                        bounds_check=VOCAB - 1, oob_is_err=False).then_inc(s["emb"], 16)

            def begin(p):
                pass

            def chunk(p, c):
                if c not in POOL_CHUNKS:
                    return
                if c == POOL_CHUNKS[0]:
                    pool.wait_ge(s["qk_ev"], p + 1)
                if not (isinstance(p, int) and p == 0 and c < TRING):
                    pool.wait_ge(s["score"], p * CH + c - TRING + 1)
                g, cc = c // CPB, c % CPB
                qv = qT[:, g * N:(g + 1) * N].rearrange("p (a m) -> p a m", a=QG)[:, :, CQ * cc:CQ * cc + CQ]
                kv = kT[:, g * N:(g + 1) * N]
                pool.tensor_tensor(
                    tbuf[:, c % TRING, :].rearrange("p (a m n) -> p a m n", a=QG, m=CQ),
                    qv.unsqueeze(3).to_broadcast([D, QG, CQ, N]),
                    kv.unsqueeze(1).unsqueeze(1).to_broadcast([D, QG, CQ, N]), ALU.add).then_inc(s["add_p"], 1)

            def rstd_of(k):
                def f(p):
                    pool.wait_ge(s["ve"], 3 * p + k + 1)
                    pool.tensor_tensor(rstd[:, :], ve[:, :], neghalf[:, :], ALU.pow).then_inc(s["rstd"], 1)
                return f

            def rstd2_of(k):
                def f(p):
                    pool.wait_ge(s["ve2"], 2 * p + k + 1)
                    pool.tensor_tensor([rstd2, rstd3][k][:, :], ve2[:, :], neghalf[:, :],
                                       ALU.pow).then_inc(s["rstd2"], 1)
                return f

            def x1_bias(p):
                pool.wait_ge(s["x1n"], p + 1)
                pool.tensor_tensor(x1b[:, :, :], x1n[:, :, :],
                                   row["bf2"][:, :].unsqueeze(1).to_broadcast([N, G, D]),
                                   ALU.add).then_inc(s["x1b"], 1)

            def normalise(k):
                def f(p):
                    pool.wait_ge(s["rs2"], 4 * p + k + 1)
                    v = pr[:, 4 * k:4 * k + 4, :]
                    pool.tensor_tensor(v, v, rs2[:, 4 * k:4 * k + 4].unsqueeze(2).to_broadcast([N, 4, N]),
                                       ALU.mult).then_inc(s["pn"], 1)
                return f

            def keep_h(p):
                gate(pool, s["hT"], p + 1)
                pool.tensor_copy(hall[:, bass.ds(p, 1), :], hT[:, :]).then_inc(s["hcopy"], 1)

            def scatter_ids(p):
                if isinstance(p, int) and p == 0:
                    pool.wait_ge(s["tab_init"], 16)
                gate(pool, s["slot"], p + 1)
                if not (isinstance(p, int) and p == 0):
                    gate(pool, s["scat"], p * 16 * G * TOPK)
                pool.tensor_copy(tid_now[:, :], choice[:, bass.ds(p * G * TOPK, G * TOPK)]).then_inc(s["tid"], 1)
                gate(pool, s["tid"], p + 1)
                scatter_batch(p, 0)

            def scatter_batch(p, g):
                for k in range(TOPK):
                    j = g * TOPK + k
                    pool.indirect_dma_start(
                        tab_dram, bass.IndirectOffsetOnAxis(ap=slot_now[:, j:j + 1].bitcast(U32), axis=0),
                        tid_now[:, j:j + 1], None, bounds_check=TABN - 1,
                        oob_is_err=False).then_inc(s["scat"], 16)

            def scatter_rest(p):
                scatter_batch(p, 1)

            pipeline(pool, begin, chunk,
                     {3: [rstd_of(0)], 6: [x1_bias], 7: [rstd_of(1)], 10: [rstd_of(2)],
                      17: [normalise(0), normalise(1)], 19: [normalise(2), normalise(3)], 26: [rstd2_of(0)],
                      28: [rstd2_of(1)], 32: [keep_h], 37: [scatter_ids], 43: [scatter_rest]},
                     {3: [gather_emb]}, 3)

            pool.wait_ge(s["scat"], 16 * TOPK * B)
            pool.wait_ge(s["tinfo"], 1)
            pool.indirect_dma_start(
                idrows[:, :], None, tab_dram.rearrange("(a b) n -> a (b n)", b=TILE),
                bass.IndirectOffsetOnAxis(ap=trow[:, :].bitcast(U32), axis=0),
                bounds_check=TABN // TILE - 1, oob_is_err=False).then_inc(s["idrows"], 16)

            pool.wait_ge(s["ttab"], 1)
            turns = turns_less(pool, 0)
            pool.wait_ge(s["tn_st"], 16 * TOPK * PAIRS)

            def gather_tile(u, r, again=True):
                t = u * RING + r
                gate(pool, s["cg"], t + 1)
                if again:
                    gate(pool, s["tr"], t - RING + 1)
                pool.indirect_dma_start(
                    hrow[r][:, :], None, tok_dram,
                    bass.IndirectOffsetOnAxis(ap=igather[:, r:r + 1].bitcast(U32), axis=0),
                    bounds_check=TOPK * T - 1, oob_is_err=False).then_inc(s_h[r], 16)

            def scatter_tile(u, r):
                t = u * RING + r
                gate(pool, s["cs"], t + 1)
                gate(pool, s["eo"], t + 1)
                pool.indirect_dma_start(
                    eo_dram, bass.IndirectOffsetOnAxis(ap=iscatter[:, r:r + 1].bitcast(U32), axis=0),
                    eo[r][:, :], None, bounds_check=TOPK * T - 1, oob_is_err=False).then_inc(s_st[r], 16)

            for r in range(RING):
                gather_tile(0, r, again=False)
            gather_tile(1, 0)
            gather_tile(1, 1)
            gather_tile(1, 2)
            scatter_tile(0, 0)
            gather_tile(1, 3)
            scatter_tile(0, 1)
            with pool.Fori(2, turns) as u:
                gather_tile(u, 0)
                scatter_tile(u - 2, 2)
                gather_tile(u, 1)
                scatter_tile(u - 2, 3)
                gather_tile(u, 2)
                scatter_tile(u - 1, 0)
                gather_tile(u, 3)
                scatter_tile(u - 1, 1)
            before, last = turns_less(pool, 2), turns_less(pool, 1)
            scatter_tile(before, 2)
            scatter_tile(before, 3)
            for r in range(RING):
                if r == 1:
                    gate(pool, s_st[2], 16 * last)
                    gate(pool, s_st[3], 16 * last)
                if r:
                    gate(pool, s_st[r - 1], 16 * (last + 1))
                scatter_tile(last, r)

            def rstd_last(p):
                pool.wait_ge(s["fve"], p + 1)
                pool.tensor_tensor(rstd[:, :], ve[:, :], neghalf[:, :], ALU.pow).then_inc(s["frstd"], 1)

            rstd_last(0)
            with pool.Fori(1, PAIRS) as p:
                rstd_last(p)

        @block.scalar
        def _(act):
            act.preload_act_table(ACT.Exp)
            act.wait_ge(s["early"], 16 * (6 + len(ROWS)))

            def begin(p):
                pass

            def chunk(p, c):
                if c in POOL_CHUNKS:
                    act.wait_ge(s["add_p"], p * len(POOL_CHUNKS) + POOL_CHUNKS.index(c) + 1)
                else:
                    mine = [x for x in range(CH) if x not in POOL_CHUNKS]
                    act.wait_ge(s["add_v"], p * len(mine) + mine.index(c) + 1)
                v = tbuf[:, c % TRING, :]
                act.activation(v, v, ACT.Tanh).then_inc(s["tanh"], 1)

            def xT_copy(p):
                act.wait_ge(s["xs_t"], p + 1)
                act.activation(xT[:, :], p_xT, ACT.Identity).then_inc(s["xT"], 1)

            def exp1(p):
                act.wait_ge(s["nmax"], p + 1)
                for g in range(G):
                    last = act.activation(p1[:, g, :], p_score[:, g, :], ACT.Exp, bias=nmax[:, g:g + 1],
                                          accum_out=esum[:, g:g + 1])
                last.then_inc(s["exp1"], 1)

            def aT_copy(p):
                act.wait_ge(s["aT_ps"], p + 1)
                act.activation(aT[:, :], b_t[:, 0:TN], ACT.Identity).then_inc(s["aT"], 1)

            def x1T_copy(p):
                act.wait_ge(s["x1T_ps"], p + 1)
                act.activation(x1T[:, :], b_t[:, 0:TN], ACT.Identity).then_inc(s["x1T"], 1)

            def relu(k):
                def f(p):
                    filled(act, p, k)
                    for j in range(2):
                        c = 2 * k + j
                        last = act.activation(hid[:, c, :], big[k][:, j * TN:(j + 1) * TN], ACT.Relu,
                                              bias=bf1[:, c:c + 1])
                    last.then_inc(s["big_a"], 1)
                return f

            def xaT_copy(p):
                act.wait_ge(s["xaT_ps"], p + 1)
                act.activation(xaT[:, :], b_t[:, 0:TN], ACT.Identity).then_inc(s["xaT"], 1)

            def g_copy(k):
                def f(p):
                    filled(act, p, 2 + k)
                    act.activation(gT[:, 2 * k:2 * k + 2, :].rearrange("p a n -> p (a n)"),
                                   big[(2 + k) % 3][:, 0:2 * TN], ACT.Identity).then_inc(s["big_a"], 1)
                return f

            def vv_copy(k):
                def f(p):
                    filled(act, p, 6 + k)
                    act.activation(vv[:, k // 2, (k % 2) * 512:(k % 2 + 1) * 512],
                                   big[(6 + k) % 3][0:N, :], ACT.Identity).then_inc(s["big_a"], 1)
                return f

            def exp2(k):
                def f(p):
                    act.wait_ge(s["nb2"], 4 * p + k + 1)
                    for j in range(4 * k, 4 * k + 4):
                        last = act.activation(pr[:, j, :], pr[:, j, :], ACT.Exp, bias=nb2[:, j:j + 1],
                                              scale=SCALE, accum_out=es2[:, j:j + 1])
                    last.then_inc(s["exp2"], 1)
                return f

            def prT_copy(k):
                def f(p):
                    filled(act, p, 14 + k)
                    act.activation(prT[:, 4 * k:4 * k + 4, :].rearrange("p a n -> p (a n)"),
                                   big[(14 + k) % 3][0:N, 0:4 * N], ACT.Identity).then_inc(s["big_a"], 1)
                return f

            def hT_affine(p):
                act.wait_ge(s["hT_ps"], p + 1)
                if not (isinstance(p, int) and p == 0):
                    act.wait_ge(s["hcopy"], p)
                act.activation(hT[:, :], b_t[:, 0:TN], ACT.Identity, bias=ln1_b, scale=ln1_g).then_inc(s["hT"], 1)

            def rT_copy(p):
                act.wait_ge(s["rT_ps"], p + 1)
                act.activation(rT[:, :], p_rT, ACT.Identity).then_inc(s["rT"], 1)

            def gate_exp(p):
                act.wait_ge(s["gap"], p + 1)
                act.activation(egap[:, :], gap[:, :], ACT.Exp, scale=1.0 / TEMP).then_inc(s["egap"], 1)

            pipeline(act, begin, chunk,
                     {-1: [exp1], 1: [aT_copy], 6: [x1T_copy, relu(0), relu(1)], 11: [xaT_copy],
                      12: [g_copy(0), g_copy(1)], 13: [g_copy(2)], 15: [vv_copy(1)],
                      17: [exp2(0), exp2(1), exp2(2)], 18: [exp2(3)], 20: [prT_copy(1), prT_copy(2)],
                      30: [hT_affine, rT_copy], 35: [gate_exp]},
                     {10: [xT_copy]}, 1)

            act.preload_act_table(ACT.Silu)
            act.wait_ge(s["ttab"], 1)
            turns = turns_less(act, 0)

            def silu(u, r):
                t = u * RING + r
                act.wait_ge(s["g1"], t + 1)
                for c in range(FC):
                    last = act.activation(act_h[:, r % 2, c * TILE:(c + 1) * TILE],
                                          big[r % 2][:, c * TILE:(c + 1) * TILE], ACT.Silu,
                                          bias=wbuf[:, r, 2 * DFF + c:2 * DFF + c + 1])
                last.then_inc(s["silu"], 1)

            def gather_index(u, r):
                if not isinstance(u, int):
                    gate(act, s_h[r], 16 * u)
                elif u > 0:
                    act.wait_ge(s_h[r], 16 * u)
                act.activation(igather[:, r:r + 1], iall[:, bass.ds(u * RING + r, 1)], ACT.Identity)\
                    .then_inc(s["cg"], 1)

            def scatter_index(u, r):
                if not isinstance(u, int):
                    gate(act, s_st[r], 16 * u)
                elif u > 0:
                    act.wait_ge(s_st[r], 16 * u)
                act.activation(iscatter[:, r:r + 1], iall[:, bass.ds(u * RING + r, 1)], ACT.Identity)\
                    .then_inc(s["cs"], 1)

            act.wait_ge(s["iall"], 1)
            for r in range(RING):
                gather_index(0, r)
            for r in range(RING):
                gather_index(1, r)
                scatter_index(0, r)
                silu(0, r)
            with act.Fori(1, turns - 1) as u:
                for r in range(RING):
                    gather_index(u + 1, r)
                    scatter_index(u, r)
                    silu(u, r)
            last = turns_less(act, 1)
            for r in range(RING):
                scatter_index(last, r)
                silu(last, r)

            def silu_shared(p):
                act.wait_ge(s["sh_ps"], p + 1)
                for c in range(SC2):
                    last = act.activation(sh[:, c, :], b_t[:, c * TN:(c + 1) * TN], ACT.Silu,
                                          bias=bs1[:, c:c + 1])
                last.then_inc(s["sh"], 1)

            def silu_last(p):
                for c in range(FC):
                    if c % 2 == 0:
                        act.wait_ge(s["f1"], 2 * p + c // 2 + 1)
                    act.activation(fh[:, c, :], big[c // 2][:, (c % 2) * TN:(c % 2 + 1) * TN],
                                   ACT.Silu, bias=fbf1[:, c:c + 1]).then_inc(s["fa"], 1)

            def f_affine(p):
                act.wait_ge(s["fT_ps"], p + 1)
                act.activation(fT[:, :], b_v[:, 0:TN], ACT.Identity, bias=ffln_b, scale=ffln_g)\
                    .then_inc(s["fT"], 1)

            def step(p):
                silu_last(p - 1)
                silu_shared(p + 1)
                f_affine(p)

            silu_shared(0)
            silu_shared(1)
            f_affine(0)
            step(1)
            with act.Fori(2, PAIRS - 1) as p:
                step(p)
            silu_last(PAIRS - 2)
            f_affine(PAIRS - 1)
            silu_last(PAIRS - 1)

        @block.vector
        def _(dve):
            class Chain:
                count, base, first = 0, None, 0

                def link(self, ins):
                    self.count += 1
                    ins.then_inc(s["chain"], 1)

                def now(self):
                    return self.count if self.base is None else self.base + self.count

                def wait(self):
                    dve.wait_ge(s["chain"], self.now())

                def gate(self):
                    gate(dve, s["chain"], self.now())

                def enter(self, p):
                    self.start, self.first = self.count, p

                def at(self, p):
                    self.base = p * DVE_LINKS + (self.start - self.first * DVE_LINKS)
                    self.count = 0

                def leave(self, p):
                    assert self.count == DVE_LINKS, self.count
                    self.base, self.count = None, self.start + (p - self.first) * DVE_LINKS

            ch = Chain()

            dve.wait_ge(s["ids"], 16)
            ch.link(dve.tensor_copy(tok_f[:, :], tok_i[:, :]))
            ch.wait()
            ch.link(dve.tensor_scalar(neg_f[:, :], tok_f[:, :], 0.0, float(VOCAB), ALU.is_lt, ALU.mult))
            ch.wait()
            ch.link(dve.tensor_tensor(tok_f[:, :], tok_f[:, :], neg_f[:, :], ALU.add))
            ch.wait()
            dve.tensor_scalar(eidx[:, :], tok_f[:, :], 0.0, float(VOCAB - 1), ALU.max, ALU.min).then_inc(s["ids"], 1)
            dve.wait_ge(s["early"], 16 * (6 + len(ROWS)))
            dve.wait_ge(s["pool_c"], 8 + RING)
            dve.tensor_scalar(bs2q[:, :], row["bs2"][:, :], SHARED, None, ALU.mult)
            dve.tensor_copy(apad[:, 31:32], ascale).then_inc(s["consts"], 1)

            def begin(p):
                dve.wait_ge(s["qkv"], p + 1)
                if not (isinstance(p, int) and p == 0):
                    dve.wait_ge(s["add_p"], p * len(POOL_CHUNKS))
                    dve.wait_ge(s["add_v"], p * (CH - len(POOL_CHUNKS)))
                dve.tensor_scalar(qT[:, :], b_qk[:, 0:TN], bq, None, ALU.add)
                dve.tensor_scalar(kT[:, :], b_qk[:, TN:2 * TN], bk, None, ALU.add).then_inc(s["qk_ev"], 1)
                dve.wait_ge(s["qk_ev"], p + 1)
                if isinstance(p, int) and p == 0:
                    v_copy(0)

            def chunk(p, c):
                if c in POOL_CHUNKS:
                    return
                if not (isinstance(p, int) and p == 0 and c < TRING):
                    dve.wait_ge(s["score"], p * CH + c - TRING + 1)
                g, cc = c // CPB, c % CPB
                qv = qT[:, g * N:(g + 1) * N].rearrange("p (a m) -> p a m", a=QG)[:, :, CQ * cc:CQ * cc + CQ]
                kv = kT[:, g * N:(g + 1) * N]
                dve.tensor_tensor(
                    tbuf[:, c % TRING, :].rearrange("p (a m n) -> p a m n", a=QG, m=CQ),
                    qv.unsqueeze(3).to_broadcast([D, QG, CQ, N]),
                    kv.unsqueeze(1).unsqueeze(1).to_broadcast([D, QG, CQ, N]), ALU.add).then_inc(s["add_v"], 1)

            def v_copy(p):
                dve.wait_ge(s["qkv"], p + 1)
                dve.tensor_tensor(vrow[:, :, :], p_v, row["bv"][:, :].unsqueeze(1).to_broadcast([N, G, D]),
                                  ALU.add).then_inc(s["v_ev"], 1)

            def v_rows(p):
                if not (isinstance(p, int) and p == 0):
                    dve.wait_ge(s["aT_ps"], p)
                    v_copy(p)

            def x_rows(p):
                dve.wait_ge(s["emb"], 16 * G * (p + 1))
                dve.scalar_tensor_tensor(xs[:, :, :], emb_rows[:, :, :], float(np.float32(D) ** np.float32(0.5)),
                                         pe_rows[:, :].unsqueeze(1).to_broadcast([N, G, D]),
                                         ALU.mult, ALU.add).then_inc(s["xs"], 1)
                dve.wait_ge(s["xs"], p + 1)
                dve.tensor_tensor(res[:, bass.ds(p, 1), :, :].rearrange("p a g d -> p (a g) d"), xs[:, :, :],
                                  row["bo"][:, :].unsqueeze(1).to_broadcast([N, G, D]), ALU.add).then_inc(s["res"], 1)

            def softmax1_max(p):
                dve.wait_ge(s["score"], CH * (p + 1))
                dve.tensor_reduce(nmax[:, :], p_score, AX.X, ALU.max, negate=True).then_inc(s["nmax"], 1)

            def p1_norm(p):
                dve.wait_ge(s["exp1"], p + 1)
                ch.link(dve.reciprocal(rsum[:, :], esum[:, :]))
                ch.wait()
                for g in range(G):
                    last = dve.tensor_scalar(p1[:, g, :], p1[:, g, :], rsum[:, g:g + 1], None, ALU.mult)
                last.then_inc(s["p1n"], 1)

            def p1T_copy(p):
                dve.wait_ge(s["p1t_ps"], p + 1)
                dve.tensor_copy(p1T[:, :, :].rearrange("p g (a m) -> p (g a) m", a=QG),
                                b_t[0:N, 0:G * SR].rearrange("p (x m) -> p x m", m=32)[:, :, 0:QR]).then_inc(s["p1T"], 1)

            def ln_stats(x, eps, mv=mv, ve=ve, done="ve"):
                for g in range(G):
                    last = dve.bn_stats(stat[:, g, :], x[:, g, :])
                ch.link(last)
                ch.gate()
                for g in range(G):
                    last = dve.bn_aggr(mv[:, g, :], stat[:, g, :])
                ch.link(last)
                ch.wait()
                dve.tensor_scalar(ve[:, :], mv[:, :, 1], eps, None, ALU.add).then_inc(s[done], 1)

            def times_gamma(x, gamma):
                for g in range(G):
                    last = dve.scalar_tensor_tensor(xg[:, g, :], x[:, g, :], mv[:, g, 0:1], row[gamma][:, :],
                                                    ALU.subtract, ALU.mult)
                ch.link(last)

            def plus_beta(p, k, beta, y):
                dve.wait_ge(s["rstd"], 3 * p + k + 1)
                ch.wait()
                for g in range(G):
                    last = dve.scalar_tensor_tensor(y[:, g, :], xg[:, g, :], rstd[:, g:g + 1], row[beta][:, :],
                                                    ALU.mult, ALU.add)
                return last

            def x1_rows(p):
                dve.wait_ge(s["y"], p + 1)
                ch.wait()
                ch.link(dve.tensor_tensor(x1[:, :, :], p_y, res[:, bass.ds(p, 1), :, :].rearrange(
                    "p a g d -> p (a g) d"), ALU.add))
                ch.wait()
                ln_stats(x1, EPS_TOK)
                times_gamma(x1, "g1")

            def x1_norm(p):
                plus_beta(p, 0, "beta1", x1n).then_inc(s["x1n"], 1)

            def relu(k):
                def f(p):
                    filled(dve, p, k)
                    for j in range(2):
                        c = 2 * k + j
                        last = dve.tensor_scalar(hid[:, c, :], big[k][:, j * TN:(j + 1) * TN], bf1[:, c:c + 1],
                                                 0.0, ALU.add, ALU.max)
                    last.then_inc(s["big_v"], 1)
                return f

            def x2_rows(p):
                dve.wait_ge(s["y2"], p + 1)
                dve.wait_ge(s["x1b"], p + 1)
                ch.link(dve.tensor_tensor(x2[:, :, :], p_y, x1b[:, :, :], ALU.add))
                ch.wait()
                ln_stats(x2, EPS_TOK)
                times_gamma(x2, "g2")

            def x2_norm(p):
                ch.link(plus_beta(p, 1, "beta2", h0))
                ch.wait()
                ln_stats(h0, EPS)

            def xa_norm(p):
                dve.wait_ge(s["rstd"], 3 * p + 3)
                for g in range(G):
                    last = dve.tensor_scalar(xa[:, g, :], h0[:, g, :], mv[:, g, 0:1], rstd[:, g:g + 1],
                                             ALU.subtract, ALU.mult)
                last.then_inc(s["xa"], 1)

            def g_copy(k):
                def f(p):
                    filled(dve, p, 2 + k)
                    dve.tensor_copy(gT[:, 2 * k:2 * k + 2, :].rearrange("p a n -> p (a n)"),
                                    big[(2 + k) % 3][:, 0:2 * TN]).then_inc(s["big_v"], 1)
                return f

            def vv_copy(k):
                def f(p):
                    filled(dve, p, 6 + k)
                    dve.tensor_copy(vv[:, k // 2, (k % 2) * 512:(k % 2 + 1) * 512],
                                    big[(6 + k) % 3][0:N, :]).then_inc(s["big_v"], 1)
                return f

            def mask_max(k):
                def f(p):
                    filled(dve, p, 10 + k, alone=True)
                    for j in range(4):
                        h = 4 * k + j
                        last = dve.tensor_tensor_reduce(
                            pr[:, h, :], big[(10 + k) % 3][0:N, j * N:(j + 1) * N], mask[:, :],
                            1.0, -3.0e38, ALU.add, ALU.max, mx2[:, h:h + 1])
                    last.then_inc(s["big_v"], 1)
                    rest = [x for x in range(BIGS) if x not in ACT_BIG]
                    dve.wait_ge(s["big_v"], p * len(rest) + rest.index(10 + k) + 1)
                    dve.tensor_scalar(nb2[:, 4 * k:4 * k + 4], mx2[:, 4 * k:4 * k + 4], -SCALE, None,
                                      ALU.mult).then_inc(s["nb2"], 1)
                return f

            def inv_sums(k):
                def f(p):
                    dve.wait_ge(s["exp2"], 4 * p + k + 1)
                    dve.reciprocal(rs2[:, 4 * k:4 * k + 4], es2[:, 4 * k:4 * k + 4]).then_inc(s["rs2"], 1)
                return f

            def prT_copy(k):
                def f(p):
                    filled(dve, p, 14 + k)
                    dve.tensor_copy(prT[:, 4 * k:4 * k + 4, :].rearrange("p a n -> p (a n)"),
                                    big[(14 + k) % 3][0:N, 0:4 * N]).then_inc(s["big_v"], 1)
                return f

            def h1_rows(p):
                dve.wait_ge(s["o"], p + 1)
                ch.link(dve.tensor_tensor(h1[:, :, :], p_o, h0[:, :, :], ALU.add))
                ch.wait()
                ln_stats(h1, EPS, mv2, ve2, "ve2")

            def h1_norm(p):
                dve.wait_ge(s["rstd2"], 2 * p + 1)
                for g in range(G):
                    last = dve.tensor_scalar(h1n[:, g, :], h1[:, g, :], mv2[:, g, 0:1], rstd2[:, g:g + 1],
                                             ALU.subtract, ALU.mult)
                ch.link(last)
                ch.link(dve.tensor_tensor(vr[:, :], mv2[:, :, 1], rstd2[:, :], ALU.mult))
                ch.wait()
                ch.link(dve.tensor_tensor(vr[:, :], vr[:, :], rstd2[:, :], ALU.mult))
                ch.wait()
                dve.tensor_scalar(ve2[:, :], vr[:, :], EPS, None, ALU.add).then_inc(s["ve2"], 1)
                dve.tensor_tensor(res[:, bass.ds(p, 1), :, :].rearrange("p a g d -> p (a g) d"),
                                  h1[:, :, :], h1n[:, :, :], ALU.add).then_inc(s["res"], 1)

            def tn_rows(p):
                dve.wait_ge(s["rstd2"], 2 * p + 2)
                if not (isinstance(p, int) and p == 0):
                    dve.wait_ge(s["tn_st"], 16 * TOPK * p)
                for g in range(G):
                    last = dve.tensor_scalar(tn[:, g, :], h1n[:, g, :], rstd3[:, g:g + 1], None, ALU.mult)
                last.then_inc(s["tn"], 1)

            def route(p):
                dve.wait_ge(s["lg"], p + 1)
                ch.link(dve.tensor_copy(lg[:, :, :].rearrange("p g e -> p (g e)"), p_lg))
                ch.gate()
                for g in range(G):
                    last = dve.max(top[:, g, :], lg[:, g, :])
                ch.link(last)
                ch.gate()
                for g in range(G):
                    last = dve.max_index(topi[:, g, :], top[:, g, :], lg[:, g, :])
                ch.link(last)
                dve.tensor_tensor(gap[:, :], top[:, :, 1], top[:, :, 0], ALU.subtract).then_inc(s["gap"], 1)

            def one_hot(p):
                ch.wait()
                ch.link(dve.tensor_copy(topf[:, :].rearrange("p (g k) -> p g k", g=G), topi[:, :, 0:TOPK]))
                ch.wait()
                ch.link(dve.tensor_tensor(
                    oh[:, :, :, :].rearrange("p g k e -> p (g k) e"),
                    iota_e[0:N, :].unsqueeze(1).to_broadcast([N, G * TOPK, E]),
                    topf[:, :].unsqueeze(2).to_broadcast([N, G * TOPK, E]), ALU.is_equal))
                ch.wait()
                dve.tensor_tensor(ohs[:, :, :], oh[:, :, 0, :], oh[:, :, 1, :], ALU.add).then_inc(s["oh"], 1)

            def gate_weights(p):
                dve.wait_ge(s["egap"], p + 1)
                ch.link(dve.tensor_scalar(egap1[:, :], egap[:, :], 1.0, None, ALU.add))
                ch.wait()
                ch.link(dve.reciprocal(wnow[:, :, 0], egap1[:, :]))
                ch.wait()
                ch.link(dve.tensor_tensor(wnow[:, :, 1], egap[:, :], wnow[:, :, 0], ALU.mult))
                ch.wait()
                dve.tensor_scalar(wts[:, bass.ds(p, 1), :].rearrange("p a j -> p (a j)"),
                                  wnow[:, :, :].rearrange("p g k -> p (g k)"), 1.0, None,
                                  ALU.mult).then_inc(s["res"], 1)

            def ranks(p):
                dve.wait_ge(s["rank_ps"], p + 1)
                for g in range(G):
                    for k in range(TOPK):
                        j = g * TOPK + k
                        last = dve.tensor_tensor_reduce(rjunk[:, j, :], p_rank[:, g, :], oh[:, g, k, :], 1.0, 0.0,
                                                        ALU.mult, ALU.add, rank[:, j:j + 1])
                last.then_inc(s["rank"], 1)
                ch.link(dve.tensor_tensor(cum[:, :], cum[:, :], ohs[:, 0, :], ALU.add))
                ch.wait()
                ch.link(dve.tensor_tensor(cum[:, :], cum[:, :], ohs[:, 1, :], ALU.add))
                ch.wait()
                ch.link(dve.scalar_tensor_tensor(slotf[:, :], topf[:, :], float(T), rank[:, :], ALU.mult, ALU.add))
                ch.wait()
                if not (isinstance(p, int) and p == 0):
                    dve.wait_ge(s["scat"], p * 16 * G * TOPK)
                dve.tensor_scalar(slot_now[:, :], slotf[:, :], 1.0, None, ALU.mult).then_inc(s["slot"], 1)

            def products(p):
                if not (isinstance(p, int) and p == 1):
                    return
                for i in range(4):
                    dve.wait_ge(s["raw_mm"], i + 1)
                    bank = [big[0], big[1], big[2], b_t][i]
                    dst = (mh if i < 2 else vo)[:, (i % 2) * 512:(i % 2 + 1) * 512]
                    dve.tensor_copy(dst, bank[:, :]).then_inc(s["raw_ev"], 1)

            pipeline(dve, begin, chunk,
                     {-12: [v_rows], -1: [softmax1_max], 0: [p1_norm], 3: [p1T_copy], 5: [x1_rows],
                      6: [x1_norm], 10: [x2_rows, x2_norm], 11: [xa_norm], 14: [g_copy(3)], 15: [vv_copy(0)],
                      16: [vv_copy(2), vv_copy(3), mask_max(0)], 18: [mask_max(1)],
                      19: [inv_sums(0), mask_max(2)], 20: [inv_sums(1), inv_sums(2), mask_max(3), prT_copy(0)],
                      21: [inv_sums(3)], 24: [prT_copy(3)], 26: [h1_rows], 28: [h1_norm], 30: [tn_rows],
                      32: [route, one_hot], 36: [ranks], 38: [gate_weights]},
                     {8: [x_rows], 12: [products]}, 1, ch)

            dve.wait_ge(s["cnt"], 1)
            ch.link(dve.tensor_scalar(cnti[:, :], b_t[0:MAXT, 0:E], float(TILE - 1), None, ALU.add))
            ch.wait()
            ch.link(dve.tensor_scalar(cnti[:, :], cnti[:, :], TILE.bit_length() - 1, None, ALU.logical_shift_right))
            ch.wait()
            ch.link(dve.tensor_copy(ntf[:, :], cnti[:, :]))
            ch.link(dve.memset(cntf[:, :], 1.0))
            ch.wait()
            ch.link(dve.tensor_tensor_scan(tend[:, :], cntf[:, :], ntf[:, :], 0.0, ALU.mult, ALU.add))
            ch.wait()
            ch.link(dve.tensor_scalar(le[:, :], tend[:, :], iota_t[0:MAXT, 0:1], None, ALU.is_le))
            ch.wait()
            ch.link(dve.tensor_reduce(tcol[:, 0:1], le[:, :], AX.X, ALU.add))
            ch.link(dve.tensor_tensor_reduce(lejunk[:, :], le[:, :], ntf[:, :], 1.0, 0.0, ALU.mult, ALU.add,
                                             tcol[:, 1:2]))
            ch.wait()
            ch.link(dve.tensor_scalar(tinfo[:, 0:1], tcol[:, 0:1], float(E - 1), None, ALU.min))
            ch.link(dve.tensor_tensor(tcol[:, 2:3], iota_t[0:MAXT, 0:1], tcol[:, 1:2], ALU.subtract))
            ch.link(dve.tensor_scalar(ui[:, :], tend[:, E - 1:E], float(RING - 1), 1.0 / RING, ALU.add, ALU.mult))
            ch.wait()
            ch.link(dve.scalar_tensor_tensor(tcol[:, 3:4], tinfo[:, 0:1], float(T // TILE), tcol[:, 2:3],
                                             ALU.mult, ALU.add))
            ch.wait()
            dve.tensor_scalar(trow[:, :], tcol[:, 3:4], float(TABN // TILE - 1), None, ALU.min)
            ch.link(dve.tensor_copy(tcol[:, 5:6], ui[:, :]))
            ch.wait()
            ch.link(dve.scalar_tensor_tensor(tcol[:, 6:7], tcol[:, 5:6], float(-RING), tend[:, E - 1:E],
                                             ALU.mult, ALU.add))
            ch.wait()
            ch.link(dve.tensor_scalar(tcol[:, 7:8], tcol[:, 6:7], float(-RING), None, ALU.is_le))
            ch.wait()
            for n in range(3):
                last = dve.tensor_scalar(tinfo[:, 1 + n:2 + n], tcol[:, 5:6], tcol[:, 7:8], float(n),
                                         ALU.subtract, ALU.subtract)
            last.then_inc(s["tinfo"], 1)
            dve.wait_ge(s["trow"], 1)
            dve.tensor_copy(ttab[0:1, :], b_y[0:1, 0:MAXT + 3]).then_inc(s["ttab"], 1)
            dve.wait_ge(s["ttab"], 1)
            turns = turns_less(dve, 0)
            dve.wait_ge(s["idrows"], 16)
            dve.tensor_copy(idf[:, :], idrows[:, :]).then_inc(s["idf"], 1)
            dve.wait_ge(s["ids_t"], 1)
            dve.tensor_copy(iall[:, :], b_v[:, 0:MAXT]).then_inc(s["iall"], 1)

            def hb_affine(u, r):
                t = u * RING + r
                dve.wait_ge(s["tr"], t + 1)
                dve.tensor_scalar(hbT[:, r % 2, :], b_t[:, 0:TILE], ln1_g, ln1_b, ALU.mult, ALU.add)\
                    .then_inc(s["hbT"], 1)

            def eo_copy(u, r):
                t = u * RING + r
                dve.wait_ge(s["g2"], t + 1)
                if not (isinstance(u, int) and u == 0):
                    dve.wait_ge(s_st[r], 16 * u)
                dve.tensor_tensor(eo[r][:, :], [b_s, b_qk][r % 2][:, 0:D], b2buf[:, r, :], ALU.add)\
                    .then_inc(s["eo"], 1)

            def turn(u, before):
                for r in range(RING):
                    hb_affine(u, r)
                    if r >= 2:
                        eo_copy(u, r - 2)
                    elif before is not None:
                        eo_copy(before, r + 2)

            turn(0, None)
            turn(1, 0)
            with dve.Fori(2, turns) as u:
                turn(u, u - 1)
            for r in (2, 3):
                eo_copy(turns_less(dve, 1), r)

            def mixture(p):
                ch2.link(dve.tensor_scalar(wl[:, :], wts[:, bass.ds(p, 1), :].rearrange("p a j -> p (a j)"), 1.0,
                                           None, ALU.mult))
                dve.wait_ge(s[f"er{p if isinstance(p, int) and p < 2 else 2}"], 16)
                ch2.wait()
                for g in range(G):
                    last = dve.scalar_tensor_tensor(hm1[:, g, :], er[:, bass.ds(p, 1), g, 0, :].rearrange("p a d -> p (a d)"), wl[:, 2 * g:2 * g + 1],
                                                    bs2q[:, :], ALU.mult, ALU.add)
                ch2.link(last)
                ch2.wait()
                for g in range(G):
                    last = dve.scalar_tensor_tensor(hm2[:, g, :], er[:, bass.ds(p, 1), g, 1, :].rearrange("p a d -> p (a d)"), wl[:, 2 * g + 1:2 * g + 2],
                                                    hm1[:, g, :], ALU.mult, ALU.add)
                ch2.link(last)
                ch2.wait()
                dve.wait_ge(s["ys"], p + 1)
                ch2.link(dve.scalar_tensor_tensor(hm[:, :, :], p_y, SHARED, hm2[:, :, :], ALU.mult, ALU.add))
                ch2.wait()
                for g in range(G):
                    last = dve.bn_stats(stat[:, g, :], hm[:, g, :])
                ch2.link(last)
                ch2.gate()
                for g in range(G):
                    last = dve.bn_aggr(mv[:, g, :], stat[:, g, :])
                ch2.link(last)
                ch2.wait()
                dve.tensor_scalar(ve[:, :], mv[:, :, 1], EPS, None, ALU.add).then_inc(s["fve"], 1)
                ch2.link(dve.tensor_tensor(rh2[:, :, :], hm[:, :, :],
                                           res[:, bass.ds(p, 1), :, :].rearrange("p a g d -> p (a g) d"), ALU.add))
                dve.wait_ge(s["frstd"], p + 1)
                for g in range(G):
                    last = dve.tensor_scalar(fn[:, g, :], hm[:, g, :], mv[:, g, 0:1], rstd[:, g:g + 1],
                                             ALU.subtract, ALU.mult)
                last.then_inc(s["fn"], 1)

            def keep_rh(p):
                if not (isinstance(p, int) and p == 0):
                    dve.wait_ge(s["of"], p)
                ch2.wait()
                ch2.link(dve.tensor_tensor(rh[:, :, :], rh2[:, :, :],
                                           row["fbf2"][:, :].unsqueeze(1).to_broadcast([N, G, D]), ALU.add))

            def output(p):
                dve.wait_ge(s["f2"], p + 1)
                ch2.wait()
                if not (isinstance(p, int) and p == 0):
                    dve.wait_ge(s["out"], 16 * p)
                for g in range(G):
                    last = dve.tensor_tensor(of[:, g, :], [b_s, b_qk][g][0:N, 0:D], rh[:, g, :], ALU.add)
                last.then_inc(s["of"], 1)

            class Chain2(Chain):
                def at(self, p):
                    self.base = p * 8 + (self.start - self.first * 8)
                    self.count = 0

                def leave(self, p):
                    assert self.count == 8, self.count
                    self.base, self.count = None, self.start + (p - self.first) * 8

            ch2 = Chain2()
            ch2.count = ch.count
            mixture(0)
            keep_rh(0)
            mixture(1)
            output(0)
            keep_rh(1)
            ch2.enter(2)
            with dve.Fori(2, PAIRS - 1) as p:
                ch2.at(p)
                mixture(p)
                output(p - 1)
                keep_rh(p)
            ch2.leave(PAIRS - 1)
            mixture(PAIRS - 1)
            output(PAIRS - 2)
            keep_rh(PAIRS - 1)
            output(PAIRS - 1)

        @block.tensor
        def _(pe):
            pe.wait_ge(s["early"], 16 * (6 + len(ROWS)))

            def begin(p):
                pass

            def chunk(p, c):
                if c == 0:
                    if isinstance(p, int) and p == 0:
                        pe.wait_ge(s["consts"], 1)
                    else:
                        pe.wait_ge(s["exp1"], p)
                pe.wait_ge(s["tanh"], p * CH + c + 1)
                g, cc = c // CPB, c % CPB
                for m in range(CQ):
                    col = CQ * cc + m
                    for a in range(QG):
                        j = a * CQ + m
                        last = pe.matmul(b_s[32 * a:32 * a + 32, g * N:(g + 1) * N], apad[:, 31 - col:63 - col],
                                         tbuf[:, c % TRING, j * N:(j + 1) * N],
                                         start=(cc == 0 and m == 0), stop=(cc == CPB - 1 and m == CQ - 1))
                last.then_inc(s["score"], 1)

            def xs_turn(p):
                pe.wait_ge(s["xs"], p + 1)
                if not (isinstance(p, int) and p == 0):
                    pe.wait_ge(s["v_ev"], p)
                if not (isinstance(p, int) and p < 3):
                    pe.wait_ge(s["ve2"], 2 * p - 5)
                for g in range(G):
                    last = pe.transpose(p_xT[:, g * N:(g + 1) * N], xs[:, g, :], ident[0:N, 0:N])
                last.then_inc(s["xs_t"], 1)

            def qkv(p):
                pe.wait_ge(s["xT"], p + 1)
                if not (isinstance(p, int) and p == 0):
                    pe.wait_ge(s["qk_ev"], p)
                for i in range(2):
                    pe.matmul(b_qk[:, i * TN:(i + 1) * TN], wqkv[:, i, :], xT[:, :], start=True, stop=True)
                for g in range(G):
                    last = pe.matmul(p_v[:, g, :], xT[:, g * N:(g + 1) * N], wqkv[:, 2, :], start=True, stop=True)
                last.then_inc(s["qkv"], 1)

            def products(p):
                if not (isinstance(p, int) and p == 1):
                    return
                pe.wait_ge(s["late"], 16 * 15)
                for i in range(4):
                    bank = [big[0], big[1], big[2], b_t][i]
                    for j in range(4):
                        h = (i % 2) * 4 + j
                        a, b = (0, 1) if i < 2 else (2, 3)
                        last = pe.matmul(bank[:, j * D:(j + 1) * D], raw[:, a, h * D:(h + 1) * D],
                                         raw[:, b, h * D:(h + 1) * D], start=True, stop=True)
                    last.then_inc(s["raw_mm"], 1)

            def p1_turn(p):
                if isinstance(p, int) and p == 0:
                    pe.wait_ge(s["raw_ev"], 4)
                pe.wait_ge(s["p1n"], p + 1)
                for g in range(G):
                    last = pe.transpose(b_t[0:N, g * SR:(g + 1) * SR], p1[:, g, :], ident[0:SR, 0:SR])
                last.then_inc(s["p1t_ps"], 1)

            def attend1(p):
                pe.wait_ge(s["p1T"], p + 1)
                pe.wait_ge(s["v_ev"], p + 1)
                for g in range(G):
                    last = pe.matmul(b_t[:, g * N:(g + 1) * N], vrow[:, g, :], p1T[:, g, :], start=True, stop=True)
                last.then_inc(s["aT_ps"], 1)

            def project1(p):
                pe.wait_ge(s["aT"], p + 1)
                if not (isinstance(p, int) and p < 2):
                    pe.wait_ge(s["rank"], p - 1)
                for g in range(G):
                    last = pe.matmul(p_y[:, g, :], aT[:, g * N:(g + 1) * N], wo[:, :], start=True, stop=True)
                last.then_inc(s["y"], 1)

            def x1_turn(p):
                pe.wait_ge(s["x1n"], p + 1)
                for g in range(G):
                    last = pe.transpose(b_t[:, g * N:(g + 1) * N], x1n[:, g, :], ident[0:N, 0:N])
                last.then_inc(s["x1T_ps"], 1)

            def ffn1(p):
                pe.wait_ge(s["x1T"], p + 1)
                for c in range(FC):
                    if c % 2 == 0:
                        big_freed(pe, p, c // 2)
                    last = pe.matmul(big[c // 2][:, (c % 2) * TN:(c % 2 + 1) * TN], w1[:, c * D:(c + 1) * D],
                                     x1T[:, :], start=True, stop=True)
                    if c % 2:
                        last.then_inc(s["big"], 1)

            def ffn2(p):
                all_emptied(pe, p, (0, 1))
                for g in range(G):
                    for c in range(FC):
                        last = pe.matmul(p_y[:, g, :], hid[:, c, g * N:(g + 1) * N], w2[:, c, :],
                                         start=(c == 0), stop=(c == FC - 1))
                last.then_inc(s["y2"], 1)

            def xa_turn(p):
                pe.wait_ge(s["xa"], p + 1)
                for g in range(G):
                    last = pe.transpose(b_t[:, g * N:(g + 1) * N], xa[:, g, :], ident[0:N, 0:N])
                last.then_inc(s["xaT_ps"], 1)

            def heads_g(k):
                def f(p):
                    pe.wait_ge(s["xaT"], p + 1)
                    big_freed(pe, p, 2 + k)
                    for j in range(2):
                        h = 2 * k + j
                        last = pe.matmul(big[(2 + k) % 3][:, j * TN:(j + 1) * TN], mh[:, h * D:(h + 1) * D],
                                         xaT[:, :], start=True, stop=True)
                    last.then_inc(s["big"], 1)
                return f

            def heads_v(k):
                def f(p):
                    big_freed(pe, p, 6 + k)
                    g = k // 2
                    pe.matmul(big[(6 + k) % 3][0:N, :], xaT[:, g * N:(g + 1) * N],
                              vo[:, (k % 2) * 512:(k % 2 + 1) * 512], start=True, stop=True).then_inc(s["big"], 1)
                return f

            def scores(k):
                def f(p):
                    all_emptied(pe, p, (2 + 2 * (k % 2), 3 + 2 * (k % 2), 7 + k))
                    g = k // 2
                    for j in range(4):
                        h = (k % 2) * 4 + j
                        last = pe.matmul(big[(10 + k) % 3][0:N, j * N:(j + 1) * N], gT[:, h, g * N:(g + 1) * N],
                                         xaT[:, g * N:(g + 1) * N], start=True, stop=True)
                    last.then_inc(s["big"], 1)
                return f

            def pr_turn(k):
                def f(p):
                    big_freed(pe, p, 14 + k)
                    pe.wait_ge(s["pn"], 4 * p + k + 1)
                    for j in range(4):
                        last = pe.transpose(big[(14 + k) % 3][0:N, j * N:(j + 1) * N], pr[:, 4 * k + j, :],
                                            ident[0:N, 0:N])
                    last.then_inc(s["big"], 1)
                return f

            def attend2(k):
                def f(p):
                    if k == 0:
                        pe.wait_ge(s["v_ev"], min(p + 3, PAIRS) if isinstance(p, int) else p + 3)
                    all_emptied(pe, p, (14 + k, 6 + 2 * (k // 2), 7 + 2 * (k // 2)))
                    g = k // 2
                    for h in range((k % 2) * 4, (k % 2) * 4 + 4):
                        last = pe.matmul(p_o[:, g, :], prT[:, g * H + h, :], vv[:, g, h * D:(h + 1) * D],
                                         start=(h == 0), stop=(h == H - 1))
                    if k == 3:
                        last.then_inc(s["o"], 1)
                return f

            def tn_turn(p):
                pe.wait_ge(s["tn"], p + 1)
                pe.wait_ge(s["xaT"], min(p + 2, PAIRS) if isinstance(p, int) else p + 2)
                for g in range(G):
                    last = pe.transpose(b_t[:, g * N:(g + 1) * N], tn[:, g, :], ident[0:N, 0:N])
                last.then_inc(s["hT_ps"], 1)

            def router(p):
                pe.wait_ge(s["hT"], p + 1)
                pe.wait_ge(s["ve"], 3 * min(p + 1, PAIRS - 1) + 2 if isinstance(p, int) else 3 * p + 5)
                pe.matmul(p_rT, wr[:, :], hT[:, :], start=True, stop=True).then_inc(s["rT_ps"], 1)

            def logits(p):
                pe.wait_ge(s["rT"], p + 1)
                for g in range(G):
                    last = pe.matmul(p_lg[:, g * E:(g + 1) * E], rT[:, g * N:(g + 1) * N], cbT[:, :],
                                     start=True, stop=True)
                last.then_inc(s["lg"], 1)

            def ranks(p):
                pe.wait_ge(s["oh"], p + 1)
                for g in range(G):
                    pe.matmul(p_rank[:, g, :], tri[:, :], ohs[:, g, :], start=True, stop=False)
                    if g == 1:
                        pe.matmul(p_rank[:, g, :], ones[:, 0:N], ohs[:, 0, :], start=False, stop=False)
                    last = pe.matmul(p_rank[:, g, :], ones[:, 0:N], cum[:, :], start=False, stop=True)
                last.then_inc(s["rank_ps"], 1)

            pipeline(pe, begin, chunk,
                     {1: [p1_turn], 2: [attend1], 3: [project1], 6: [x1_turn], 7: [ffn1], 8: [ffn2],
                      12: [xa_turn], 13: [heads_g(0), heads_g(1), heads_g(2), heads_g(3), heads_v(0)],
                      16: [heads_v(1), heads_v(2), heads_v(3), scores(0), scores(1)], 17: [scores(2)],
                      19: [scores(3), pr_turn(0)], 20: [attend2(0), pr_turn(1), pr_turn(2)], 21: [pr_turn(3)],
                      22: [attend2(1), attend2(2)], 24: [attend2(3)], 30: [tn_turn], 31: [router],
                      32: [logits], 33: [ranks]},
                     {8: [xs_turn], 11: [qkv], 12: [products]}, None)

            pe.wait_ge(s["slot"], PAIRS)
            pe.matmul(b_t[0:MAXT, 0:E], ones[:, 0:MAXT], cum[:, :], start=True, stop=True).then_inc(s["cnt"], 1)
            pe.wait_ge(s["tinfo"], 1)
            pe.matmul(b_y[0:1, 0:MAXT], tinfo[:, 0:1], ident[0:MAXT, 0:MAXT], start=True, stop=True)
            for i in range(3):
                last = pe.matmul(b_y[0:1, MAXT + i:MAXT + i + 1], tinfo[:, 1 + i:2 + i],
                                 ident[0:MAXT, 0:1], start=True, stop=True)
            last.then_inc(s["trow"], 1)
            pe.wait_ge(s["idf"], 1)
            pe.transpose(b_v[:, 0:MAXT], idf[:, :], ident[0:MAXT, 0:MAXT]).then_inc(s["ids_t"], 1)
            pe.wait_ge(s["ttab"], 1)
            turns = turns_less(pe, 0)

            def tile_turn(u, r):
                t = u * RING + r
                if not (isinstance(t, int) and t == 0):
                    pe.wait_ge(s["hbT"], t)
                pe.wait_ge(s_h[r], 16 * (u + 1))
                pe.transpose(b_t[:, 0:TILE], hrow[r][:, :], ident[:, :]).then_inc(s["tr"], 1)

            def expert1(u, r):
                t = u * RING + r
                pe.wait_ge(s["hbT"], t + 1)
                pe.wait_ge(s_w[r], 32 * (u + 1))
                for c in range(FC):
                    last = pe.matmul(big[r % 2][:, c * TILE:(c + 1) * TILE], wbuf[:, r, c * D:(c + 1) * D],
                                     hbT[:, r % 2, :], start=True, stop=True)
                last.then_inc(s["g1"], 1)

            def expert2(u, r, before):
                t = u * RING + r
                pe.wait_ge(s["silu"], t + 1)
                if r:
                    if not (isinstance(t, int) and t < 2):
                        pe.wait_ge(s["eo"], t - 1)
                elif before is not None:
                    pe.wait_ge(s["eo"], before * RING + RING - 1)
                o = [b_s, b_qk][r % 2][:, 0:D]
                for c in range(FC):
                    last = pe.matmul(o, act_h[:, r % 2, c * TILE:(c + 1) * TILE],
                                     wbuf[:, r, DFF + c * D:DFF + (c + 1) * D], start=(c == 0), stop=(c == FC - 1))
                last.then_inc(s["g2"], 1)

            def turn(u, before, after):
                for r in range(RING):
                    expert1(u, r)
                    if r < RING - 1:
                        tile_turn(u, r + 1)
                    elif after is not None:
                        tile_turn(after, 0)
                    if r:
                        expert2(u, r - 1, before)
                    elif before is not None:
                        expert2(before, RING - 1, None)

            tile_turn(0, 0)
            turn(0, None, 1)
            with pe.Fori(1, turns - 1) as u:
                turn(u, u - 1, u + 1)
            last, before = turns_less(pe, 1), turns_less(pe, 2)
            turn(last, before, None)
            expert2(last, RING - 1, before)

            def shared1(p):
                if not (isinstance(p, int) and p == 0):
                    pe.wait_ge(s["sh"], p)
                for c in range(SC2):
                    last = pe.matmul(b_t[:, c * TN:(c + 1) * TN], ws1[:, c * D:(c + 1) * D],
                                     hall[:, bass.ds(p, 1), :].rearrange("p a n -> p (a n)"),
                                     start=True, stop=True)
                last.then_inc(s["sh_ps"], 1)

            def shared2(p):
                pe.wait_ge(s["sh"], p + 1)
                if not (isinstance(p, int) and p == 0):
                    pe.wait_ge(s["fve"], p)
                for g in range(G):
                    for c in range(SC2):
                        last = pe.matmul(p_y[:, g, :], sh[:, c, g * N:(g + 1) * N], ws2[:, c, :],
                                         start=(c == 0), stop=(c == SC2 - 1))
                last.then_inc(s["ys"], 1)

            def f_turn(p):
                pe.wait_ge(s["fn"], p + 1)
                for g in range(G):
                    last = pe.transpose(b_v[:, g * N:(g + 1) * N], fn[:, g, :], ident[0:N, 0:N])
                last.then_inc(s["fT_ps"], 1)

            def last1(p):
                pe.wait_ge(s["fT"], p + 1)
                if not (isinstance(p, int) and p == 0):
                    pe.wait_ge(s["fa"], FC * p)
                for c in range(FC):
                    last = pe.matmul(big[c // 2][:, (c % 2) * TN:(c % 2 + 1) * TN], wf1[:, c * D:(c + 1) * D],
                                     fT[:, :], start=True, stop=True)
                    if c % 2:
                        last.then_inc(s["f1"], 1)

            def last2(p):
                if not (isinstance(p, int) and p == 0):
                    pe.wait_ge(s["of"], p)
                for c in range(FC):
                    pe.wait_ge(s["fa"], FC * p + c + 1)
                    for g in range(G):
                        last = pe.matmul([b_s, b_qk][g][0:N, 0:D], fh[:, c, g * N:(g + 1) * N], wf2[:, c, :],
                                         start=(c == 0), stop=(c == FC - 1))
                last.then_inc(s["f2"], 1)

            pe.wait_ge(s["eo"], turns * RING)
            pe.sem_inc(s["gate"], 1)
            shared1(0)
            shared2(0)
            shared1(1)
            f_turn(0)

            def step(p):
                shared2(p)
                last1(p - 1)
                if not (isinstance(p, int) and p == PAIRS - 1):
                    shared1(p + 1)
                last2(p - 1)
                f_turn(p)

            step(1)
            with pe.Fori(2, PAIRS - 1) as p:
                step(p)
            step(PAIRS - 1)
            last1(PAIRS - 1)
            last2(PAIRS - 1)


def _inputs(inputs):
    f = {k: np.ascontiguousarray(np.asarray(v)) for k, v in inputs.items()}
    a = {}
    a["x"] = np.ascontiguousarray(f["x"].T)
    a["L0_tok_emb"] = f["L0_tok_emb"]
    for n in ["L0_tok_Wq", "L0_tok_Wk", "L0_tok_Wv", "L0_tok_Wo", "L0_tok_W1", "L0_tok_W2", "L0_ffn_Wr",
              "L0_ffn_Ws1", "L0_ffn_Ws2", "L0_ffn_Wf1", "L0_ffn_Wf2", "L0_ffn_b2"]:
        a[n] = f[n]
    a["attn_Wq"], a["attn_Wk"], a["attn_Wv"] = f["L0_attn_Wq"], f["L0_attn_Wk"], f["L0_attn_Wv"]
    a["attn_WoT"] = np.ascontiguousarray(f["L0_attn_Wo"].T)
    a["cbT"] = np.ascontiguousarray(f["L0_ffn_codebook"].T)
    for n, src in zip(ROWS, ["L0_tok_bv", "L0_tok_bo", "L0_tok_g1", "L0_tok_beta1", "L0_tok_bf2", "L0_tok_g2",
                             "L0_tok_beta2", "L0_ffn_bs2", "L0_ffn_bf2"]):
        a["row_" + n] = f[src]
    a["cols"] = np.concatenate(
        [f[n].reshape(-1, D).T for n in ["L0_tok_bq", "L0_tok_bk", "L0_tok_attn_scale", "L0_ffn_ln1_g",
                                         "L0_ffn_ln1_b", "L0_ffn_ffln_g", "L0_ffn_ffln_b", "L0_tok_bf1",
                                         "L0_ffn_bs1", "L0_ffn_bf1"]], axis=1)
    w1 = f["L0_ffn_W1"]
    w2 = f["L0_ffn_W2"].reshape(E, FC, D, D).transpose(0, 2, 1, 3).reshape(E, D, DFF)
    b1 = f["L0_ffn_b1"].reshape(E, FC, D).transpose(0, 2, 1)
    a["wpack"] = np.concatenate([w1, w2, b1], axis=2)
    pos = np.arange(N)[:, None].astype(np.float64)
    i = np.arange(D)[None, :]
    ang = pos / np.power(10000.0, 2 * (i // 2) / np.float32(D))
    ang[:, 0::2] = np.sin(ang[:, 0::2])
    ang[:, 1::2] = np.cos(ang[:, 1::2])
    a["pe"] = ang.astype(np.float32)
    a["ident"] = np.eye(128, dtype=np.float32)
    a["mask"] = np.triu(np.full((N, N), NEG, np.float32), 1)
    a["tri"] = np.triu(np.ones((N, N), np.float32), 1)
    return {k: np.ascontiguousarray(v) for k, v in a.items()}


def kernel(**inputs):
    import concourse.bacc as bacc
    from concourse.bass_utils import run_bass_kernel_spmd

    nc = bacc.Bacc("TRN2", target_bir_lowering=False, num_devices=1)
    arrays = _inputs(inputs)
    io = {n: nc.dram_tensor("in_" + n, a.shape, mybir.dt.from_np(a.dtype), kind="ExternalInput").ap()
          for n, a in arrays.items()}
    out = nc.dram_tensor("out", (B, N, D), F32, kind="ExternalOutput").ap()
    program(nc, io, out)
    r = run_bass_kernel_spmd(nc, [{"in_" + n: a for n, a in arrays.items()}], core_ids=[0])
    return r.results[0]["out"]
```
